# Optimizing a Trainium2 kernel written in Bass

```python
import numpy as np
import jax
import jax.numpy as jnp

def _softmax(x, axis=-1):
    return jax.nn.softmax(x, axis=axis)

def _gelu(x):
    return jax.nn.gelu(x, approximate=True)

def _silu(x):
    return jax.nn.silu(x)

def _sigmoid(x):
    return jax.nn.sigmoid(x)

def _layernorm(x, axis=-1, eps=1e-05):
    m = jnp.mean(x, axis=axis, keepdims=True)
    v = jnp.var(x, axis=axis, keepdims=True)
    return (x - m) / jnp.sqrt(v + eps)

def _scatter_add(tgt, idx, src, axis=0):
    return tgt.at[idx].add(src)

def _segment_sum(src, seg, n):
    return jax.ops.segment_sum(src, seg, n)
kernel_name = 'mk_flamingo_gated_d2_seqx_r8_c0b0f7'

def setup_inputs(seed: int=0):
    np.random.seed(seed)
    _w = jnp.asarray

    def _rec_inputs():
        import jax
        import jax.numpy as jnp
        _rk = jax.random.key(seed)
        x = 7.22e-05 + 1 * jax.random.normal(jax.random.fold_in(_rk, 1), (64, 64, 256), jnp.float32)
        _lenS = 64 - jax.random.randint(jax.random.fold_in(_rk, 7), (64,), 0, max(1, 64 // 4) + 1, jnp.int32)
        _lenS2 = 64 - jax.random.randint(jax.random.fold_in(_rk, 8), (64,), 0, max(1, 64 // 4) + 1, jnp.int32)
        _ctx_512P = jax.random.normal(jax.random.fold_in(_rk, 11), (64, 16, 64), jnp.float32)
        _ctx_512c = jax.random.dirichlet(jax.random.fold_in(_rk, 511), 0.3 * jnp.ones((16,), jnp.float32), (64, 64))
        _ctx_512t = jnp.einsum('bsk,bkd->bsd', _ctx_512c, _ctx_512P)
        _ctx_512t = _ctx_512t * jax.lax.rsqrt(jnp.mean(jnp.square(_ctx_512t)) + 1e-12) * 0.953939
        ctx_512 = -0.000514642 + 1.00011 * (_ctx_512t + 0.3 * jax.random.normal(jax.random.fold_in(_rk, 611), (64, 64, 64), jnp.float32))
        _g = jax.random.normal(jax.random.fold_in(_rk, 9001), (2, 2), jnp.float32)
        _g = jnp.sign(_g) * jnp.maximum(jnp.abs(_g), 1.0) + (_g == 0) * 1.0
        g_xattn = _g[0]
        g_ffn = _g[1]
        return (x, ctx_512, g_xattn, g_ffn)
    x, ctx_512, g_xattn, g_ffn = _rec_inputs()

    def _L0_xattn_setup():
        import jax, jax.numpy as jnp
        import numpy as np
        B, S, E = (2, 256, 256)
        QH, KVH = (32, 8)
        D = E // QH
        G = QH // KVH
        DROPOUT = 1.0
        key = jax.random.key(seed)
        k1, k2, k3 = jax.random.split(key, 3)
        q = jax.random.normal(k1, (B, S, E), dtype=jnp.float32)
        k = jax.random.normal(k2, (B, S, E // G), dtype=jnp.float32)
        v = jax.random.normal(k3, (B, S, E // G), dtype=jnp.float32)
        return {'q': q, 'k': k, 'v': v}
    _L0_xattn_all = _L0_xattn_setup()
    _L0_xattn_in = {k: v for k, v in _L0_xattn_all.items() if k in ()}
    del _L0_xattn_all

    def _L0_ffn_setup():
        import jax, jax.numpy as jnp
        import numpy as np
        H = 256
        E = 64
        I = 64
        SI = 64
        TOP_K = 8
        B, T = (2, 64)
        key = jax.random.key(seed)
        ks = jax.random.split(key, 8)
        s = 0.02
        return {'h': jax.random.normal(ks[0], (B, T, H), jnp.float32), 'gate_w': jax.random.normal(ks[1], (E, H), jnp.float32) * s, 'gu_w': jax.random.normal(ks[2], (E, 2 * I, H), jnp.float32) * s, 'dp_w': jax.random.normal(ks[3], (E, H, I), jnp.float32) * s, 'sh_gate_w': jax.random.normal(ks[4], (SI, H), jnp.float32) * s, 'sh_up_w': jax.random.normal(ks[5], (SI, H), jnp.float32) * s, 'sh_down_w': jax.random.normal(ks[6], (H, SI), jnp.float32) * s, 'sh_gate1_w': jax.random.normal(ks[7], (1, H), jnp.float32) * s}
    _L0_ffn_all = _L0_ffn_setup()
    _L0_ffn_in = {k: v for k, v in _L0_ffn_all.items() if k in ('gate_w', 'gu_w', 'dp_w', 'sh_gate_w', 'sh_up_w', 'sh_down_w', 'sh_gate1_w')}
    del _L0_ffn_all

    def _L1_xattn_setup():
        import jax, jax.numpy as jnp
        import numpy as np
        import math
        D_MODEL = 256
        N_HEADS = 16
        N_GROUPS = 4
        HEADS_PER_GROUP = N_HEADS // N_GROUPS
        HEAD_DIM = D_MODEL // N_HEADS
        B, S = (2, 256)
        key = jax.random.key(seed)
        k1, k2, k3, k4, k5 = jax.random.split(key, 5)
        q = jax.random.normal(k1, (B, S, D_MODEL), dtype=jnp.float32)
        k = jax.random.normal(k2, (B, S, N_GROUPS * HEAD_DIM), dtype=jnp.float32)
        v = jax.random.normal(k3, (B, S, N_GROUPS * HEAD_DIM), dtype=jnp.float32)
        lim = 1.0 / math.sqrt(D_MODEL)
        Wc = jax.random.uniform(k4, (D_MODEL, D_MODEL), minval=-lim, maxval=lim, dtype=jnp.float32)
        bc = jax.random.uniform(k5, (D_MODEL,), minval=-lim, maxval=lim, dtype=jnp.float32)
        return {'q': q, 'k': k, 'v': v, 'Wc': Wc, 'bc': bc}
    _L1_xattn_all = _L1_xattn_setup()
    _L1_xattn_in = {k: v for k, v in _L1_xattn_all.items() if k in ('Wc', 'bc')}
    del _L1_xattn_all

    def _L1_ffn_setup():
        import jax, jax.numpy as jnp
        import numpy as np
        FP8_MAX = 448.0

        def _fp8_matmul(x2d, w):
            scale_x = jnp.maximum(jnp.max(jnp.abs(x2d)) / FP8_MAX, 1e-06)
            scale_w = jnp.maximum(jnp.max(jnp.abs(w)) / FP8_MAX, 1e-06)
            x8 = (x2d / scale_x).astype(jnp.float8_e4m3fn)
            w8 = (w / scale_w).astype(jnp.float8_e4m3fn)
            out = jnp.matmul(x8.astype(x2d.dtype), w8.astype(x2d.dtype).T)
            return out * (scale_x * scale_w)
        key = jax.random.key(seed)
        k1, k2, k3 = jax.random.split(key, 3)
        dim = 256
        B, S = (4, 256)
        x = jax.random.normal(k1, (B, S, dim), dtype=jnp.float32)
        std = 0.5 * dim ** (-0.5)
        w_fc = jax.random.normal(k2, (4 * dim, dim), dtype=jnp.float32) * std
        w_proj = jax.random.normal(k3, (dim, 4 * dim), dtype=jnp.float32) * std
        return {'x': x, 'w_fc': w_fc, 'w_proj': w_proj}
    _L1_ffn_all = _L1_ffn_setup()
    _L1_ffn_in = {k: v for k, v in _L1_ffn_all.items() if k in ('w_fc', 'w_proj')}
    del _L1_ffn_all
    return {'x': x, 'ctx_512': ctx_512, 'g_xattn': g_xattn, 'g_ffn': g_ffn, 'L0_ffn_gate_w': _L0_ffn_in['gate_w'], 'L0_ffn_gu_w': _L0_ffn_in['gu_w'], 'L0_ffn_dp_w': _L0_ffn_in['dp_w'], 'L0_ffn_sh_gate_w': _L0_ffn_in['sh_gate_w'], 'L0_ffn_sh_up_w': _L0_ffn_in['sh_up_w'], 'L0_ffn_sh_down_w': _L0_ffn_in['sh_down_w'], 'L0_ffn_sh_gate1_w': _L0_ffn_in['sh_gate1_w'], 'L1_xattn_Wc': _L1_xattn_in['Wc'], 'L1_xattn_bc': _L1_xattn_in['bc'], 'L1_ffn_w_fc': _L1_ffn_in['w_fc'], 'L1_ffn_w_proj': _L1_ffn_in['w_proj']}

def reference(x, ctx_512, g_xattn, g_ffn, L0_ffn_gate_w, L0_ffn_gu_w, L0_ffn_dp_w, L0_ffn_sh_gate_w, L0_ffn_sh_up_w, L0_ffn_sh_down_w, L0_ffn_sh_gate1_w, L1_xattn_Wc, L1_xattn_bc, L1_ffn_w_fc, L1_ffn_w_proj):
    import jax
    import jax.numpy as jnp

    def _L0_xattn_ref(q, k, v):
        import jax, jax.numpy as jnp
        import numpy as np
        B, S, E = (2, 256, 256)
        QH, KVH = (32, 8)
        D = E // QH
        G = QH // KVH
        DROPOUT = 1.0
        b, s, _ = q.shape
        qh = q.reshape(b, s, KVH, G, D).transpose(0, 2, 3, 1, 4)
        kh = k.reshape(b, s, KVH, D).transpose(0, 2, 1, 3)
        vh = v.reshape(b, s, KVH, D).transpose(0, 2, 1, 3)
        scale = 1.0 / jnp.sqrt(jnp.float32(D))
        scores = jnp.einsum('bkgsd,bktd->bkgst', qh, kh) * scale
        attn = jax.nn.softmax(scores, axis=-1) / DROPOUT
        out = jnp.einsum('bkgst,bktd->bkgsd', attn, vh)
        return out.transpose(0, 3, 1, 2, 4).reshape(b, s, E)

    def _L0_ffn_ref(h, gate_w, gu_w, dp_w, sh_gate_w, sh_up_w, sh_down_w, sh_gate1_w):
        import jax, jax.numpy as jnp
        import numpy as np
        H = 256
        E = 64
        I = 64
        SI = 64
        TOP_K = 8
        B, T = (2, 64)
        Bb, Tt, Hh = h.shape
        x = h.reshape(Bb * Tt, Hh)
        N = x.shape[0]
        logits = x @ gate_w.T
        topv, topi = jax.lax.top_k(logits, TOP_K)
        rw = jax.nn.softmax(topv.astype(jnp.float32), axis=-1).astype(x.dtype)
        W = jnp.zeros((N, E), x.dtype).at[jnp.arange(N)[:, None], topi].set(rw)
        gu = jnp.einsum('nh,eih->nei', x, gu_w)
        gate, up = (gu[..., :I], gu[..., I:])
        inter = jax.nn.silu(gate) * up
        inter_w = inter * W[:, :, None]
        out = jnp.einsum('nei,ehi->nh', inter_w, dp_w)
        sh_inter = jax.nn.silu(x @ sh_gate_w.T) * (x @ sh_up_w.T)
        sh_out = sh_inter @ sh_down_w.T
        sh_g = jax.nn.sigmoid(x @ sh_gate1_w.T)
        out = out + sh_g * sh_out
        return out.reshape(Bb, Tt, Hh)

    def _L1_xattn_ref(q, k, v, Wc, bc):
        import jax, jax.numpy as jnp
        import numpy as np
        import math
        D_MODEL = 256
        N_HEADS = 16
        N_GROUPS = 4
        HEADS_PER_GROUP = N_HEADS // N_GROUPS
        HEAD_DIM = D_MODEL // N_HEADS
        B, S = (2, 256)
        b, s, _ = q.shape
        qh = q.reshape(b, s, N_GROUPS, HEADS_PER_GROUP, HEAD_DIM).transpose(0, 2, 3, 1, 4)
        kh = k.reshape(b, s, N_GROUPS, HEAD_DIM).transpose(0, 2, 1, 3)
        vh = v.reshape(b, s, N_GROUPS, HEAD_DIM).transpose(0, 2, 1, 3)
        scale = 1.0 / math.sqrt(HEAD_DIM)
        scores = jnp.einsum('bghsd,bgtd->bghst', qh, kh) * scale
        probs = jax.nn.softmax(scores, axis=-1)
        out = jnp.einsum('bghst,bgtd->bghsd', probs, vh)
        out = out.transpose(0, 3, 1, 2, 4).reshape(b, s, D_MODEL)
        return out @ Wc.T + bc

    def _L1_ffn_ref(x, w_fc, w_proj):
        import jax, jax.numpy as jnp
        import numpy as np
        FP8_MAX = 448.0

        def _fp8_matmul(x2d, w):
            scale_x = jnp.maximum(jnp.max(jnp.abs(x2d)) / FP8_MAX, 1e-06)
            scale_w = jnp.maximum(jnp.max(jnp.abs(w)) / FP8_MAX, 1e-06)
            x8 = (x2d / scale_x).astype(jnp.float8_e4m3fn)
            w8 = (w / scale_w).astype(jnp.float8_e4m3fn)
            out = jnp.matmul(x8.astype(x2d.dtype), w8.astype(x2d.dtype).T)
            return out * (scale_x * scale_w)
        shape = x.shape
        x2d = x.reshape(-1, shape[-1])
        h = _fp8_matmul(x2d, w_fc)
        h = jnp.square(jax.nn.relu(h))
        out = _fp8_matmul(h, w_proj)
        return out.reshape(*shape[:-1], -1)
    x = x + jnp.tanh(g_xattn[0]) * _L0_xattn_ref(_layernorm(x, axis=-1), ctx_512, ctx_512)
    x = x + jnp.tanh(g_ffn[0]) * _L0_ffn_ref(_layernorm(x, axis=-1), L0_ffn_gate_w, L0_ffn_gu_w, L0_ffn_dp_w, L0_ffn_sh_gate_w, L0_ffn_sh_up_w, L0_ffn_sh_down_w, L0_ffn_sh_gate1_w)
    x = x + jnp.tanh(g_xattn[1]) * _L1_xattn_ref(_layernorm(x, axis=-1), ctx_512, ctx_512, L1_xattn_Wc, L1_xattn_bc)
    x = x + jnp.tanh(g_ffn[1]) * _L1_ffn_ref(_layernorm(x, axis=-1), L1_ffn_w_fc, L1_ffn_w_proj)
    return x

_drawn_inputs = setup_inputs


def setup_inputs(seed=0):
    import zlib

    import numpy as np

    out = dict(_drawn_inputs(seed))
    spreads = {'g_ffn': (-1.0, 0.6)}
    factors = {'L0_ffn_gate_w': 8.0,
     'L0_ffn_gu_w': 8.0,
     'L0_ffn_dp_w': 8.0,
     'L0_ffn_sh_gate_w': 7.557,
     'L0_ffn_sh_up_w': 8.0,
     'L0_ffn_sh_down_w': 8.0,
     'L0_ffn_sh_gate1_w': 8.0,
     'L1_xattn_bc': 6.024}
    for name, (base, spread) in spreads.items():
        noise = np.random.default_rng([zlib.crc32(name.encode()), seed]).standard_normal(out[name].shape)
        drawn = base * np.exp(spread * noise) if base else spread * noise
        out[name] = jnp.asarray(drawn.astype(out[name].dtype))
    for name, factor in factors.items():
        out[name] = (out[name] * factor).astype(out[name].dtype)
    return out
```

```python
import numpy as np
import concourse.bass as bass
from concourse import mybir

ALU = mybir.AluOpType
ACT = mybir.ActivationFunctionType
AX = mybir.AxisListType
F32 = mybir.dt.float32
F16 = mybir.dt.float16
BF16 = mybir.dt.bfloat16
RMAX = bass.bass_isa.ReduceOp.max

P = 128
B, S, H = 64, 64, 256
C = 64
NT = B * S // P
G = 4
E, I = 64, 64
NPAIR = E // 2
CH = 512
NCH = B * S // CH
TPC = CH // P
KT = H // P
FF = 1024
NF = FF // P
PW = KT * 2 * P + H
SMW = 4 * 64
EPS = 1e-5
FP8_MAX = 448.0
GRID = float(2 ** 20)
FLOOR = 1.5 * 2.0 ** 14
LAYERS = ((8, 8), (4, 16))


def const_columns():
    at, out = 0, {}
    for name, width in (("ident", P), ("mask0", 8), ("mask1", 4), ("neg0", 8), ("neg1", 4),
                        ("vmask0", 4 * C), ("vmask1", 2 * C), ("ones0", 4 * 8), ("ones1", 2 * 4)):
        out[name] = (at, width)
        at += width
    return out, at


def const_table():
    cols, width = const_columns()
    t = np.zeros((P, width), np.float32)
    r = np.arange(P)[:, None]

    def put(name, block):
        a, w = cols[name]
        t[:, a:a + w] = block.reshape(P, w)

    put("ident", np.eye(P))
    for layer, (nk, d) in enumerate(LAYERS):
        k = np.arange(nk)[None, :]
        put(f"mask{layer}", (r % C) // d == k)
        put(f"neg{layer}", np.where(r < C, r // d == k, -1.0 * (r - C == k)))
        pair = np.arange(nk // 2)[None, :, None]
        head = 2 * pair + (r[:, :, None] >= S)
        put(f"vmask{layer}", np.arange(C)[None, None, :] // d == head)
        put(f"ones{layer}", np.arange(nk)[None, None, :] == head)
    return t


def selectors():
    r = np.arange(P)[:, None] % E
    return (r == np.arange(NPAIR * P)[None, :] // I).astype(np.float16)


def known(t):
    return isinstance(t, int)


def stand_alone(eng, side):
    eng.sem_inc(side, 1)


def inside(t):
    return not known(t) or 0 <= t < NT


def past(t, n):
    return not known(t) or t >= n


def sweep(eng, step):
    for t in range(-3, 4):
        step(t, t % 2)
    with eng.Fori(4, NT - 5, 2) as t:
        step(t, 0)
        step(t + 1, 1)
    for t in range(NT - 4, NT + 1):
        step(t, t % 2)


def chunks(eng, body):
    body(0, False, True)
    with eng.Fori(1, NCH - 1) as c:
        body(c, True, True)
    body(NCH - 1, True, False)


def tiles(eng, n, body):
    body(0, 0)
    body(1, 1)
    with eng.Fori(2, n - 1, 2) as t:
        body(t, 0)
        body(t + 1, 1)


def flamingo_block(nc, x_in, ctx, ctxT, gates, consts, sel_in, wpairs, wsmall, wshdown, wc_in, bc_in, wfc_in, wproj_in, out):
    sb = lambda name, shape, dt=F32: nc.alloc_sbuf_tensor(name, shape, dt)
    sem = nc.alloc_semaphore

    cols, CW = const_columns()
    x = sb("x", [P, NT, H])
    cst = sb("cst", [P, CW])
    region = sb("region", [P, NPAIR * PW * 2], F16)
    WH = region[:, 0:NPAIR * PW].rearrange("p (n w) -> p n w", w=PW)
    WL = region[:, NPAIR * PW:2 * NPAIR * PW].rearrange("p (n w) -> p n w", w=PW)
    V = sb("V", [P, B, C])
    KH = sb("KH", [P, B, S], F16)
    KL = sb("KL", [P, B, S], F16)
    gate = sb("gate", [P, 4])
    tg = sb("tg", [P, 4])
    neghalf = sb("neghalf", [P, 1])
    epsilon = sb("epsilon", [P, 1])
    small_h = sb("small_h", [P, KT, SMW], F16)
    small_l = sb("small_l", [P, KT, SMW], F16)
    shd_h = sb("shd_h", [I, H], F16)
    shd_l = sb("shd_l", [I, H], F16)

    st = sb("st", [P, 2, 6])
    mv = sb("mv", [P, 2, 2])
    ve = sb("ve", [P, 2, 1])
    rs = sb("rs", [P, 2, 1])

    arena_bytes = 42 * 1024
    arena = sb("arena", [P, arena_bytes // 4])
    used = [0]

    def carve(shape, dt=F32):
        n = int(np.prod(shape))
        size = 4 if dt == F32 else 2
        a = used[0]
        used[0] += -(-n * size // 64) * 16
        assert used[0] <= arena_bytes // 4, used[0] * 4
        v = arena[:, a:a + -(-n * size // 4)]
        if dt != F32:
            v = v.bitcast(dt)
        if len(shape) == 2:
            v = v.rearrange("p (a b) -> p a b", b=shape[1])
        if len(shape) == 3:
            v = v.rearrange("p (a b c) -> p a b c", b=shape[1], c=shape[2])
        if len(shape) == 4:
            v = v.rearrange("p (a b c d) -> p a b c d", b=shape[1], c=shape[2], d=shape[3])
        return v

    W0 = C + 8
    XG = [carve([G, C + W0]) for _ in range(2)]
    Q1 = [carve([G, P], F16) for _ in range(2)]
    Q2 = [carve([G, P], F16) for _ in range(2)]
    KD1 = [carve([2, 8 * S], F16) for _ in range(2)]
    KD2 = [carve([2, 8 * S], F16) for _ in range(2)]
    VD = [carve([2, 4 * W0]) for _ in range(2)]
    EX = [carve([512]) for _ in range(4)]
    PVS = carve([G, P])
    RC = carve([G, 8])
    ON = [carve([H]) for _ in range(2)]
    ont_at = used[0]
    stage = [carve([PW]) for _ in range(2)]
    used[0] = ont_at
    ONT = [carve([KT, P]) for _ in range(2)]
    used[0] = 0
    XN = carve([H])
    XNH, XNL = carve([KT, CH], F16), carve([KT, CH], F16)
    XCH, XCL = carve([KT, CH], F16), carve([KT, CH], F16)
    WNT, WCT = carve([CH], F16), carve([CH], F16)
    LG, MR, EXL, MK, WU = carve([E]), carve([E]), carve([E]), carve([E]), carve([E])
    WD = carve([2, E])
    V8, NV, SU, RI = carve([8]), carve([1]), carve([1]), carve([1])
    SL = [carve([CH]) for _ in range(2)]
    IN = [carve([CH]) for _ in range(2)]
    IH = [carve([CH], F16) for _ in range(3)]
    IL = [carve([CH], F16) for _ in range(3)]
    SG = carve([CH])
    DT = carve([KT, CH])
    sel = carve([NPAIR, P], F16)
    used[0] = 0
    R = [carve([CH]) for _ in range(2)]
    HS = [carve([CH]) for _ in range(2)]
    CC = [carve([2 * CH]) for _ in range(2)]
    UU = [carve([2 * CH]) for _ in range(2)]
    XD = [carve([H]) for _ in range(2)]
    YO = [carve([H]) for _ in range(2)]
    AM, AP1, HM, FS = carve([NT]), carve([4]), carve([NCH * NF]), carve([24])
    fr = region[:, :].bitcast(F32)
    XF = fr[:, 0:KT * NT * P].rearrange("p (k n) -> p k n", k=KT)
    WF = fr[:, 8192:8192 + KT * FF]
    WP = fr[:, 10240:10240 + NF * H]
    wc = fr[:, 22528:23040].rearrange("p (k h) -> p k h", k=KT)
    bc, bcg = fr[:, 23040:23296], fr[:, 23296:23552]
    hb = region[:, 24576:].bitcast(BF16)
    X8 = hb[:, 0:KT * NT * P].rearrange("p (k n) -> p k n", k=KT)
    WF8 = hb[:, 8192:8192 + KT * FF].rearrange("p (k f) -> p k f", k=KT)
    WP8 = hb[:, 10240:10240 + NF * H].rearrange("p (f h) -> p f h", f=NF)
    H8 = [hb[:, 12288 + 4096 * n:12288 + 4096 * (n + 1)].rearrange("p (f t) -> p f t", f=NF) for n in range(2)]

    bank = [nc.alloc_psum_tensor(f"bank{n}", [P, 512], F32) for n in range(8)]

    def cv(name):
        a, w = cols[name]
        return cst[:, a:a + w]

    ident = cv("ident")

    d_small, d_late, d_sel, d_ctx, d_kt, d_xa, d_xb, d_w = (sem(n) for n in ("d_small", "d_late", "d_sel", "d_ctx", "d_kt", "d_xa", "d_xb", "d_w"))
    d_wsm, d_wf, d_wp = (sem(n) for n in ("d_wsm", "d_wf", "d_wp"))
    stored = [sem("stored0"), sem("stored1")]
    kt_hi, kv_ready, tanh_done = sem("kt_hi"), sem("kv_ready"), sem("tanh_done")
    whi_done, wlo_done = sem("whi_done"), sem("wlo_done")
    sm_hi, sm_ready, bcg_done, half_set = sem("sm_hi"), sem("sm_ready"), sem("bcg_done"), sem("half_set")
    side_v, side_s = sem("side_vector"), sem("side_sync")
    ln_stats, ln_mv, ln_ve, ln_rs, ln_twice, ln_out = (sem(n) for n in ("ln_stats", "ln_mv", "ln_ve", "ln_rs", "ln_twice", "ln_out"))
    names = ("t1_ready", "q_hi", "q_ready", "kd_ready", "vd_set", "vd_ready", "mx_ready", "mx_done", "t2_ready", "q2_ready",
             "sc_ready", "ex_ready", "pv_ready", "pvs_ready", "ot_ready", "rc_done", "rg_done", "on_ready",
             "ont_ready", "onts_ready", "y_ready", "y_read", "x_done")
    A = [{n: sem(f"{n}{layer}") for n in names} for layer in range(2)]

    KF = region[:, NPAIR * PW * 2 - 2 * B * S:].bitcast(F32)
    smf = region[:, NPAIR * PW * 2 - 2 * B * S - 2 * (KT * SMW + H):NPAIR * PW * 2 - 2 * B * S].bitcast(F32)

    STAT_BASE = [0, NT, 2 * NT, 3 * NT]

    xv = x_in.rearrange("(n p) h -> p n h", p=P)
    ov = out.rearrange("(n p) h -> p n h", p=P)

    def tile_x(t):
        return x[:, bass.ds(t, 1), :].rearrange("p a h -> p (a h)") if not known(t) else x[:, t, :]

    def attention_shape(layer):
        nk, d = LAYERS[layer]
        return nk, d, nk // 2, C + nk, G * nk * S // 512, nk // 4

    mnames = ("tp_ready", "xt_hi", "xt_ready", "lg_ready", "lg_done", "v8_done", "mr_done", "nv_done", "ex_done", "mk_done",
              "wu_done", "ri_done", "wd_done", "wt_ready", "wt_hi", "wts_ready", "turned",
              "g_ready", "u_ready", "wb_ready", "sl_ready", "ut_done", "in_ready", "ih_ready", "il_ready", "dn_done",
              "z_ready", "sg_ready", "dt_ready", "ft_ready", "ft_done")
    M = {n: sem("m_" + n) for n in mnames}
    ST = NPAIR + 1
    fnames = ("tp_ready", "xf_ready", "am_done", "amx", "ams", "amr", "c_done", "u_done", "x8_ready", "w8_ready", "abs_ready", "hm_done", "hmx",
              "hr", "fs", "h_ready", "r_ready", "hs_ready", "hc_done", "hu_done", "h8_ready", "y_ready", "y_done", "wamx", "was")
    F = {n: sem("f_" + n) for n in fnames}

    with nc.Block() as block:

        @block.sync
        def _(sp):
            sp.dma_start(cst[:, :], consts).then_inc(d_small, 16)
            for n, g in enumerate(gates):
                sp.dma_start(gate[:, 2 * n:2 * n + 2], g.rearrange("(a d) -> a d", a=1).to_broadcast([P, 2])).then_inc(d_small, 16)
            sp.dma_start(KF[0:C, :], ctxT).then_inc(d_kt, 16)
            sp.dma_start(KF[C:P, :], ctxT).then_inc(d_kt, 16)
            sp.dma_start(x[:, 0:4, :], xv[:, 0:4, :]).then_inc(d_xa, 16)
            for half in range(2):
                sp.dma_start(V[half * S:(half + 1) * S, :, :], ctx.rearrange("b t c -> t b c")).then_inc(d_ctx, 16)
            sp.dma_start(x[:, 4:NT, :], xv[:, 4:NT, :]).then_inc(d_xb, 16)
            sp.dma_start(smf[:, 0:KT * SMW], wsmall).then_inc(d_wsm, 16)
            sp.dma_start(smf[0:I, KT * SMW:KT * SMW + H], wshdown).then_inc(d_wsm, 16)
            for n in range(2):
                sp.dma_start(stage[n], wpairs[:, n, :]).then_inc(d_w, 16)
                sp.wait_ge(d_w, 16 * (n + 1))
            with sp.Fori(2, NPAIR - 1, 2) as n:
                for j in range(2):
                    sp.wait_ge(wlo_done, n + j - 1)
                    stand_alone(sp, side_s)
                    sp.dma_start(stage[j], wpairs[:, bass.ds(n + j, 1), :].rearrange("p a w -> p (a w)")).then_inc(d_w, 16)
                    sp.wait_ge(d_w, 16 * (n + j + 1))
                    stand_alone(sp, side_s)
            sp.wait_ge(A[0]["x_done"], NT)
            sp.wait_ge(wlo_done, NPAIR)
            sp.dma_start(sel.rearrange("p n m -> p (n m)"), sel_in).then_inc(d_sel, 16)
            sp.wait_ge(M["dn_done"], NCH * ST)
            sp.dma_start(wc, wc_in).then_inc(d_late, 16)
            sp.dma_start(bc, bc_in.rearrange("(a d) -> a d", a=1).to_broadcast([P, H])).then_inc(d_late, 16)
            sp.dma_start(WF, wfc_in).then_inc(d_wf, 16)
            sp.dma_start(WP, wproj_in).then_inc(d_wp, 16)
            with sp.Fori(0, NT - 1, 2) as t:
                for j in range(2):
                    sp.wait_ge(F["y_done"], t + j + 1)
                    stand_alone(sp, side_s)
                    sp.dma_start(ov[:, bass.ds(t + j, 1), :].rearrange("p a h -> p (a h)"), YO[j]).then_inc(stored[j], 16)
            for j in range(2):
                sp.wait_ge(stored[j], 16 * (NT // 2))

        @block.gpsimd
        def _(pool):
            pool.memset(neghalf[:, :], -0.5).then_inc(half_set, 1)
            pool.memset(epsilon[:, :], EPS).then_inc(half_set, 1)
            pool.wait_ge(half_set, 2)

            def rstd(t, j, layer):
                n = STAT_BASE[layer] + t + 1
                pool.wait_ge(ln_mv, n)
                pool.tensor_tensor(ve[:, j, :], mv[:, j, 1:2], epsilon[:, :], ALU.add).then_inc(ln_ve, 1)
                pool.wait_ge(ln_ve, n)
                pool.tensor_tensor(rs[:, j, :], ve[:, j, :], neghalf[:, :], ALU.pow).then_inc(ln_rs, 1)

            def attention(layer, a):
                nk, d, npair, w, _, _ = attention_shape(layer)
                mask, neg = cv(f"mask{layer}"), cv(f"neg{layer}")
                vmask, ones = cv(f"vmask{layer}"), cv(f"ones{layer}")
                if layer == 0:
                    pool.wait_ge(d_small, 16 * 3)
                else:
                    pool.wait_ge(M["ft_done"], NT)
                for j in range(2):
                    for b in range(2):
                        pool.tensor_copy(VD[j][:, b, 0:npair * w].rearrange("p (n w) -> p n w", w=w)[:, :, C:w],
                                         ones.rearrange("p (n k) -> p n k", k=nk)).then_inc(a["vd_set"], 1)

                def step(t, j):
                    if inside(t + 3):
                        rstd(t + 3, 1 - j, 0 if layer == 0 else 2)
                    if inside(t + 2):
                        if past(t, 0):
                            pool.wait_ge(a["sc_ready"], (t + 1) * 2 * (nk // 4))
                        if layer == 0 and known(t) and t == -2:
                            pool.wait_ge(kv_ready, 2)
                            pool.wait_ge(sm_ready, 2)
                        for b in range(2):
                            for dst, keys, m in ((KD1[j], KH, mask), (KD2[j], KL, neg)):
                                pool.tensor_tensor(dst[:, b, 0:nk * S].rearrange("p (k t) -> p k t", k=nk),
                                                   keys[:, bass.ds((t + 2) * 2 + b, 1), :].to_broadcast([P, nk, S]),
                                                   m.unsqueeze(2).to_broadcast([P, nk, S]), ALU.mult).then_inc(a["kd_ready"], 1)
                        if past(t, 0):
                            pool.wait_ge(a["pv_ready"], t + 1)
                        if layer == 0 and known(t) and t == -2:
                            pool.wait_ge(d_ctx, 32)
                        for b in range(2):
                            pool.tensor_tensor(VD[j][:, b, 0:npair * w].rearrange("p (n w) -> p n w", w=w)[:, :, 0:C],
                                               V[:, bass.ds((t + 2) * 2 + b, 1), :].to_broadcast([P, npair, C]),
                                               vmask.rearrange("p (n c) -> p n c", c=C), ALU.mult).then_inc(a["vd_ready"], 1)
                    if layer == 0 and inside(t):
                        pool.wait_ge(d_w, 16 * (t + 1))
                        hi = WH[:, bass.ds(t, 1), :].rearrange("p a w -> p (a w)")
                        lo = WL[:, bass.ds(t, 1), :].rearrange("p a w -> p (a w)")
                        pool.tensor_copy(hi, stage[j]).then_inc(whi_done, 1)
                        pool.wait_ge(whi_done, t + 1)
                        pool.tensor_tensor(lo, stage[j], hi, ALU.subtract).then_inc(wlo_done, 1)

                sweep(pool, step)

            attention(0, A[0])

            def low(n, s):
                pool.wait_ge(M["ih_ready"], n)
                pool.tensor_tensor(IL[s % 3], IN[s % 2], IH[s % 3], ALU.subtract).then_inc(M["il_ready"], 1)

            for t in range(TPC):
                rstd(t, t % 2, 1)

            def chunk(c, back, ahead):
                for s in range(ST):
                    low(c * ST + s + 1, s)
                    if ahead and s % 8 == 0 and s < NPAIR:
                        i = s // 8
                        rstd((c + 1) * TPC + i, i % 2, 1)

            chunks(pool, chunk)
            attention(1, A[1])

            tiles(pool, NT, lambda t, j: rstd(t, j, 3))
            pool.wait_ge(F["am_done"], NT + 3)
            pool.partition_all_reduce(FS[:, 3:6], FS[:, 0:3], P, RMAX).then_inc(F["amx"], 1)
            pool.wait_ge(F["hr"], 1)
            pool.partition_all_reduce(FS[:, 7:8], FS[:, 6:7], P, RMAX).then_inc(F["hmx"], 1)

            def rounded(c, j):
                if past(c, 2):
                    pool.wait_ge(F["y_ready"], (c - 1) * TPC)
                for f in range(NF):
                    pool.wait_ge(F["hu_done"], c * NF + f + 1)
                    pool.tensor_tensor(H8[j][:, f, :], UU[f % 2][:, 0:CH], CC[f % 2][:, 0:CH], ALU.subtract).then_inc(F["h8_ready"], 1)

            tiles(pool, NCH, rounded)

        @block.scalar
        def _(act):
            act.wait_ge(d_small, 16 * 3)
            act.activation(tg[:, :], gate[:, :], ACT.Tanh).then_inc(tanh_done, 1)
            act.wait_ge(d_kt, 32)
            act.copy(KH[:, :, :].rearrange("p b t -> p (b t)"), KF).then_inc(kt_hi, 1)

            def attention(layer, a):
                nk, d, npair, w, nmx, nsc = attention_shape(layer)

                def exps(t, j, u):
                    n = t * 2 * nsc + u
                    back = 4 // (2 * nsc)
                    if past(t, back):
                        act.wait_ge(a["pv_ready"], t - back + 1)
                    act.wait_ge(a["sc_ready"], n + 1)
                    act.activation(EX[(u + (0 if nsc == 2 else 2 * j)) % 4], bank[4 + u % 2][:, :], ACT.Exp,
                                   scale=d ** -0.5).then_inc(a["ex_ready"], 1)

                def step(t, j):
                    if inside(t + 1):
                        if past(t, 1):
                            act.wait_ge(a["sc_ready"], t * 2 * nsc)
                        act.wait_ge(a["t1_ready"], t + 2)
                        act.copy(Q1[1 - j], bank[0][:, :].rearrange("p (g s) -> p g s", g=G)).then_inc(a["q_hi"], 1)
                    if inside(t):
                        for u in range(nsc):
                            exps(t, j, u)
                    if layer == 1 and inside(t - 1):
                        act.wait_ge(a["ont_ready"], t)
                        act.copy(ONT[1 - j], bank[7][:, 0:H].rearrange("p (k t) -> p k t", k=KT)).then_inc(a["onts_ready"], 1)
                    if inside(t):
                        for u in range(nsc, 2 * nsc):
                            exps(t, j, u)
                    if inside(t + 1):
                        act.wait_ge(a["t2_ready"], t + 2)
                        act.copy(Q2[1 - j][0:w], bank[1][0:w, :].rearrange("p (g s) -> p g s", g=G)).then_inc(a["q2_ready"], 1)
                    if inside(t):
                        act.wait_ge(a["pv_ready"], t + 1)
                        if past(t, 1):
                            act.wait_ge(a["ot_ready"], t)
                        act.copy(PVS[0:w].rearrange("p g (b s) -> p g b s", b=2),
                                 bank[6][0:w, :].rearrange("p (b g s) -> p g b s", b=2, g=G)).then_inc(a["pvs_ready"], 1)

                sweep(act, step)

            attention(0, A[0])

            def prep(t, i):
                cols_i = slice(i * P, (i + 1) * P)

                def turn():
                    act.wait_ge(M["tp_ready"], t + 1)
                    act.copy(XNH[:, :, cols_i], bank[7][:, 0:H].rearrange("p (k t) -> p k t", k=KT)).then_inc(M["xt_hi"], 1)

                def exp():
                    act.wait_ge(M["nv_done"], t + 1)
                    act.activation(EXL, LG, ACT.Exp, bias=NV).then_inc(M["ex_done"], 1)

                def weights():
                    act.wait_ge(M["wt_ready"], t + 1)
                    act.copy(WNT[:, cols_i], bank[7][:, 0:P]).then_inc(M["wt_hi"], 1)

                return turn, exp, weights

            act.wait_ge(A[0]["x_done"], NT)
            for t in range(TPC):
                for part in prep(t, t):
                    part()

            def chunk(c, back, ahead):
                base = c * ST

                def silu(s):
                    rows = P if s < NPAIR else I
                    act.wait_ge(M["g_ready"], base + s + 1)
                    if back or s >= 2:
                        act.wait_ge(M["in_ready"], base + max(s - 1, 0))
                    act.activation(SL[s % 2][0:rows, :], bank[s % 2][0:rows, :], ACT.Silu).then_inc(M["sl_ready"], 1)

                def high(s):
                    rows = P if s < NPAIR else I
                    act.wait_ge(M["in_ready"], base + s + 1)
                    if back or s >= 3:
                        act.wait_ge(M["dn_done"], base + s - 2)
                    act.copy(IH[s % 3][0:rows, :], IN[s % 2][0:rows, :]).then_inc(M["ih_ready"], 1)

                for s in range(ST):
                    if s == NPAIR:
                        act.wait_ge(M["z_ready"], c + 1)
                        act.activation(SG[0:I, :], bank[4][0:I, :], ACT.Sigmoid).then_inc(M["sg_ready"], 1)
                    silu(s)
                    if s >= 1:
                        high(s - 1)
                    i, at = s // 8, s % 8
                    if ahead:
                        if s and at == 0:
                            prep((c + 1) * TPC + i - 1, i - 1)[2]()
                        if at == 4:
                            prep((c + 1) * TPC + i, i)[0]()
                        if at == 6:
                            prep((c + 1) * TPC + i, i)[1]()
                high(ST - 1)
                act.wait_ge(M["dn_done"], (c + 1) * ST)
                if back:
                    act.wait_ge(M["ft_ready"], c * TPC)
                for k in range(KT):
                    act.mul(DT[:, k, :], bank[5 + k][:, :], tg[:, 2:3]).then_inc(M["dt_ready"], 1)

            chunks(act, chunk)
            attention(1, A[1])

            act.wait_ge(A[1]["x_done"], NT)

            def keep(t, j):
                act.wait_ge(F["tp_ready"], t + 1)
                act.copy(XF[:, :, bass.ds(t * P, P)], bank[j][:, 0:H].rearrange("p (k t) -> p k t", k=KT)).then_inc(F["xf_ready"], 1)

            tiles(act, NT, keep)
            act.wait_ge(F["ams"], 4)
            act.wait_ge(F["xf_ready"], NT)
            act.wait_ge(d_wf, 16)
            act.wait_ge(d_wp, 16)
            todo = [(XF.rearrange("p k n -> p (k n)"), 17, KT * NT * P), (WF, 18, KT * FF), (WP, 19, NF * H)]
            n = 0
            for src, at, width in todo:
                for m in range(width // (2 * CH)):
                    if n >= 2:
                        act.wait_ge(F["x8_ready"], n - 1)
                    act.activation(CC[n % 2], src[:, m * 2 * CH:(m + 1) * 2 * CH], ACT.Abs, scale=FS[:, at:at + 1]).then_inc(F["abs_ready"], 1)
                    n += 1
            act.wait_ge(F["fs"], 1)

            def squares(c, j):
                def square(f):
                    n = c * NF + f
                    act.wait_ge(F["r_ready"], n + 1)
                    if past(c, 1) or f >= 2:
                        act.wait_ge(F["hu_done"], n - 1)
                    act.activation(HS[f % 2], R[f % 2], ACT.Square).then_inc(F["hs_ready"], 1)

                for f in range(NF):
                    if past(c, 1) or f >= 2:
                        act.wait_ge(F["hs_ready"], c * NF + f - 1)
                    act.wait_ge(F["h_ready"], NCH * NF + c * NF + f + 1)
                    act.activation(R[f % 2], bank[f % 4][:, :], ACT.Relu, scale=FS[:, 16:17]).then_inc(F["r_ready"], 1)
                    if f:
                        square(f - 1)
                square(NF - 1)

            tiles(act, NCH, squares)

        @block.vector
        def _(dve):
            dve.wait_ge(kt_hi, 1)
            dve.tensor_tensor(KL[0:C, :, :].rearrange("p b t -> p (b t)"), KF[0:C, :], KH[0:C, :, :].rearrange("p b t -> p (b t)"),
                              ALU.subtract).then_inc(kv_ready, 1)
            dve.memset(KL[C:P, :, :].rearrange("p b t -> p (b t)"), 1.0).then_inc(kv_ready, 1)
            dve.wait_ge(d_wsm, 32)
            dve.tensor_copy(small_h[:, :, :].rearrange("p k w -> p (k w)"), smf[:, 0:KT * SMW]).then_inc(sm_hi, 1)
            dve.tensor_copy(shd_h[:, :], smf[0:I, KT * SMW:KT * SMW + H]).then_inc(sm_hi, 1)
            dve.wait_ge(sm_hi, 2)
            dve.tensor_tensor(small_l[:, :, :].rearrange("p k w -> p (k w)"), smf[:, 0:KT * SMW],
                              small_h[:, :, :].rearrange("p k w -> p (k w)"), ALU.subtract).then_inc(sm_ready, 1)
            dve.tensor_tensor(shd_l[:, :], smf[0:I, KT * SMW:KT * SMW + H], shd_h[:, :], ALU.subtract).then_inc(sm_ready, 1)

            def stats(t, j, layer):
                n = STAT_BASE[layer] + t + 1
                dve.bn_stats(st[:, j, :], tile_x(t)).then_inc(ln_stats, 1)
                dve.wait_ge(ln_stats, n)
                stand_alone(dve, side_v)
                dve.bn_aggr(mv[:, j, :], st[:, j, :]).then_inc(ln_mv, 1)

            def norm(t, j, layer, dst, src):
                dve.wait_ge(ln_rs, STAT_BASE[layer] + t + 1)
                for d in dst[:-1]:
                    dve.tensor_scalar(d, src, mv[:, j, 0:1], rs[:, j, :], ALU.subtract, ALU.mult).then_inc(ln_twice, 1)
                dve.tensor_scalar(dst[-1], src, mv[:, j, 0:1], rs[:, j, :], ALU.subtract, ALU.mult).then_inc(ln_out, 1)

            def attention(layer, a):
                nk, d, npair, w, nmx, nsc = attention_shape(layer)
                gpu = G // nmx
                ln = 0 if layer == 0 else 2
                if layer == 0:
                    dve.wait_ge(tanh_done, 1)
                else:
                    dve.wait_ge(M["ft_done"], NT)
                    dve.wait_ge(d_late, 16 * 2)
                    dve.tensor_scalar(bcg, bc, tg[:, 1:2], None, ALU.mult).then_inc(bcg_done, 1)
                    dve.wait_ge(bcg_done, 1)

                def heads(ap):
                    return ap.rearrange("p (k g d) -> p g k d", g=G, d=d)

                def maxima(t, j, u):
                    n = t * nmx + u + 1
                    dve.wait_ge(a["mx_ready"], n)
                    dve.tensor_reduce(XG[j][:, u * gpu:(u + 1) * gpu, 2 * C:C + w],
                                      bank[2 + u % 2][:, :].rearrange("p (g k t) -> p g k t", g=gpu, t=S),
                                      AX.X, ALU.max).then_inc(a["mx_done"], 1)

                def step(t, j):
                    if inside(t + 1):
                        dve.wait_ge(a["q_hi"], t + 2)
                        dve.tensor_tensor(Q1[1 - j][C:P], bank[0][C:P, :].rearrange("p (g s) -> p g s", g=G),
                                          Q1[1 - j][C:P], ALU.subtract).then_inc(a["q_ready"], 1)
                    if inside(t - 1):
                        o = bank[7][:, 0:G * w].rearrange("p (g w) -> p g w", g=G)
                        dve.wait_ge(a["ot_ready"], t)
                        dve.reciprocal(RC[:, :, 0:nk], o[:, :, C:w]).then_inc(a["rc_done"], 1)
                        dve.wait_ge(a["rc_done"], t)
                        if layer == 1 and past(t, 3):
                            dve.wait_ge(a["ont_ready"], t - 2)
                        for g in range(G):
                            dve.tensor_tensor(heads(ON[1 - j])[:, g], o[:, g, 0:C].rearrange("p (k d) -> p k d", d=d),
                                              RC[:, g, 0:nk].unsqueeze(2).to_broadcast([P, nk, d]), ALU.mult).then_inc(a["on_ready"], 1)
                    if inside(t + 1):
                        for u in range(nmx // 2):
                            maxima(t + 1, 1 - j, u)
                    if inside(t + 3):
                        if layer == 0 and known(t) and t == -3:
                            dve.wait_ge(d_xa, 16)
                        if layer == 0 and known(t) and t == 1:
                            dve.wait_ge(d_xb, 16)
                        stats(t + 3, 1 - j, ln)
                    if inside(t - 1) and layer == 0:
                        dve.wait_ge(a["on_ready"], G * t)
                        dve.scalar_tensor_tensor(tile_x(t - 1), ON[1 - j], tg[:, 0:1], tile_x(t - 1), ALU.mult, ALU.add).then_inc(a["x_done"], 1)
                    if inside(t + 1):
                        for u in range(nmx // 2, nmx):
                            maxima(t + 1, 1 - j, u)
                    if inside(t + 2):
                        if past(t, 0):
                            dve.wait_ge(a["t2_ready"], t + 1)
                        norm(t + 2, j, ln, [XG[j][:, :, r * C:(r + 1) * C].rearrange("p g (k d) -> p g k d", d=d) for r in range(2)],
                             heads(tile_x(t + 2)))
                    if inside(t - 1) and layer == 1:
                        dve.wait_ge(a["y_ready"], t)
                        dve.scalar_tensor_tensor(tile_x(t - 1), bank[7][:, 0:H], tg[:, 1:2], tile_x(t - 1), ALU.mult, ALU.add).then_inc(a["y_read"], 1)
                        dve.wait_ge(a["y_read"], t)
                        dve.tensor_tensor(tile_x(t - 1), tile_x(t - 1), bcg, ALU.add).then_inc(a["x_done"], 1)

                sweep(dve, step)

            attention(0, A[0])

            dve.wait_ge(A[0]["x_done"], NT)
            dve.wait_ge(wlo_done, NPAIR)

            def prep(t, i):
                cols_i = slice(i * P, (i + 1) * P)

                def measure():
                    stats(t, i % 2, 1)

                def normalise():
                    if past(t, 1):
                        dve.wait_ge(M["tp_ready"], t)
                    norm(t, i % 2, 1, [XN], tile_x(t))

                def turn():
                    dve.wait_ge(M["xt_hi"], t + 1)
                    dve.tensor_tensor(XNL[:, :, cols_i], bank[7][:, 0:H].rearrange("p (k t) -> p k t", k=KT),
                                      XNH[:, :, cols_i], ALU.subtract).then_inc(M["xt_ready"], 1)

                def route():
                    dve.wait_ge(M["lg_ready"], t + 1)
                    dve.tensor_copy(LG, bank[7][:, 0:E]).then_inc(M["lg_done"], 1)
                    dve.wait_ge(M["lg_done"], t + 1)
                    stand_alone(dve, side_v)
                    dve.max(V8, LG).then_inc(M["v8_done"], 1)
                    dve.wait_ge(M["v8_done"], t + 1)
                    dve.tensor_scalar(NV, V8[:, 0:1], -1.0, None, ALU.mult).then_inc(M["nv_done"], 1)
                    dve.match_replace(MR, V8, LG, -3.0e38).then_inc(M["mr_done"], 1)
                    dve.wait_ge(M["mr_done"], t + 1)
                    dve.tensor_tensor(MK, MR, LG, ALU.not_equal).then_inc(M["mk_done"], 1)

                def weigh():
                    dve.wait_ge(M["mk_done"], t + 1)
                    dve.wait_ge(M["ex_done"], t + 1)
                    dve.tensor_tensor(WU, EXL, MK, ALU.mult).then_inc(M["wu_done"], 1)
                    dve.wait_ge(M["wu_done"], 3 * t + 1)
                    dve.tensor_reduce(SU, WU, AX.X, ALU.add).then_inc(M["wu_done"], 1)
                    dve.wait_ge(M["wu_done"], 3 * t + 2)
                    dve.reciprocal(RI, SU).then_inc(M["wu_done"], 1)
                    dve.wait_ge(M["wu_done"], 3 * t + 3)
                    dve.tensor_scalar(WD, WU.unsqueeze(1).to_broadcast([P, 2, E]), RI, None, ALU.mult).then_inc(M["wd_done"], 1)

                def weights():
                    dve.wait_ge(M["wt_hi"], t + 1)
                    dve.tensor_tensor(WNT[E:P, cols_i], bank[7][E:P, 0:P], WNT[E:P, cols_i], ALU.subtract).then_inc(M["wts_ready"], 1)

                return measure, normalise, turn, route, weigh, weights

            def hand_over(c):
                if not (known(c) and c == 0):
                    dve.wait_ge(M["u_ready"], c * ST)
                dve.wait_ge(M["wts_ready"], (c + 1) * TPC)
                dve.wait_ge(M["xt_ready"], (c + 1) * TPC)
                dve.tensor_copy(XCH.rearrange("p k t -> p (k t)"), XNH.rearrange("p k t -> p (k t)")).then_inc(M["turned"], 1)
                dve.tensor_copy(XCL.rearrange("p k t -> p (k t)"), XNL.rearrange("p k t -> p (k t)")).then_inc(M["turned"], 1)
                dve.tensor_copy(WCT, WNT).then_inc(M["turned"], 1)

            for t in range(TPC):
                for part in prep(t, t):
                    part()
            hand_over(0)

            def hand_back(t):
                dve.wait_ge(M["ft_ready"], t + 1)
                dve.tensor_tensor(tile_x(t), tile_x(t), bank[7][:, 0:H], ALU.add).then_inc(M["ft_done"], 1)

            def chunk(c, back, ahead):
                base = c * ST
                for s in range(ST):
                    rows = P if s < NPAIR else I
                    dve.wait_ge(M["sl_ready"], base + s + 1)
                    dve.wait_ge(M["u_ready"], base + s + 1)
                    dve.tensor_tensor(SL[s % 2][0:rows, :], bank[2 + s % 2][0:rows, :], SL[s % 2][0:rows, :],
                                      ALU.mult).then_inc(M["ut_done"], 1)
                    dve.wait_ge(M["ut_done"], base + s + 1)
                    if back or s >= 2:
                        dve.wait_ge(M["il_ready"], base + max(s - 1, 0))
                    if s < NPAIR:
                        dve.wait_ge(M["wb_ready"], c * NPAIR + s + 1)
                        w = bank[4][:, :]
                    else:
                        dve.wait_ge(M["sg_ready"], c + 1)
                        w = SG[0:I, :]
                    dve.tensor_tensor(IN[s % 2][0:rows, :], SL[s % 2][0:rows, :], w, ALU.mult).then_inc(M["in_ready"], 1)
                    i, at = s // 8, s % 8
                    if back and at == 2:
                        hand_back((c - 1) * TPC + i)
                    if ahead:
                        if s and at == 0:
                            prep((c + 1) * TPC + i - 1, i - 1)[5]()
                        for part, place in enumerate((0, 1, 4, 5, 6)):
                            if at == place and s < NPAIR:
                                prep((c + 1) * TPC + i, i)[part]()
                if ahead:
                    hand_over(c + 1)

            chunks(dve, chunk)
            for i in range(TPC):
                hand_back((NCH - 1) * TPC + i)
            attention(1, A[1])

            def biggest(dst, src):
                dve.tensor_reduce(dst, src, AX.X, ALU.max, apply_absolute_value=True).then_inc(F["am_done"], 1)

            dve.wait_ge(A[1]["x_done"], NT)

            def normalise(t, j):
                if past(t, 2):
                    dve.wait_ge(F["tp_ready"], t - 1)
                norm(t, j, 3, [XD[j]], tile_x(t))
                dve.wait_ge(ln_out, STAT_BASE[3] + t + 1)
                dve.tensor_reduce(AM[:, bass.ds(t, 1)], XD[j], AX.X, ALU.max, apply_absolute_value=True).then_inc(F["am_done"], 1)

            stats(0, 0, 3)
            stats(1, 1, 3)
            normalise(0, 0)
            stats(2, 0, 3)
            normalise(1, 1)
            stats(3, 1, 3)
            normalise(2, 0)
            with dve.Fori(3, NT - 2, 2) as t:
                stats(t + 1, 0, 3)
                normalise(t, 1)
                stats(t + 2, 1, 3)
                normalise(t + 1, 0)
            normalise(NT - 1, 1)
            dve.wait_ge(F["am_done"], NT)
            biggest(FS[:, 0:1], AM)
            dve.wait_ge(d_wf, 16)
            biggest(FS[:, 1:2], WF)
            dve.wait_ge(d_wp, 16)
            biggest(FS[:, 2:3], WP)
            dve.wait_ge(F["amx"], 1)
            dve.tensor_scalar(FS[:, 8:11], FS[:, 3:6], 1.0 / FP8_MAX, 1e-6, ALU.mult, ALU.max).then_inc(F["ams"], 1)
            dve.wait_ge(F["ams"], 1)
            dve.reciprocal(FS[:, 11:14], FS[:, 8:11]).then_inc(F["ams"], 1)
            dve.wait_ge(F["ams"], 2)
            dve.tensor_scalar(FS[:, 17:20], FS[:, 11:14], GRID, None, ALU.mult).then_inc(F["ams"], 1)
            dve.tensor_tensor(FS[:, 16:17], FS[:, 8:9], FS[:, 9:10], ALU.mult).then_inc(F["ams"], 1)
            dve.wait_ge(F["ams"], 4)

            def quantise(dst, src, inv, n):
                cc, uu = CC[n % 2], UU[n % 2]
                dve.wait_ge(F["abs_ready"], n + 1)
                dve.tensor_scalar(cc, cc, FLOOR, None, ALU.max).then_inc(F["c_done"], 1)
                dve.wait_ge(F["c_done"], n + 1)
                dve.scalar_tensor_tensor(uu, src, inv, cc, ALU.mult, ALU.add).then_inc(F["u_done"], 1)
                dve.wait_ge(F["u_done"], n + 1)
                dve.tensor_tensor(dst, uu, cc, ALU.subtract).then_inc(F["x8_ready"], 1)

            dve.wait_ge(F["xf_ready"], NT)
            XFf = XF.rearrange("p k n -> p (k n)")
            X8f = X8.rearrange("p k n -> p (k n)")
            for n in range(KT * NT * P // (2 * CH)):
                sl = slice(n * 2 * CH, (n + 1) * 2 * CH)
                quantise(X8f[:, sl], XFf[:, sl], FS[:, 11:12], n)
            nq = KT * NT * P // (2 * CH)
            for k, (dst, src) in enumerate(((WF8, WF), (WP8, WP))):
                for m in range(2):
                    sl = slice(m * 2 * CH, (m + 1) * 2 * CH)
                    quantise(dst.rearrange("p k f -> p (k f)")[:, sl], src[:, sl], FS[:, 12 + k:13 + k], nq)
                    nq += 1
            def largest(c, j):
                for f in range(NF):
                    dve.wait_ge(F["h_ready"], c * NF + f + 1)
                    dve.tensor_reduce(HM[:, bass.ds(c * NF + f, 1)], bank[f % 4][:, :], AX.X, ALU.max).then_inc(F["hm_done"], 1)

            tiles(dve, NCH, largest)
            dve.wait_ge(F["hm_done"], NCH * NF)
            dve.tensor_reduce(FS[:, 6:7], HM, AX.X, ALU.max).then_inc(F["hr"], 1)
            dve.wait_ge(F["hmx"], 1)
            dve.tensor_scalar(FS[:, 20:21], FS[:, 7:8], 0.0, FS[:, 16:17], ALU.max, ALU.mult).then_inc(F["ams"], 1)
            dve.wait_ge(F["ams"], 5)
            dve.tensor_tensor(FS[:, 21:22], FS[:, 20:21], FS[:, 20:21], ALU.mult).then_inc(F["ams"], 1)
            dve.wait_ge(F["ams"], 6)
            dve.tensor_scalar(FS[:, 20:21], FS[:, 21:22], 1.0 / FP8_MAX, 1e-6, ALU.mult, ALU.max).then_inc(F["ams"], 1)
            dve.wait_ge(F["ams"], 7)
            dve.reciprocal(FS[:, 21:22], FS[:, 20:21]).then_inc(F["ams"], 1)
            dve.tensor_scalar(FS[:, 23:24], FS[:, 20:21], FS[:, 10:11], tg[:, 3:4], ALU.mult, ALU.mult).then_inc(F["ams"], 1)
            dve.wait_ge(F["ams"], 9)
            dve.tensor_scalar(FS[:, 22:23], FS[:, 21:22], GRID, None, ALU.mult).then_inc(F["fs"], 1)
            dve.wait_ge(F["fs"], 1)

            def rounding(c, j):
                for f in range(NF):
                    n = c * NF + f
                    dve.wait_ge(F["hs_ready"], n + 1)
                    if past(c, 1) or f >= 2:
                        dve.wait_ge(F["h8_ready"], n - 1)
                    dve.tensor_scalar(CC[f % 2][:, 0:CH], HS[f % 2], FS[:, 22:23], FLOOR, ALU.mult, ALU.max).then_inc(F["hc_done"], 1)
                    dve.wait_ge(F["hc_done"], n + 1)
                    dve.scalar_tensor_tensor(UU[f % 2][:, 0:CH], HS[f % 2], FS[:, 21:22], CC[f % 2][:, 0:CH],
                                             ALU.mult, ALU.add).then_inc(F["hu_done"], 1)
                if past(c, 1):
                    finish(c - 1)

            def finish(c):
                for i in range(TPC):
                    n = c * TPC + i
                    dve.wait_ge(F["y_ready"], n + 1)
                    if past(c, 1) or i >= 2:
                        dve.wait_ge(stored[i % 2], 16 * (c * (TPC // 2) + i // 2))
                    dve.scalar_tensor_tensor(YO[i % 2], bank[4 + i % 2][:, 0:H], FS[:, 23:24], tile_x(n), ALU.mult, ALU.add).then_inc(F["y_done"], 1)

            tiles(dve, NCH, rounding)
            finish(NCH - 1)

        @block.tensor
        def _(pe):
            def attention(layer, a):
                nk, d, npair, w, nmx, nsc = attention_shape(layer)
                gpu = G // nmx
                if layer == 0:
                    pe.wait_ge(d_small, 16 * 3)
                else:
                    pe.wait_ge(M["ft_done"], NT)
                ln = STAT_BASE[0 if layer == 0 else 2]

                def maxima(t, j, u):
                    n = t * nmx + u
                    if past(t, 1) or u >= 2:
                        pe.wait_ge(a["mx_done"], n - 1)
                    for g in range(gpu):
                        for b in range(2):
                            mm = pe.matmul(bank[2 + u % 2][b * S:(b + 1) * S, g * nk * S:(g + 1) * nk * S],
                                           Q1[j][:, u * gpu + g, b * S:(b + 1) * S], KD1[j][:, b, 0:nk * S],
                                           start=True, stop=True)
                    mm.then_inc(a["mx_ready"], 1)

                def scores(t, j, u):
                    n = t * 2 * nsc + u
                    if past(t, 1) or u >= 2:
                        pe.wait_ge(a["ex_ready"], n - 1)
                    b, first = u // nsc, 2 * (u % nsc)
                    for p in range(2):
                        o = bank[4 + u % 2][:, p * 256:(p + 1) * 256]
                        kc = slice((first + p) * P, (first + p + 1) * P)
                        pe.matmul(o, KD1[j][:, b, kc], Q1[j][:, :, b * S:(b + 1) * S], start=True, stop=False)
                        mm = pe.matmul(o, KD2[j][0:w, b, kc], Q2[j][0:w, :, b * S:(b + 1) * S], start=False, stop=True)
                    mm.then_inc(a["sc_ready"], 1)

                def values(t, j, b):
                    if b == 0:
                        pe.wait_ge(a["vd_ready"], 2 * t + 2)
                        if past(t, 1):
                            pe.wait_ge(a["pvs_ready"], t)
                    pe.wait_ge(a["ex_ready"], t * 2 * nsc + (b + 1) * nsc)
                    for p in range(npair):
                        e = EX[(b * nsc + p // 2 + (0 if nsc == 2 else 2 * j)) % 4]
                        mm = pe.matmul(bank[6][0:w, b * 256:(b + 1) * 256], VD[j][:, b, p * w:(p + 1) * w],
                                       e[:, (p % 2) * 256:(p % 2 + 1) * 256], start=(p == 0), stop=(p == npair - 1))
                    if b == 1:
                        mm.then_inc(a["pv_ready"], 1)

                def step(t, j):
                    if inside(t + 1):
                        pe.wait_ge(ln_out, ln + t + 2)
                        if past(t, 0):
                            pe.wait_ge(a["q_ready"], t + 1)
                        for g in range(G):
                            mm = pe.transpose(bank[0][:, g * P:(g + 1) * P],
                                              XG[1 - j][:, g, 0:2 * C], ident)
                        mm.then_inc(a["t1_ready"], 1)
                    if inside(t - 1):
                        pe.wait_ge(a["pvs_ready"], t)
                        if past(t, 2):
                            pe.wait_ge(a["on_ready"], G * (t - 1))
                            if layer == 1:
                                pe.wait_ge(a["y_read"], t - 1)
                        for g in range(G):
                            mm = pe.transpose(bank[7][:, g * w:(g + 1) * w],
                                              PVS[0:w, g, :], ident[0:w, 0:w])
                        mm.then_inc(a["ot_ready"], 1)
                    if inside(t):
                        pe.wait_ge(a["q2_ready"], t + 1)
                        for u in range(nsc):
                            scores(t, j, u)
                    if inside(t + 1):
                        pe.wait_ge(a["q_ready"], t + 2)
                        pe.wait_ge(a["kd_ready"], 4 * (t + 2))
                        for u in range(nmx // 2):
                            maxima(t + 1, 1 - j, u)
                    if inside(t - 1) and layer == 1:
                        pe.wait_ge(a["on_ready"], G * t)
                        for k in range(KT):
                            mm = pe.transpose(bank[7][:, k * P:(k + 1) * P], ON[1 - j][:, k * P:(k + 1) * P], ident)
                        mm.then_inc(a["ont_ready"], 1)
                    if inside(t):
                        for u in range(nsc, 2 * nsc):
                            scores(t, j, u)
                    if inside(t + 1):
                        for u in range(nmx // 2, nmx):
                            maxima(t + 1, 1 - j, u)
                    if inside(t):
                        values(t, j, 0)
                    if inside(t - 1) and layer == 1:
                        pe.wait_ge(a["onts_ready"], t)
                        for k in range(KT):
                            mm = pe.matmul(bank[7][:, 0:H], ONT[1 - j][:, k, :], wc[:, k, :], start=(k == 0), stop=(k == KT - 1))
                        mm.then_inc(a["y_ready"], 1)
                    if inside(t + 1):
                        pe.wait_ge(a["mx_done"], (t + 2) * nmx)
                        if past(t, 0):
                            pe.wait_ge(a["q2_ready"], t + 1)
                        for g in range(G):
                            mm = pe.transpose(bank[1][0:w, g * P:(g + 1) * P], XG[1 - j][:, g, C:C + w], ident)
                        mm.then_inc(a["t2_ready"], 1)
                    if inside(t):
                        values(t, j, 1)

                if layer == 1:
                    pe.wait_ge(d_late, 16 * 2)
                pe.wait_ge(A[layer]["vd_set"], 4)
                sweep(pe, step)

            attention(0, A[0])

            def prep(t, i):
                def turn(after):
                    pe.wait_ge(ln_out, STAT_BASE[1] + t + 1)
                    after()
                    for k in range(KT):
                        mm = pe.transpose(bank[7][:, k * P:(k + 1) * P], XN[:, k * P:(k + 1) * P], ident)
                    mm.then_inc(M["tp_ready"], 1)

                def logits():
                    pe.wait_ge(M["xt_ready"], t + 1)
                    n = 0
                    for k in range(KT):
                        for xx, ww in ((XNH, small_h), (XNH, small_l), (XNL, small_h)):
                            mm = pe.matmul(bank[7][:, 0:E], xx[:, k, i * P:(i + 1) * P], ww[:, k, 0:E], start=(n == 0), stop=(n == 3 * KT - 1))
                            n += 1
                    mm.then_inc(M["lg_ready"], 1)

                def weights():
                    pe.wait_ge(M["wd_done"], t + 1)
                    pe.transpose(bank[7][:, 0:P], WD.rearrange("p a e -> p (a e)"), ident).then_inc(M["wt_ready"], 1)

                return turn, logits, weights

            pe.wait_ge(A[0]["x_done"], NT)
            pe.wait_ge(sm_ready, 2)
            pe.wait_ge(d_sel, 16)
            pe.wait_ge(wlo_done, NPAIR)
            for t in range(TPC):
                turn, logits, weights = prep(t, t)
                turn(lambda: pe.wait_ge(M["wts_ready"], t) if t else None)
                logits()
                weights()

            def chunk(c, back, ahead):
                base = c * ST
                pe.wait_ge(M["turned"], 3 * (c + 1))

                def into(o, wh, wl, m0, rows):
                    n = 0
                    for k in range(KT):
                        for ww, xx in ((wh, XCH), (wl, XCH), (wh, XCL)):
                            mm = pe.matmul(o, ww(k), xx[:, k, :], start=(n == 0), stop=(n == 3 * KT - 1))
                            n += 1
                    return mm

                def gate_up(s):
                    if back or s >= 2:
                        pe.wait_ge(M["sl_ready"], base + max(s - 1, 0))
                    rows = P if s < NPAIR else I
                    for part, (b, done) in enumerate(((bank[s % 2], "g_ready"), (bank[2 + s % 2], "u_ready"))):
                        if part and (back or s >= 2):
                            pe.wait_ge(M["ut_done"], base + max(s - 1, 0))
                        if s < NPAIR:
                            cc = lambda k: slice((2 * k + part) * P, (2 * k + part + 1) * P)
                            mm = into(b[:, :], lambda k: WH[:, s, cc(k)], lambda k: WL[:, s, cc(k)], 0, rows)
                        else:
                            cc = slice(E * (part + 1), E * (part + 2))
                            mm = into(b[0:I, :], lambda k: small_h[:, k, cc], lambda k: small_l[:, k, cc], 0, rows)
                        mm.then_inc(M[done], 1)
                        if part == 0:
                            if back or s >= 1:
                                pe.wait_ge(M["in_ready"], base + s)
                            if s < NPAIR:
                                pe.matmul(bank[4][:, :], sel[:, s, :], WCT, start=True, stop=True).then_inc(M["wb_ready"], 1)
                            else:
                                z = slice(3 * E, 4 * E)
                                into(bank[4][0:I, :], lambda k: small_h[:, k, z], lambda k: small_l[:, k, z], 0, I).then_inc(M["z_ready"], 1)

                def down(s):
                    pe.wait_ge(M["il_ready"], base + s + 1)
                    if s == 0 and back:
                        pe.wait_ge(M["dt_ready"], KT * c)
                    rows = P if s < NPAIR else I
                    for k in range(KT):
                        hc = slice(k * P, (k + 1) * P)
                        wh = WH[:, s, 2 * KT * P:PW] if s < NPAIR else shd_h[:, :]
                        wl = WL[:, s, 2 * KT * P:PW] if s < NPAIR else shd_l[:, :]
                        for n, (ww, ii) in enumerate(((wh, IH), (wl, IH), (wh, IL))):
                            mm = pe.matmul(bank[5 + k][:, :], ww[:, hc], ii[s % 3][0:rows, :],
                                           start=(s == 0 and n == 0), stop=(s == ST - 1 and n == 2))
                    mm.then_inc(M["dn_done"], 1)
                def turn_back(t, i):
                    if i == 0:
                        pe.wait_ge(M["dt_ready"], KT * c)
                    for k in range(KT):
                        mm = pe.transpose(bank[7][:, k * P:(k + 1) * P], DT[:, k, i * P:(i + 1) * P], ident)
                    mm.then_inc(M["ft_ready"], 1)

                for s in range(ST):
                    gate_up(s)
                    if s >= 2:
                        down(s - 2)
                    if s == NPAIR:
                        break
                    i = s // 8
                    if back and s % 8 == 1:
                        t = (c - 1) * TPC + i
                        if ahead or i == 0:
                            pe.wait_ge(M["wts_ready"], (c + 1) * TPC + i)
                        else:
                            pe.wait_ge(M["ft_done"], t)
                        turn_back(t, i)
                    if ahead:
                        turn, logits, weights = prep((c + 1) * TPC + i, i)
                        if s % 8 == 3:
                            if back:
                                turn(lambda: pe.wait_ge(M["ft_done"], (c - 1) * TPC + i + 1))
                            else:
                                turn(lambda: pe.wait_ge(M["wts_ready"], TPC + i))
                        if s % 8 == 5:
                            logits()
                        if s % 8 == 7:
                            weights()
                down(ST - 2)
                down(ST - 1)

            chunks(pe, chunk)
            for i in range(TPC):
                t = (NCH - 1) * TPC + i
                pe.wait_ge(M["ft_done"], t)
                pe.wait_ge(M["dt_ready"], KT * NCH)
                for k in range(KT):
                    mm = pe.transpose(bank[7][:, k * P:(k + 1) * P], DT[:, k, i * P:(i + 1) * P], ident)
                mm.then_inc(M["ft_ready"], 1)
            attention(1, A[1])

            pe.wait_ge(A[1]["x_done"], NT)

            def turn_x(t, j):
                pe.wait_ge(ln_out, STAT_BASE[3] + t + 1)
                if past(t, 2):
                    pe.wait_ge(F["xf_ready"], t - 1)
                for k in range(KT):
                    mm = pe.transpose(bank[j][:, k * P:(k + 1) * P], XD[j][:, k * P:(k + 1) * P], ident)
                mm.then_inc(F["tp_ready"], 1)

            tiles(pe, NT, turn_x)
            pe.wait_ge(F["x8_ready"], KT * NT * P // (2 * CH) + 4)

            def hidden(c, f, free):
                if past(c, 1) or f >= 4:
                    pe.wait_ge(free, c * NF + f - 3)
                for k in range(KT):
                    mm = pe.matmul(bank[f % 4][:, :], WF8[:, k, f * P:(f + 1) * P], X8[:, k, bass.ds(c * CH, CH)],
                                   start=(k == 0), stop=(k == KT - 1))
                mm.then_inc(F["h_ready"], 1)

            def first_pass(c, j):
                for f in range(NF):
                    hidden(c, f, F["hm_done"])

            def project(c, j):
                pe.wait_ge(F["h8_ready"], (c + 1) * NF)
                for i in range(TPC):
                    if past(c, 1) or i >= 2:
                        pe.wait_ge(F["y_done"], c * TPC + i - 1)
                    for f in range(NF):
                        mm = pe.matmul(bank[4 + i % 2][:, 0:H], H8[j][:, f, i * P:(i + 1) * P], WP8[:, f, :], start=(f == 0), stop=(f == NF - 1))
                    mm.then_inc(F["y_ready"], 1)

            def second_pass(c, j):
                for f in range(NF):
                    hidden(c, f, F["r_ready"])
                if past(c, 1):
                    project(c - 1, 1 - j)

            tiles(pe, NCH, first_pass)
            pe.wait_ge(F["hm_done"], NCH * NF)
            tiles(pe, NCH, second_pass)
            project(NCH - 1, (NCH - 1) % 2)


def kernel(**inputs):
    import concourse.bacc as bacc
    from concourse.bass_utils import run_bass_kernel_spmd as run

    a = {k: np.asarray(v) for k, v in inputs.items()}
    ctx = a["ctx_512"]

    def by_k(w):
        return w.T.reshape(KT, P, -1).transpose(1, 0, 2)

    gu = a["L0_ffn_gu_w"].reshape(NPAIR, 2, 2, I, KT, P).transpose(5, 0, 4, 2, 1, 3).reshape(P, NPAIR, KT * 2 * P)
    dp = a["L0_ffn_dp_w"].reshape(NPAIR, 2, H, I).transpose(1, 3, 0, 2).reshape(P, NPAIR, H)
    small = np.concatenate([by_k(a["L0_ffn_gate_w"]), by_k(a["L0_ffn_sh_gate_w"]), by_k(a["L0_ffn_sh_up_w"]),
                            by_k(np.broadcast_to(a["L0_ffn_sh_gate1_w"], (E, H)))], axis=2)
    arrays = {
        "x": a["x"].reshape(B * S, H),
        "ctx": ctx,
        "ctxT": ctx.transpose(2, 0, 1).reshape(C, B * S),
        "g_xattn": a["g_xattn"],
        "g_ffn": a["g_ffn"],
        "consts": const_table(),
        "selectors": selectors(),
        "wpairs": np.concatenate([gu, dp], axis=2),
        "wsmall": small.reshape(P, KT * SMW),
        "wshdown": a["L0_ffn_sh_down_w"].T,
        "wc": by_k(a["L1_xattn_Wc"]),
        "bc": a["L1_xattn_bc"],
        "wfc": by_k(a["L1_ffn_w_fc"]).reshape(P, KT * FF),
        "wproj": a["L1_ffn_w_proj"].T.reshape(NF, P, H).transpose(1, 0, 2).reshape(P, NF * H),
    }
    nc = bacc.Bacc("TRN2", target_bir_lowering=False, num_devices=1)
    data, args = {}, {}
    for name, v in arrays.items():
        v = np.ascontiguousarray(v)
        data[f"in_{name}"] = v
        args[name] = nc.dram_tensor(f"in_{name}", v.shape, mybir.dt.from_np(v.dtype), kind="ExternalInput").ap()
    out = nc.dram_tensor("out", (B * S, H), F32, kind="ExternalOutput").ap()
    flamingo_block(nc, args["x"], args["ctx"], args["ctxT"], (args["g_xattn"], args["g_ffn"]), args["consts"], args["selectors"],
                   args["wpairs"], args["wsmall"], args["wshdown"], args["wc"], args["bc"], args["wfc"], args["wproj"], out)
    r = run(nc, [data], core_ids=[0])
    return r.results[0]["out"].reshape(B, S, H)
```

```python
import numpy as np
import concourse.bass as bass
from concourse import mybir

ALU = mybir.AluOpType
ACT = mybir.ActivationFunctionType
AX = mybir.AxisListType
F32 = mybir.dt.float32
F16 = mybir.dt.float16
BF16 = mybir.dt.bfloat16
RMAX = bass.bass_isa.ReduceOp.max

P = 128
B, S, H = 64, 64, 256
C = 64
NT = B * S // P
G = 4
E, I = 64, 64
NPAIR = E // 2
CH = 512
NCH = B * S // CH
TPC = CH // P
KT = H // P
FF = 1024
NF = FF // P
NWB = 4
PW = KT * 2 * P + H
SMW = 4 * 64
EPS = 1e-5
FP8_MAX = 448.0
GRID = float(2 ** 20)
FLOOR = 1.5 * 2.0 ** 14
LAST = (NT, NT + 2)
LAYERS = ((8, 8), (4, 16))


def const_columns():
    at, out = 0, {}
    for name, width in (("ident", P), ("mask0", 8), ("mask1", 4), ("neg0", 8), ("neg1", 4),
                        ("vmask0", 4 * C), ("vmask1", 2 * C), ("ones0", 4 * 8), ("ones1", 2 * 4)):
        out[name] = (at, width)
        at += width
    return out, at


def const_table():
    cols, width = const_columns()
    t = np.zeros((P, width), np.float32)
    r = np.arange(P)[:, None]

    def put(name, block):
        a, w = cols[name]
        t[:, a:a + w] = block.reshape(P, w)

    put("ident", np.eye(P))
    for layer, (nk, d) in enumerate(LAYERS):
        k = np.arange(nk)[None, :]
        put(f"mask{layer}", (r % C) // d == k)
        put(f"neg{layer}", np.where(r < C, r // d == k, -1.0 * (r - C == k)))
        pair = np.arange(nk // 2)[None, :, None]
        head = 2 * pair + (r[:, :, None] >= S)
        put(f"vmask{layer}", np.arange(C)[None, None, :] // d == head)
        put(f"ones{layer}", np.arange(nk)[None, None, :] == head)
    return t


def known(t):
    return isinstance(t, int)


def stand_alone(eng, side):
    eng.sem_inc(side, 1)


def inside(t):
    return not known(t) or 0 <= t < NT


def past(t, n):
    return not known(t) or t >= n


def sweep(eng, step, last):
    for t in range(-3, 4):
        step(t, t % 2)
    with eng.Fori(4, NT - 5, 2) as t:
        step(t, 0)
        step(t + 1, 1)
    for t in range(NT - 4, last + 1):
        step(t, t % 2)


def chunks(eng, body):
    body(0, False, True)
    with eng.Fori(1, NCH - 1) as c:
        body(c, True, True)
    body(NCH - 1, True, False)


def tiles(eng, n, body, tail=0):
    body(0, 0)
    body(1, 1)
    with eng.Fori(2, n - tail - 1, 2) as t:
        body(t, 0)
        body(t + 1, 1)
    for t in range(n - tail, n):
        body(t, t % 2)


def flamingo_block(nc, x_in, ctx, ctxT, gates, consts, wpairs, wsmall, wshdown, wc_in, bc_in, wfc_in, wproj_in, out):
    sb = lambda name, shape, dt=F32: nc.alloc_sbuf_tensor(name, shape, dt)
    sem = nc.alloc_semaphore

    cols, CW = const_columns()
    x = sb("x", [P, NT, H])
    cst = sb("cst", [P, CW])
    region = sb("region", [P, NPAIR * PW * 2], F16)
    WH = region[:, 0:NPAIR * PW].rearrange("p (n w) -> p n w", w=PW)
    WL = region[:, NPAIR * PW:2 * NPAIR * PW].rearrange("p (n w) -> p n w", w=PW)
    V = sb("V", [P, B, C])
    KH = sb("KH", [P, B, S], F16)
    KL = sb("KL", [P, B, S], F16)
    gate = sb("gate", [P, 4])
    tg = sb("tg", [P, 4])
    neghalf = sb("neghalf", [P, 1])
    epsilon = sb("epsilon", [P, 1])
    small_h = sb("small_h", [P, KT, SMW], F16)
    small_l = sb("small_l", [P, KT, SMW], F16)
    shd_h = sb("shd_h", [I, H], F16)
    shd_l = sb("shd_l", [I, H], F16)

    AM, HM, FS = sb("AM", [P, NT]), sb("HM", [P, NCH * NF]), sb("FS", [P, 24])
    st = sb("st", [P, 4, 6])
    mv = sb("mv", [P, 4, 2])
    ve = sb("ve", [P, 4, 1])
    rs = sb("rs", [P, 4, 1])

    arena_bytes = 41 * 1024 + 512
    arena = sb("arena", [P, arena_bytes // 4])
    used = [0]

    def carve(shape, dt=F32):
        n = int(np.prod(shape))
        size = 4 if dt == F32 else 2
        a = used[0]
        used[0] += -(-n * size // 64) * 16
        assert used[0] <= arena_bytes // 4, used[0] * 4
        v = arena[:, a:a + -(-n * size // 4)]
        if dt != F32:
            v = v.bitcast(dt)
        if len(shape) == 2:
            v = v.rearrange("p (a b) -> p a b", b=shape[1])
        if len(shape) == 3:
            v = v.rearrange("p (a b c) -> p a b c", b=shape[1], c=shape[2])
        if len(shape) == 4:
            v = v.rearrange("p (a b c d) -> p a b c d", b=shape[1], c=shape[2], d=shape[3])
        return v

    W0 = C + 8
    XG = [carve([G, C + W0]) for _ in range(2)]
    Q1 = [carve([G, P], F16) for _ in range(2)]
    Q2 = [carve([G, P], F16) for _ in range(2)]
    KD1 = [carve([2, 8 * S], F16) for _ in range(2)]
    KD2 = [carve([2, 8 * S], F16) for _ in range(2)]
    VD = [carve([2, 4 * W0]) for _ in range(2)]
    EX = [carve([512]) for _ in range(4)]
    PVS = carve([G, P])
    RC = carve([G, 8])
    ON = [carve([H]) for _ in range(2)]
    ont_at = used[0]
    stage = [carve([PW]) for _ in range(2)]
    used[0] = ont_at
    ONT = [carve([KT, P]) for _ in range(2)]
    XD = [carve([H]) for _ in range(2)]
    used[0] = 0
    XN = carve([H])
    XNH, XNL = carve([KT, CH], F16), carve([KT, CH], F16)
    XCH, XCL = carve([KT, CH], F16), carve([KT, CH], F16)
    WNT = carve([CH])
    LG, MR, EXL, MK, WU = carve([E]), carve([E]), carve([E]), carve([E]), carve([E])
    WD = carve([2, E])
    V8, NV, SU, RI = carve([8]), carve([1]), carve([1]), carve([1])
    SL = [carve([CH]) for _ in range(2)]
    IN = [carve([CH]) for _ in range(2)]
    IH = [carve([CH], F16) for _ in range(3)]
    IL = [carve([CH], F16) for _ in range(3)]
    SG = carve([CH])
    DT = carve([KT, CH])
    WB = [carve([CH]) for _ in range(NWB)]
    routing = nc.dram_tensor("routing", (NCH, E, CH), F32, kind="Internal").ap()
    used[0] = 0
    R, HS, CC, UU = ([carve([CH]) for _ in range(4)] for _ in range(4))
    YO = [carve([H]) for _ in range(TPC)]
    CX = [arena[:, n * 2 * CH:(n + 1) * 2 * CH] for n in range(2)]
    UX = [arena[:, n * 2 * CH:(n + 1) * 2 * CH] for n in range(2, 4)]
    fr = region[:, :].bitcast(F32)
    XF = fr[:, 0:KT * NT * P].rearrange("p (k n) -> p k n", k=KT)
    WF = fr[:, 8192:8192 + KT * FF]
    WP = fr[:, 10240:10240 + NF * H]
    wc = fr[:, 22528:23040].rearrange("p (k h) -> p k h", k=KT)
    bc, bcg = fr[:, 23040:23296], fr[:, 23296:23552]
    hb = region[:, 24576:].bitcast(BF16)
    CW8, UW8 = ([fr[:, 12288 + 1024 * n:12288 + 1024 * (n + 1)] for n in (2 * m, 2 * m + 1)] for m in range(2))
    X8 = hb[:, 0:KT * NT * P].rearrange("p (k n) -> p k n", k=KT)
    WF8 = hb[:, 8192:8192 + KT * FF].rearrange("p (k f) -> p k f", k=KT)
    WP8 = hb[:, 10240:10240 + NF * H].rearrange("p (f h) -> p f h", f=NF)
    H8 = [hb[:, 12288 + 4096 * n:12288 + 4096 * (n + 1)].rearrange("p (f t) -> p f t", f=NF) for n in range(2)]

    bank = [nc.alloc_psum_tensor(f"bank{n}", [P, 512], F32) for n in range(8)]

    def cv(name):
        a, w = cols[name]
        return cst[:, a:a + w]

    ident = cv("ident")

    d_small, d_late, d_w = (sem(n) for n in ("d_small", "d_late", "d_w"))
    d_wb = [sem(f"d_wb{i}") for i in range(NWB)]
    routed = sem("routed")
    d_x, d_kt, d_ctx = ([sem(f"{n}{part}") for part in range(2)] for n in ("d_x", "d_kt", "d_ctx"))
    FIRST = ((0, 8), (8, B))
    d_wsm, d_wf, d_wp = (sem(n) for n in ("d_wsm", "d_wf", "d_wp"))
    stored = [sem(f"stored{i}") for i in range(TPC)]
    kt_hi, kv_ready, kv_ones, tanh_done = sem("kt_hi"), sem("kv_ready"), sem("kv_ones"), sem("tanh_done")
    whi_done, wlo_done = sem("whi_done"), sem("wlo_done")
    sm_hi, sm_ready, bcg_done, half_set = sem("sm_hi"), sem("sm_ready"), sem("bcg_done"), sem("half_set")
    side_v, side_s = sem("side_vector"), sem("side_sync")
    lnames = ("stats", "mv", "ve", "rs", "twice", "out")
    LNA = {n: sem("ln_" + n) for n in lnames}
    LND = {n: sem("lnd_" + n) for n in lnames}
    names = ("t1_ready", "q_hi", "q_ready", "kd_ready", "kl_ready", "bias_in", "vd_set", "vd_ready", "mx_ready", "mx_done", "t2_ready", "q2_ready",
             "sc_ready", "ex_ready", "pv_ready", "pvs_ready", "ot_ready", "rc_done", "rg_done", "on_ready",
             "ont_ready", "onts_ready", "y_ready", "x_done")
    A = [{n: sem(f"{n}{layer}") for n in names} for layer in range(2)]

    KF = region[:, NPAIR * PW * 2 - 2 * B * S:].bitcast(F32)
    smf = region[:, NPAIR * PW * 2 - 2 * B * S - 2 * (KT * SMW + H):NPAIR * PW * 2 - 2 * B * S].bitcast(F32)

    STAT_BASE = [0, NT, 2 * NT, 0]
    LNS = [LNA, LNA, LNA, LND]

    xv = x_in.rearrange("(n p) h -> p n h", p=P)
    ov = out.rearrange("(n p) h -> p n h", p=P)

    def tile_x(t):
        return x[:, bass.ds(t, 1), :].rearrange("p a h -> p (a h)") if not known(t) else x[:, t, :]

    def attention_shape(layer):
        nk, d = LAYERS[layer]
        return nk, d, nk // 2, C + nk, G * nk * S // 512, nk // 4

    mnames = ("tp_ready", "xt_hi", "xt_ready", "lg_ready", "lg_done", "v8_done", "mr_done", "nv_done", "ex_done", "mk_done",
              "wu_done", "ri_done", "wd_done", "wt_ready", "wts_ready", "turned",
              "g_ready", "u_ready", "sl_ready", "ut_done", "in_ready", "ih_ready", "il_ready", "dn_done",
              "z_ready", "sg_ready", "dt_ready", "ft_ready", "ft_done")
    M = {n: sem("m_" + n) for n in mnames}
    ST = NPAIR + 1
    fnames = ("tp_ready", "xf_ready", "am_done", "amx", "ams", "abs_ready", "c_done", "u_done", "x8_ready",
              "wam", "wamx", "was", "wabs", "wc_done", "wu_done", "w8_ready", "hm_done", "hmx",
              "hr", "fs", "h_ready", "r_ready", "hs_ready", "hc_done", "hu_done", "h8_ready", "y_ready", "y_done")
    F = {n: sem("f_" + n) for n in fnames}

    with nc.Block() as block:

        @block.sync
        def _(sp):
            sp.dma_start(cst[:, :], consts).then_inc(d_small, 16)
            sp.dma_start(x[:, 0:4, :], xv[:, 0:4, :]).then_inc(d_x[0], 16)
            for n, g in enumerate(gates):
                sp.dma_start(gate[:, 2 * n:2 * n + 2], g.rearrange("(a d) -> a d", a=1).to_broadcast([P, 2])).then_inc(d_small, 16)
            for part, (b0, b1) in enumerate(FIRST):
                for half in range(2):
                    sp.dma_start(KF[half * C:(half + 1) * C, b0 * S:b1 * S], ctxT[:, b0 * S:b1 * S]).then_inc(d_kt[part], 16)
                for half in range(2):
                    sp.dma_start(V[half * S:(half + 1) * S, b0:b1, :], ctx[b0:b1].rearrange("b t c -> t b c")).then_inc(d_ctx[part], 16)
            sp.dma_start(x[:, 4:NT, :], xv[:, 4:NT, :]).then_inc(d_x[1], 16)
            sp.dma_start(smf[:, 0:KT * SMW], wsmall).then_inc(d_wsm, 16)
            sp.dma_start(smf[0:I, KT * SMW:KT * SMW + H], wshdown).then_inc(d_wsm, 16)
            for n in range(2):
                sp.dma_start(stage[n], wpairs[:, n, :]).then_inc(d_w, 16)
                sp.wait_ge(d_w, 16 * (n + 1))
            with sp.Fori(2, NPAIR - 1, 2) as n:
                for j in range(2):
                    sp.wait_ge(wlo_done, n + j - 1)
                    stand_alone(sp, side_s)
                    sp.dma_start(stage[j], wpairs[:, bass.ds(n + j, 1), :].rearrange("p a w -> p (a w)")).then_inc(d_w, 16)
                    sp.wait_ge(d_w, 16 * (n + j + 1))
                    stand_alone(sp, side_s)
            sp.wait_ge(A[0]["x_done"], NT)
            sp.wait_ge(wlo_done, NPAIR)

            def route(c):
                sp.wait_ge(M["wts_ready"], (c + 1) * TPC)
                stand_alone(sp, side_s)
                sp.dma_start(routing[bass.ds(c, 1)].rearrange("a e t -> (a e) t"), WNT[0:E, :]).then_inc(routed, 16)
                sp.wait_ge(routed, 16 * (c + 1))
                stand_alone(sp, side_s)

            def spread(c, back, ahead):
                for s in range(NPAIR):
                    if back or s >= NWB:
                        sp.wait_ge(M["in_ready"], c * ST + s + 1 - NWB - (s < NWB))
                        stand_alone(sp, side_s)
                    for half in range(2):
                        sp.dma_start(WB[s % NWB][half * I:(half + 1) * I, :],
                                     routing[bass.ds(c, 1), 2 * s + half, :].to_broadcast([I, CH])).then_inc(d_wb[s % NWB], 16)
                if ahead:
                    route(c + 1)

            route(0)
            chunks(sp, spread)
            sp.wait_ge(M["dn_done"], NCH * ST)
            sp.dma_start(wc, wc_in).then_inc(d_late, 16)
            sp.dma_start(bc, bc_in.rearrange("(a d) -> a d", a=1).to_broadcast([P, H])).then_inc(d_late, 16)
            sp.dma_start(WF, wfc_in).then_inc(d_wf, 16)
            sp.dma_start(WP, wproj_in).then_inc(d_wp, 16)
            with sp.Fori(0, NCH) as c:
                for i in range(TPC):
                    sp.wait_ge(F["y_done"], c * TPC + i + 1)
                    stand_alone(sp, side_s)
                    sp.dma_start(ov[:, bass.ds(c * TPC + i, 1), :].rearrange("p a h -> p (a h)"), YO[i]).then_inc(stored[i], 16)
            for i in range(TPC):
                sp.wait_ge(stored[i], 16 * NCH)

        @block.gpsimd
        def _(pool):
            pool.memset(neghalf[:, :], -0.5).then_inc(half_set, 1)
            pool.memset(epsilon[:, :], EPS).then_inc(half_set, 1)
            pool.wait_ge(half_set, 2)
            pool.memset(KL[C:P, :, :].rearrange("p b t -> p (b t)"), 1.0).then_inc(kv_ones, 1)
            pool.wait_ge(kv_ones, 1)

            def rstd(t, j, layer):
                n, l = STAT_BASE[layer] + t + 1, LNS[layer]
                pool.wait_ge(l["mv"], n)
                pool.tensor_tensor(ve[:, j, :], mv[:, j, 1:2], epsilon[:, :], ALU.add).then_inc(l["ve"], 1)
                pool.wait_ge(l["ve"], n)
                pool.tensor_tensor(rs[:, j, :], ve[:, j, :], neghalf[:, :], ALU.pow).then_inc(l["rs"], 1)

            def attention(layer, a):
                nk, d, npair, w, _, _ = attention_shape(layer)
                mask, neg = cv(f"mask{layer}"), cv(f"neg{layer}")
                vmask, ones = cv(f"vmask{layer}"), cv(f"ones{layer}")
                if layer == 0:
                    pool.wait_ge(d_small, 16 * 3)
                else:
                    pool.wait_ge(M["ft_done"], NT)
                for j in range(2):
                    for b in range(2):
                        pool.tensor_copy(VD[j][:, b, 0:npair * w].rearrange("p (n w) -> p n w", w=w)[:, :, C:w],
                                         ones.rearrange("p (n k) -> p n k", k=nk)).then_inc(a["vd_set"], 1)

                def diagonal(t, dst, keys, m, done):
                    for b in range(2):
                        pool.tensor_tensor(dst[:, b, 0:nk * S].rearrange("p (k t) -> p k t", k=nk),
                                           keys[:, bass.ds(t * 2 + b, 1), :].to_broadcast([P, nk, S]),
                                           m.unsqueeze(2).to_broadcast([P, nk, S]), ALU.mult).then_inc(done, 1)

                def step(t, j):
                    if layer == 1 and known(t) and t == -2:
                        pool.wait_ge(F["wam"], 2)
                        pool.partition_all_reduce(FS[:, 4:6], FS[:, 1:3], P, RMAX).then_inc(F["wamx"], 1)
                    if inside(t + 2):
                        if past(t, 0):
                            pool.wait_ge(a["sc_ready"], (t + 1) * 2 * (nk // 4))
                        if layer == 0 and known(t) and t in (-2, 2):
                            pool.wait_ge(kv_ready, 1 if t < 0 else 2)
                            pool.wait_ge(d_ctx[t > 0], 32)
                        diagonal(t + 2, KD1[j], KH, mask, a["kd_ready"])
                    if layer == 1 and inside(t - 2):
                        rstd(t - 2, 2 + j, 3)
                    if inside(t + 3):
                        rstd(t + 3, 1 - j, 0 if layer == 0 else 2)
                    if inside(t + 2):
                        diagonal(t + 2, KD2[j], KL, neg, a["kl_ready"])
                    if layer == 1 and inside(t):
                        pool.wait_ge(LNA["out"], STAT_BASE[2] + t + 1)
                        pool.tensor_tensor(tile_x(t), tile_x(t), bcg, ALU.add).then_inc(a["bias_in"], 1)
                    if inside(t + 2):
                        if past(t, 0):
                            pool.wait_ge(a["pv_ready"], t + 1)
                        for b in range(2):
                            pool.tensor_tensor(VD[j][:, b, 0:npair * w].rearrange("p (n w) -> p n w", w=w)[:, :, 0:C],
                                               V[:, bass.ds((t + 2) * 2 + b, 1), :].to_broadcast([P, npair, C]),
                                               vmask.rearrange("p (n c) -> p n c", c=C), ALU.mult).then_inc(a["vd_ready"], 1)

                sweep(pool, step, LAST[layer])

            attention(0, A[0])

            def low(n, s):
                pool.wait_ge(M["ih_ready"], n)
                pool.tensor_tensor(IL[s % 3], IN[s % 2], IH[s % 3], ALU.subtract).then_inc(M["il_ready"], 1)

            for t in range(TPC):
                rstd(t, t % 2, 1)

            def chunk(c, back, ahead):
                for s in range(ST):
                    low(c * ST + s + 1, s)
                    if ahead and s % 8 == 0 and s < NPAIR:
                        i = s // 8
                        rstd((c + 1) * TPC + i, i % 2, 1)

            chunks(pool, chunk)
            attention(1, A[1])

            pool.wait_ge(F["am_done"], NT + 1)
            pool.partition_all_reduce(FS[:, 3:4], FS[:, 0:1], P, RMAX).then_inc(F["amx"], 1)

            def rounded_x(c, j):
                pool.wait_ge(F["u_done"], c + 1)
                pool.tensor_tensor(X8[:, :, bass.ds(c * CH, CH)], UX[j].rearrange("p (k t) -> p k t", k=KT),
                                   CX[j].rearrange("p (k t) -> p k t", k=KT), ALU.subtract).then_inc(F["x8_ready"], 1)

            tiles(pool, NCH, rounded_x)
            pool.wait_ge(F["hr"], 1)
            pool.partition_all_reduce(FS[:, 7:8], FS[:, 6:7], P, RMAX).then_inc(F["hmx"], 1)

            def rounded(c, j):
                if past(c, 2):
                    pool.wait_ge(F["y_ready"], (c - 1) * TPC)
                for f in range(NF):
                    pool.wait_ge(F["hu_done"], c * NF + f + 1)
                    pool.tensor_tensor(H8[j][:, f, :], UU[f % 4], CC[f % 4], ALU.subtract).then_inc(F["h8_ready"], 1)

            tiles(pool, NCH, rounded)

        @block.scalar
        def _(act):
            act.wait_ge(d_small, 16 * 3)
            act.activation(tg[:, :], gate[:, :], ACT.Tanh).then_inc(tanh_done, 1)
            for part, (b0, b1) in enumerate(FIRST):
                act.wait_ge(d_kt[part], 32)
                act.copy(KH[:, b0:b1, :].rearrange("p b t -> p (b t)"), KF[:, b0 * S:b1 * S]).then_inc(kt_hi, 1)

            def attention(layer, a):
                nk, d, npair, w, nmx, nsc = attention_shape(layer)

                def exps(t, j, u):
                    n = t * 2 * nsc + u
                    back = 4 // (2 * nsc)
                    if past(t, back):
                        act.wait_ge(a["pv_ready"], t - back + 1)
                    act.wait_ge(a["sc_ready"], n + 1)
                    act.activation(EX[(u + (0 if nsc == 2 else 2 * j)) % 4], bank[4 + u % 2][:, :], ACT.Exp,
                                   scale=d ** -0.5).then_inc(a["ex_ready"], 1)

                def step(t, j):
                    if inside(t):
                        for u in range(nsc):
                            exps(t, j, u)
                    if layer == 1 and known(t) and -1 <= t < 3:
                        n = t + 1
                        act.wait_ge(F["was"], 3)
                        if n >= 2:
                            act.wait_ge(F["w8_ready"], n - 1)
                        src = (WF, WP)[n // 2][:, (n % 2) * 2 * CH:(n % 2 + 1) * 2 * CH]
                        act.activation(CW8[n % 2], src, ACT.Abs, scale=FS[:, 18 + n // 2:19 + n // 2]).then_inc(F["wabs"], 1)
                    if layer == 0 and inside(t):
                        act.wait_ge(d_w, 16 * (t + 1))
                        act.copy(WH[:, bass.ds(t, 1), :].rearrange("p a w -> p (a w)"), stage[j]).then_inc(whi_done, 1)
                    if inside(t):
                        for u in range(nsc, 2 * nsc):
                            exps(t, j, u)
                    if inside(t + 2):
                        if past(t, 0):
                            act.wait_ge(a["sc_ready"], (t + 1) * 2 * nsc)
                        act.wait_ge(a["t1_ready"], t + 3)
                        act.copy(Q1[j], bank[0][:, :].rearrange("p (g s) -> p g s", g=G)).then_inc(a["q_hi"], 1)
                    if layer == 1 and inside(t - 1):
                        act.wait_ge(a["ont_ready"], t)
                        act.copy(ONT[1 - j], bank[7][:, 0:H].rearrange("p (k t) -> p k t", k=KT)).then_inc(a["onts_ready"], 1)
                    if inside(t + 1):
                        act.wait_ge(a["t2_ready"], t + 2)
                        act.copy(Q2[1 - j][0:w], bank[1][0:w, :].rearrange("p (g s) -> p g s", g=G)).then_inc(a["q2_ready"], 1)
                    if inside(t):
                        act.wait_ge(a["pv_ready"], t + 1)
                        if past(t, 1):
                            act.wait_ge(a["ot_ready"], t)
                        act.copy(PVS[0:w].rearrange("p g (b s) -> p g b s", b=2),
                                 bank[6][0:w, :].rearrange("p (b g s) -> p g b s", b=2, g=G)).then_inc(a["pvs_ready"], 1)
                    if layer == 1 and inside(t - 3):
                        act.wait_ge(F["tp_ready"], t - 2)
                        act.copy(XF[:, :, bass.ds((t - 3) * P, P)], bank[0][:, 0:H].rearrange("p (k t) -> p k t", k=KT)).then_inc(F["xf_ready"], 1)

                sweep(act, step, LAST[layer])

            attention(0, A[0])

            def prep(t, i):
                cols_i = slice(i * P, (i + 1) * P)

                def turn():
                    act.wait_ge(M["tp_ready"], t + 1)
                    act.copy(XNH[:, :, cols_i], bank[7][:, 0:H].rearrange("p (k t) -> p k t", k=KT)).then_inc(M["xt_hi"], 1)

                def exp():
                    act.wait_ge(M["nv_done"], t + 1)
                    act.activation(EXL, LG, ACT.Exp, bias=NV).then_inc(M["ex_done"], 1)

                def weights(before):
                    act.wait_ge(M["wt_ready"], t + 1)
                    if i == 0 and not (known(before) and before == 0):
                        act.wait_ge(routed, 16 * before)
                    act.copy(WNT[0:E, cols_i], bank[7][0:E, 0:P]).then_inc(M["wts_ready"], 1)

                return turn, exp, weights

            act.wait_ge(A[0]["x_done"], NT)
            for t in range(TPC):
                turn, exp, weights = prep(t, t)
                turn()
                exp()
                weights(0)

            def chunk(c, back, ahead):
                base = c * ST

                def silu(s):
                    rows = P if s < NPAIR else I
                    act.wait_ge(M["g_ready"], base + s + 1)
                    if back or s >= 2:
                        act.wait_ge(M["in_ready"], base + max(s - 1, 0))
                    act.activation(SL[s % 2][0:rows, :], bank[s % 2][0:rows, :], ACT.Silu).then_inc(M["sl_ready"], 1)

                def high(s):
                    rows = P if s < NPAIR else I
                    act.wait_ge(M["in_ready"], base + s + 1)
                    if back or s >= 3:
                        act.wait_ge(M["dn_done"], base + s - 2)
                    act.copy(IH[s % 3][0:rows, :], IN[s % 2][0:rows, :]).then_inc(M["ih_ready"], 1)

                for s in range(ST):
                    if s == NPAIR:
                        act.wait_ge(M["z_ready"], c + 1)
                        act.activation(SG[0:I, :], bank[4][0:I, :], ACT.Sigmoid).then_inc(M["sg_ready"], 1)
                    silu(s)
                    if s >= 1:
                        high(s - 1)
                    i, at = s // 8, s % 8
                    if ahead:
                        if at == 3:
                            prep((c + 1) * TPC + i, i)[0]()
                        if at == 5:
                            prep((c + 1) * TPC + i, i)[1]()
                        if at == 7:
                            prep((c + 1) * TPC + i, i)[2](c + 1)
                high(ST - 1)
                act.wait_ge(M["dn_done"], (c + 1) * ST)
                if back:
                    act.wait_ge(M["ft_ready"], c * TPC)
                for k in range(KT):
                    act.mul(DT[:, k, :], bank[5 + k][:, :], tg[:, 2:3]).then_inc(M["dt_ready"], 1)

            chunks(act, chunk)
            attention(1, A[1])

            act.wait_ge(F["ams"], 4)
            act.wait_ge(F["xf_ready"], NT)

            def magnitudes(c, j):
                if past(c, 2):
                    act.wait_ge(F["x8_ready"], c - 1)
                act.activation(CX[j].rearrange("p (k t) -> p k t", k=KT), XF[:, :, bass.ds(c * CH, CH)], ACT.Abs,
                               scale=FS[:, 17:18]).then_inc(F["abs_ready"], 1)

            tiles(act, NCH, magnitudes)
            act.wait_ge(F["fs"], 1)

            def squares(c, j):
                def square(f):
                    n = c * NF + f
                    act.wait_ge(F["r_ready"], n + 1)
                    if past(c, 1) or f >= 4:
                        act.wait_ge(F["hu_done"], n - 3)
                    act.activation(HS[f % 4], R[f % 4], ACT.Square).then_inc(F["hs_ready"], 1)

                for f in range(NF):
                    if past(c, 1) or f >= 4:
                        act.wait_ge(F["hs_ready"], c * NF + f - 3)
                    act.wait_ge(F["h_ready"], NCH * NF + c * NF + f + 1)
                    act.activation(R[f % 4], bank[f % 4][:, :], ACT.Relu, scale=FS[:, 16:17]).then_inc(F["r_ready"], 1)
                    if f:
                        square(f - 1)
                square(NF - 1)

            tiles(act, NCH, squares)

        @block.vector
        def _(dve):
            def low_keys(part):
                b0, b1 = FIRST[part]
                dve.wait_ge(kt_hi, part + 1)
                dve.tensor_tensor(KL[0:C, b0:b1, :].rearrange("p b t -> p (b t)"), KF[0:C, b0 * S:b1 * S],
                                  KH[0:C, b0:b1, :].rearrange("p b t -> p (b t)"), ALU.subtract).then_inc(kv_ready, 1)

            def small_halves():
                dve.wait_ge(d_wsm, 32)
                dve.tensor_copy(small_h[:, :, :].rearrange("p k w -> p (k w)"), smf[:, 0:KT * SMW]).then_inc(sm_hi, 1)
                dve.tensor_copy(shd_h[:, :], smf[0:I, KT * SMW:KT * SMW + H]).then_inc(sm_hi, 1)
                dve.wait_ge(sm_hi, 2)
                dve.tensor_tensor(small_l[:, :, :].rearrange("p k w -> p (k w)"), smf[:, 0:KT * SMW],
                                  small_h[:, :, :].rearrange("p k w -> p (k w)"), ALU.subtract).then_inc(sm_ready, 1)
                dve.tensor_tensor(shd_l[:, :], smf[0:I, KT * SMW:KT * SMW + H], shd_h[:, :], ALU.subtract).then_inc(sm_ready, 1)

            def stats(t, j, layer):
                n, l = STAT_BASE[layer] + t + 1, LNS[layer]
                dve.bn_stats(st[:, j, :], tile_x(t)).then_inc(l["stats"], 1)
                dve.wait_ge(l["stats"], n)
                stand_alone(dve, side_v)
                dve.bn_aggr(mv[:, j, :], st[:, j, :]).then_inc(l["mv"], 1)

            def norm(t, j, layer, dst, src):
                l = LNS[layer]
                dve.wait_ge(l["rs"], STAT_BASE[layer] + t + 1)
                for d in dst[:-1]:
                    dve.tensor_scalar(d, src, mv[:, j, 0:1], rs[:, j, :], ALU.subtract, ALU.mult).then_inc(l["twice"], 1)
                dve.tensor_scalar(dst[-1], src, mv[:, j, 0:1], rs[:, j, :], ALU.subtract, ALU.mult).then_inc(l["out"], 1)

            def biggest(dst, src, done):
                dve.tensor_reduce(dst, src, AX.X, ALU.max, apply_absolute_value=True).then_inc(done, 1)

            def weight_scales(t):
                if t == -3:
                    dve.wait_ge(d_wf, 16)
                    biggest(FS[:, 1:2], WF, F["wam"])
                    dve.wait_ge(d_wp, 16)
                    biggest(FS[:, 2:3], WP, F["wam"])
                else:
                    dve.wait_ge(F["wamx"], 1)
                    dve.tensor_scalar(FS[:, 9:11], FS[:, 4:6], 1.0 / FP8_MAX, 1e-6, ALU.mult, ALU.max).then_inc(F["was"], 1)
                    dve.wait_ge(F["was"], 1)
                    dve.reciprocal(FS[:, 12:14], FS[:, 9:11]).then_inc(F["was"], 1)
                    dve.wait_ge(F["was"], 2)
                    dve.tensor_scalar(FS[:, 18:20], FS[:, 12:14], GRID, None, ALU.mult).then_inc(F["was"], 1)

            def quantise(src, inv, cc, uu, n, kind):
                dve.wait_ge(F[{"w": "wabs", "": "abs_ready"}[kind]], n + 1)
                dve.tensor_scalar(cc, cc, FLOOR, None, ALU.max).then_inc(F[kind + "c_done"], 1)
                dve.wait_ge(F[kind + "c_done"], n + 1)
                dve.scalar_tensor_tensor(uu, src, inv, cc, ALU.mult, ALU.add).then_inc(F[kind + "u_done"], 1)

            def attention(layer, a):
                nk, d, npair, w, nmx, nsc = attention_shape(layer)
                gpu = G // nmx
                ln = 0 if layer == 0 else 2
                if layer == 0:
                    low_keys(0)
                    dve.wait_ge(tanh_done, 1)
                else:
                    dve.wait_ge(M["ft_done"], NT)
                    dve.wait_ge(d_late, 16 * 2)
                    dve.tensor_scalar(bcg, bc, tg[:, 1:2], None, ALU.mult).then_inc(bcg_done, 1)
                    dve.wait_ge(bcg_done, 1)

                def heads(ap):
                    return ap.rearrange("p (k g d) -> p g k d", g=G, d=d)

                def maxima(t, j, u):
                    n = t * nmx + u + 1
                    dve.wait_ge(a["mx_ready"], n)
                    dve.tensor_reduce(XG[j][:, u * gpu:(u + 1) * gpu, 2 * C:C + w],
                                      bank[2 + u % 2][:, :].rearrange("p (g k t) -> p g k t", g=gpu, t=S),
                                      AX.X, ALU.max).then_inc(a["mx_done"], 1)

                def step(t, j):
                    if layer == 1 and known(t) and t in (-3, -1):
                        weight_scales(t)
                    if inside(t + 1):
                        for u in range(nmx // 2):
                            maxima(t + 1, 1 - j, u)
                    if inside(t - 1):
                        o = bank[7][:, 0:G * w].rearrange("p (g w) -> p g w", g=G)
                        dve.wait_ge(a["ot_ready"], t)
                        dve.reciprocal(RC[:, :, 0:nk], o[:, :, C:w]).then_inc(a["rc_done"], 1)
                        dve.wait_ge(a["rc_done"], t)
                        if layer == 1 and past(t, 3):
                            dve.wait_ge(a["ont_ready"], t - 2)
                        dve.tensor_tensor(heads(ON[1 - j]), o[:, :, 0:C].rearrange("p g (k d) -> p g k d", d=d),
                                          RC[:, :, 0:nk].unsqueeze(3).to_broadcast([P, G, nk, d]), ALU.mult).then_inc(a["on_ready"], 1)
                    if inside(t + 1):
                        for u in range(nmx // 2, nmx):
                            maxima(t + 1, 1 - j, u)
                    if layer == 1 and inside(t - 2):
                        dve.wait_ge(a["x_done"], t - 1)
                        stand_alone(dve, side_v)
                        stats(t - 2, 2 + j, 3)
                    if inside(t + 3):
                        if layer == 0 and known(t) and t == -3:
                            dve.wait_ge(d_x[0], 16)
                        if layer == 0 and known(t) and t == 1:
                            dve.wait_ge(d_x[1], 16)
                        stats(t + 3, 1 - j, ln)
                    if inside(t - 1) and layer == 0:
                        dve.wait_ge(a["on_ready"], t)
                        dve.scalar_tensor_tensor(tile_x(t - 1), ON[1 - j], tg[:, 0:1], tile_x(t - 1), ALU.mult, ALU.add).then_inc(a["x_done"], 1)
                    if layer == 0 and inside(t):
                        dve.wait_ge(whi_done, t + 1)
                        dve.tensor_tensor(WL[:, bass.ds(t, 1), :].rearrange("p a w -> p (a w)"), stage[j],
                                          WH[:, bass.ds(t, 1), :].rearrange("p a w -> p (a w)"), ALU.subtract).then_inc(wlo_done, 1)
                    if inside(t + 2):
                        dve.wait_ge(a["q_hi"], t + 3)
                        dve.tensor_tensor(Q1[j][C:P], bank[0][C:P, :].rearrange("p (g s) -> p g s", g=G),
                                          Q1[j][C:P], ALU.subtract).then_inc(a["q_ready"], 1)
                    if inside(t + 3):
                        if past(t, -1):
                            dve.wait_ge(a["t2_ready"], t + 2)
                        norm(t + 3, 1 - j, ln, [XG[1 - j][:, :, r * C:(r + 1) * C].rearrange("p g (k d) -> p g k d", d=d) for r in range(2)],
                             heads(tile_x(t + 3)))
                    if layer == 1 and inside(t - 2):
                        if past(t, 4):
                            dve.wait_ge(F["tp_ready"], t - 3)
                        norm(t - 2, 2 + j, 3, [XD[j]], tile_x(t - 2))
                        dve.wait_ge(LND["out"], t - 1)
                        dve.tensor_reduce(AM[:, bass.ds(t - 2, 1)], XD[j], AX.X, ALU.max, apply_absolute_value=True).then_inc(F["am_done"], 1)
                    if inside(t - 1) and layer == 1:
                        dve.wait_ge(a["y_ready"], t)
                        dve.wait_ge(a["bias_in"], t)
                        dve.scalar_tensor_tensor(tile_x(t - 1), bank[1][:, 0:H], tg[:, 1:2], tile_x(t - 1), ALU.mult, ALU.add).then_inc(a["x_done"], 1)
                    if layer == 1 and known(t) and 0 <= t < 4:
                        src = (WF, WP)[t // 2][:, (t % 2) * 2 * CH:(t % 2 + 1) * 2 * CH]
                        dst = (WF8, WP8)[t // 2].rearrange("p k f -> p (k f)")[:, (t % 2) * 2 * CH:(t % 2 + 1) * 2 * CH]
                        quantise(src, FS[:, 12 + t // 2:13 + t // 2], CW8[t % 2], UW8[t % 2], t, "w")
                        dve.wait_ge(F["wu_done"], t + 1)
                        dve.tensor_tensor(dst, UW8[t % 2], CW8[t % 2], ALU.subtract).then_inc(F["w8_ready"], 1)
                    if layer == 0 and known(t) and t == 0:
                        low_keys(1)
                        small_halves()

                sweep(dve, step, LAST[layer])

            attention(0, A[0])

            dve.wait_ge(A[0]["x_done"], NT)
            dve.wait_ge(wlo_done, NPAIR)

            def prep(t, i):
                cols_i = slice(i * P, (i + 1) * P)

                def measure():
                    stats(t, i % 2, 1)

                def normalise():
                    if past(t, 1):
                        dve.wait_ge(M["tp_ready"], t)
                    norm(t, i % 2, 1, [XN], tile_x(t))

                def turn():
                    dve.wait_ge(M["xt_hi"], t + 1)
                    dve.tensor_tensor(XNL[:, :, cols_i], bank[7][:, 0:H].rearrange("p (k t) -> p k t", k=KT),
                                      XNH[:, :, cols_i], ALU.subtract).then_inc(M["xt_ready"], 1)

                def route():
                    dve.wait_ge(M["lg_ready"], t + 1)
                    dve.tensor_copy(LG, bank[7][:, 0:E]).then_inc(M["lg_done"], 1)
                    dve.wait_ge(M["lg_done"], t + 1)
                    stand_alone(dve, side_v)
                    dve.max(V8, LG).then_inc(M["v8_done"], 1)
                    dve.wait_ge(M["v8_done"], t + 1)
                    dve.tensor_scalar(NV, V8[:, 0:1], -1.0, None, ALU.mult).then_inc(M["nv_done"], 1)
                    dve.match_replace(MR, V8, LG, -3.0e38).then_inc(M["mr_done"], 1)
                    dve.wait_ge(M["mr_done"], t + 1)
                    dve.tensor_tensor(MK, MR, LG, ALU.not_equal).then_inc(M["mk_done"], 1)

                def weigh():
                    dve.wait_ge(M["mk_done"], t + 1)
                    dve.wait_ge(M["ex_done"], t + 1)
                    dve.tensor_tensor(WU, EXL, MK, ALU.mult).then_inc(M["wu_done"], 1)
                    dve.wait_ge(M["wu_done"], 3 * t + 1)
                    dve.tensor_reduce(SU, WU, AX.X, ALU.add).then_inc(M["wu_done"], 1)
                    dve.wait_ge(M["wu_done"], 3 * t + 2)
                    dve.reciprocal(RI, SU).then_inc(M["wu_done"], 1)
                    dve.wait_ge(M["wu_done"], 3 * t + 3)
                    dve.tensor_scalar(WD, WU.unsqueeze(1).to_broadcast([P, 2, E]), RI, None, ALU.mult).then_inc(M["wd_done"], 1)

                return measure, normalise, turn, route, weigh

            def hand_over(c):
                if not (known(c) and c == 0):
                    dve.wait_ge(M["u_ready"], c * ST)
                dve.wait_ge(M["xt_ready"], (c + 1) * TPC)
                dve.tensor_copy(XCH.rearrange("p k t -> p (k t)"), XNH.rearrange("p k t -> p (k t)")).then_inc(M["turned"], 1)
                dve.tensor_copy(XCL.rearrange("p k t -> p (k t)"), XNL.rearrange("p k t -> p (k t)")).then_inc(M["turned"], 1)

            for t in range(TPC):
                for part in prep(t, t):
                    part()
            hand_over(0)

            def hand_back(t):
                dve.wait_ge(M["ft_ready"], t + 1)
                dve.tensor_tensor(tile_x(t), tile_x(t), bank[7][:, 0:H], ALU.add).then_inc(M["ft_done"], 1)

            def chunk(c, back, ahead):
                base = c * ST
                for s in range(ST):
                    rows = P if s < NPAIR else I
                    dve.wait_ge(M["sl_ready"], base + s + 1)
                    dve.wait_ge(M["u_ready"], base + s + 1)
                    dve.tensor_tensor(SL[s % 2][0:rows, :], bank[2 + s % 2][0:rows, :], SL[s % 2][0:rows, :],
                                      ALU.mult).then_inc(M["ut_done"], 1)
                    dve.wait_ge(M["ut_done"], base + s + 1)
                    if back or s >= 2:
                        dve.wait_ge(M["il_ready"], base + max(s - 1, 0))
                    if s < NPAIR:
                        dve.wait_ge(d_wb[s % NWB], 32 * (c * (NPAIR // NWB) + s // NWB + 1))
                        w = WB[s % NWB]
                    else:
                        dve.wait_ge(M["sg_ready"], c + 1)
                        w = SG[0:I, :]
                    dve.tensor_tensor(IN[s % 2][0:rows, :], SL[s % 2][0:rows, :], w, ALU.mult).then_inc(M["in_ready"], 1)
                    i, at = s // 8, s % 8
                    if back and at == 1 and s < NPAIR:
                        hand_back((c - 1) * TPC + i)
                    if ahead:
                        for part, place in enumerate((0, 1, 3, 4, 5)):
                            if at == place and s < NPAIR:
                                prep((c + 1) * TPC + i, i)[part]()
                if ahead:
                    hand_over(c + 1)

            chunks(dve, chunk)
            for i in range(TPC):
                hand_back((NCH - 1) * TPC + i)
            attention(1, A[1])

            dve.wait_ge(F["am_done"], NT)
            biggest(FS[:, 0:1], AM[:, :], F["am_done"])
            dve.wait_ge(F["amx"], 1)
            dve.tensor_scalar(FS[:, 8:9], FS[:, 3:4], 1.0 / FP8_MAX, 1e-6, ALU.mult, ALU.max).then_inc(F["ams"], 1)
            dve.wait_ge(F["ams"], 1)
            dve.reciprocal(FS[:, 11:12], FS[:, 8:9]).then_inc(F["ams"], 1)
            dve.wait_ge(F["ams"], 2)
            dve.tensor_scalar(FS[:, 17:18], FS[:, 11:12], GRID, None, ALU.mult).then_inc(F["ams"], 1)
            dve.tensor_tensor(FS[:, 16:17], FS[:, 8:9], FS[:, 9:10], ALU.mult).then_inc(F["ams"], 1)
            dve.wait_ge(F["ams"], 4)

            def round_x(c, j):
                both = lambda ap: ap.rearrange("p (k t) -> p k t", k=KT)
                if past(c, 2):
                    dve.wait_ge(F["x8_ready"], c - 1)
                quantise(XF[:, :, bass.ds(c * CH, CH)], FS[:, 11:12], both(CX[j]), both(UX[j]), c, "")

            def first_pass(c, j):
                if not known(c) or c + 1 < NCH:
                    round_x(c + 1, 1 - j)
                for f in range(NF):
                    dve.wait_ge(F["h_ready"], c * NF + f + 1)
                    dve.tensor_reduce(HM[:, bass.ds(c * NF + f, 1)], bank[f % 4][:, :], AX.X, ALU.max).then_inc(F["hm_done"], 1)

            round_x(0, 0)
            tiles(dve, NCH, first_pass, 2)
            dve.wait_ge(F["hm_done"], NCH * NF)
            dve.tensor_reduce(FS[:, 6:7], HM[:, :], AX.X, ALU.max).then_inc(F["hr"], 1)
            dve.wait_ge(F["hmx"], 1)
            dve.tensor_scalar(FS[:, 20:21], FS[:, 7:8], 0.0, FS[:, 16:17], ALU.max, ALU.mult).then_inc(F["ams"], 1)
            dve.wait_ge(F["ams"], 5)
            dve.tensor_tensor(FS[:, 21:22], FS[:, 20:21], FS[:, 20:21], ALU.mult).then_inc(F["ams"], 1)
            dve.wait_ge(F["ams"], 6)
            dve.tensor_scalar(FS[:, 20:21], FS[:, 21:22], 1.0 / FP8_MAX, 1e-6, ALU.mult, ALU.max).then_inc(F["ams"], 1)
            dve.wait_ge(F["ams"], 7)
            dve.reciprocal(FS[:, 21:22], FS[:, 20:21]).then_inc(F["ams"], 1)
            dve.tensor_scalar(FS[:, 23:24], FS[:, 20:21], FS[:, 10:11], tg[:, 3:4], ALU.mult, ALU.mult).then_inc(F["ams"], 1)
            dve.wait_ge(F["ams"], 9)
            dve.tensor_scalar(FS[:, 22:23], FS[:, 21:22], GRID, None, ALU.mult).then_inc(F["fs"], 1)
            dve.wait_ge(F["fs"], 1)

            def rounding(c, j):
                for f in range(NF):
                    n = c * NF + f
                    dve.wait_ge(F["hs_ready"], n + 1)
                    if past(c, 1) or f >= 4:
                        dve.wait_ge(F["h8_ready"], n - 3)
                    dve.tensor_scalar(CC[f % 4], HS[f % 4], FS[:, 22:23], FLOOR, ALU.mult, ALU.max).then_inc(F["hc_done"], 1)
                    dve.wait_ge(F["hc_done"], n + 1)
                    dve.scalar_tensor_tensor(UU[f % 4], HS[f % 4], FS[:, 21:22], CC[f % 4],
                                             ALU.mult, ALU.add).then_inc(F["hu_done"], 1)
                if past(c, 1):
                    finish(c - 1)

            def finish(c):
                for i in range(TPC):
                    n = c * TPC + i
                    dve.wait_ge(F["y_ready"], n + 1)
                    if past(c, 1):
                        dve.wait_ge(stored[i], 16 * c)
                    dve.scalar_tensor_tensor(YO[i], bank[4 + i][:, 0:H], FS[:, 23:24], tile_x(n), ALU.mult, ALU.add).then_inc(F["y_done"], 1)

            tiles(dve, NCH, rounding)
            finish(NCH - 1)

        @block.tensor
        def _(pe):
            def attention(layer, a):
                nk, d, npair, w, nmx, nsc = attention_shape(layer)
                gpu = G // nmx
                if layer == 0:
                    pe.wait_ge(d_small, 16 * 3)
                else:
                    pe.wait_ge(M["ft_done"], NT)
                ln = STAT_BASE[0 if layer == 0 else 2]

                def maxima(t, j, u):
                    n = t * nmx + u
                    if past(t, 1) or u >= 2:
                        pe.wait_ge(a["mx_done"], n - 1)
                    for g in range(gpu):
                        for b in range(2):
                            mm = pe.matmul(bank[2 + u % 2][b * S:(b + 1) * S, g * nk * S:(g + 1) * nk * S],
                                           Q1[j][:, u * gpu + g, b * S:(b + 1) * S], KD1[j][:, b, 0:nk * S],
                                           start=True, stop=True)
                    mm.then_inc(a["mx_ready"], 1)

                def scores(t, j, u):
                    n = t * 2 * nsc + u
                    if past(t, 1) or u >= 2:
                        pe.wait_ge(a["ex_ready"], n - 1)
                    b, first = u // nsc, 2 * (u % nsc)
                    for p in range(2):
                        o = bank[4 + u % 2][:, p * 256:(p + 1) * 256]
                        kc = slice((first + p) * P, (first + p + 1) * P)
                        pe.matmul(o, KD1[j][:, b, kc], Q1[j][:, :, b * S:(b + 1) * S], start=True, stop=False)
                        mm = pe.matmul(o, KD2[j][0:w, b, kc], Q2[j][0:w, :, b * S:(b + 1) * S], start=False, stop=True)
                    mm.then_inc(a["sc_ready"], 1)

                def values(t, j, b):
                    if b == 0:
                        pe.wait_ge(a["vd_ready"], 2 * t + 2)
                        if past(t, 1):
                            pe.wait_ge(a["pvs_ready"], t)
                    pe.wait_ge(a["ex_ready"], t * 2 * nsc + (b + 1) * nsc)
                    for p in range(npair):
                        e = EX[(b * nsc + p // 2 + (0 if nsc == 2 else 2 * j)) % 4]
                        mm = pe.matmul(bank[6][0:w, b * 256:(b + 1) * 256], VD[j][:, b, p * w:(p + 1) * w],
                                       e[:, (p % 2) * 256:(p % 2 + 1) * 256], start=(p == 0), stop=(p == npair - 1))
                    if b == 1:
                        mm.then_inc(a["pv_ready"], 1)

                def step(t, j):
                    if inside(t + 1):
                        pe.wait_ge(a["q_ready"], t + 2)
                        pe.wait_ge(a["kd_ready"], 2 * (t + 2))
                        for u in range(nmx // 2):
                            maxima(t + 1, 1 - j, u)
                    if inside(t):
                        pe.wait_ge(a["q2_ready"], t + 1)
                        pe.wait_ge(a["kl_ready"], 2 * (t + 1))
                        for u in range(nsc):
                            scores(t, j, u)
                    if inside(t - 1):
                        pe.wait_ge(a["pvs_ready"], t)
                        if past(t, 2):
                            pe.wait_ge(a["on_ready"], t - 1)
                            if layer == 1:
                                pe.wait_ge(a["onts_ready"], t - 1)
                        for g in range(G):
                            mm = pe.transpose(bank[7][:, g * w:(g + 1) * w],
                                              PVS[0:w, g, :], ident[0:w, 0:w])
                        mm.then_inc(a["ot_ready"], 1)
                    if inside(t):
                        for u in range(nsc, 2 * nsc):
                            scores(t, j, u)
                    if inside(t + 1):
                        for u in range(nmx // 2, nmx):
                            maxima(t + 1, 1 - j, u)
                    if inside(t + 2):
                        pe.wait_ge(LNA["out"], ln + t + 3)
                        if past(t, -1):
                            pe.wait_ge(a["q_ready"], t + 2)
                        if layer == 1 and past(t, 4):
                            pe.wait_ge(F["xf_ready"], t - 3)
                        for g in range(G):
                            mm = pe.transpose(bank[0][:, g * P:(g + 1) * P],
                                              XG[j][:, g, 0:2 * C], ident)
                        mm.then_inc(a["t1_ready"], 1)
                    if inside(t):
                        values(t, j, 0)
                    if inside(t - 1) and layer == 1:
                        pe.wait_ge(a["on_ready"], t)
                        for k in range(KT):
                            mm = pe.transpose(bank[7][:, k * P:(k + 1) * P], ON[1 - j][:, k * P:(k + 1) * P], ident)
                        mm.then_inc(a["ont_ready"], 1)
                    if inside(t + 1):
                        pe.wait_ge(a["mx_done"], (t + 2) * nmx)
                        if past(t, 0):
                            pe.wait_ge(a["q2_ready"], t + 1)
                        if layer == 1 and past(t, 2):
                            pe.wait_ge(a["x_done"], t - 1)
                        for g in range(G):
                            mm = pe.transpose(bank[1][0:w, g * P:(g + 1) * P], XG[1 - j][:, g, C:C + w], ident)
                        mm.then_inc(a["t2_ready"], 1)
                    if inside(t):
                        values(t, j, 1)
                    if inside(t - 1) and layer == 1:
                        pe.wait_ge(a["onts_ready"], t)
                        pe.wait_ge(a["q2_ready"], min(t + 2, NT) if known(t) else t + 2)
                        for k in range(KT):
                            mm = pe.matmul(bank[1][:, 0:H], ONT[1 - j][:, k, :], wc[:, k, :], start=(k == 0), stop=(k == KT - 1))
                        mm.then_inc(a["y_ready"], 1)
                    if layer == 1 and inside(t - 3):
                        pe.wait_ge(LND["out"], t - 2)
                        pe.wait_ge(a["q_ready"], min(t + 3, NT) if known(t) else t + 3)
                        if past(t, 4):
                            pe.wait_ge(F["xf_ready"], t - 3)
                        for k in range(KT):
                            mm = pe.transpose(bank[0][:, k * P:(k + 1) * P], XD[1 - j][:, k * P:(k + 1) * P], ident)
                        mm.then_inc(F["tp_ready"], 1)

                if layer == 1:
                    pe.wait_ge(d_late, 16 * 2)
                pe.wait_ge(A[layer]["vd_set"], 4)
                sweep(pe, step, LAST[layer])

            attention(0, A[0])

            def prep(t, i):
                def turn(after):
                    pe.wait_ge(LNA["out"], STAT_BASE[1] + t + 1)
                    after()
                    for k in range(KT):
                        mm = pe.transpose(bank[7][:, k * P:(k + 1) * P], XN[:, k * P:(k + 1) * P], ident)
                    mm.then_inc(M["tp_ready"], 1)

                def logits():
                    pe.wait_ge(M["xt_ready"], t + 1)
                    n = 0
                    for k in range(KT):
                        for xx, ww in ((XNH, small_h), (XNH, small_l), (XNL, small_h)):
                            mm = pe.matmul(bank[7][:, 0:E], xx[:, k, i * P:(i + 1) * P], ww[:, k, 0:E], start=(n == 0), stop=(n == 3 * KT - 1))
                            n += 1
                    mm.then_inc(M["lg_ready"], 1)

                def weights():
                    pe.wait_ge(M["wd_done"], t + 1)
                    pe.transpose(bank[7][:, 0:P], WD.rearrange("p a e -> p (a e)"), ident).then_inc(M["wt_ready"], 1)

                return turn, logits, weights

            pe.wait_ge(A[0]["x_done"], NT)
            pe.wait_ge(sm_ready, 2)
            pe.wait_ge(wlo_done, NPAIR)
            for t in range(TPC):
                turn, logits, weights = prep(t, t)
                turn(lambda: pe.wait_ge(M["wts_ready"], t) if t else None)
                logits()
                weights()

            def chunk(c, back, ahead):
                base = c * ST
                pe.wait_ge(M["turned"], 2 * (c + 1))

                def into(o, wh, wl, m0, rows):
                    n = 0
                    for k in range(KT):
                        for ww, xx in ((wh, XCH), (wl, XCH), (wh, XCL)):
                            mm = pe.matmul(o, ww(k), xx[:, k, :], start=(n == 0), stop=(n == 3 * KT - 1))
                            n += 1
                    return mm

                def gate_up(s):
                    if back or s >= 2:
                        pe.wait_ge(M["sl_ready"], base + max(s - 1, 0))
                    rows = P if s < NPAIR else I
                    for part, (b, done) in enumerate(((bank[s % 2], "g_ready"), (bank[2 + s % 2], "u_ready"))):
                        if part and (back or s >= 2):
                            pe.wait_ge(M["ut_done"], base + max(s - 1, 0))
                        if s < NPAIR:
                            cc = lambda k: slice((2 * k + part) * P, (2 * k + part + 1) * P)
                            mm = into(b[:, :], lambda k: WH[:, s, cc(k)], lambda k: WL[:, s, cc(k)], 0, rows)
                        else:
                            cc = slice(E * (part + 1), E * (part + 2))
                            mm = into(b[0:I, :], lambda k: small_h[:, k, cc], lambda k: small_l[:, k, cc], 0, rows)
                        mm.then_inc(M[done], 1)
                        if part == 0 and s == NPAIR:
                            if back:
                                pe.wait_ge(M["sg_ready"], c)
                            z = slice(3 * E, 4 * E)
                            into(bank[4][0:I, :], lambda k: small_h[:, k, z], lambda k: small_l[:, k, z], 0, I).then_inc(M["z_ready"], 1)

                def down(s):
                    pe.wait_ge(M["il_ready"], base + s + 1)
                    if s == 0 and back:
                        pe.wait_ge(M["dt_ready"], KT * c)
                    rows = P if s < NPAIR else I
                    for k in range(KT):
                        hc = slice(k * P, (k + 1) * P)
                        wh = WH[:, s, 2 * KT * P:PW] if s < NPAIR else shd_h[:, :]
                        wl = WL[:, s, 2 * KT * P:PW] if s < NPAIR else shd_l[:, :]
                        for n, (ww, ii) in enumerate(((wh, IH), (wl, IH), (wh, IL))):
                            mm = pe.matmul(bank[5 + k][:, :], ww[:, hc], ii[s % 3][0:rows, :],
                                           start=(s == 0 and n == 0), stop=(s == ST - 1 and n == 2))
                    mm.then_inc(M["dn_done"], 1)
                def turn_back(t, i):
                    if i == 0:
                        pe.wait_ge(M["dt_ready"], KT * c)
                    for k in range(KT):
                        mm = pe.transpose(bank[7][:, k * P:(k + 1) * P], DT[:, k, i * P:(i + 1) * P], ident)
                    mm.then_inc(M["ft_ready"], 1)

                for s in range(ST):
                    gate_up(s)
                    if s >= 2:
                        down(s - 2)
                    if s == NPAIR:
                        break
                    i = s // 8
                    if back and s % 8 == 0:
                        t = (c - 1) * TPC + i
                        if ahead or i == 0:
                            pe.wait_ge(M["wts_ready"], (c + 1) * TPC + i)
                        else:
                            pe.wait_ge(M["ft_done"], t)
                        turn_back(t, i)
                    if ahead:
                        turn, logits, weights = prep((c + 1) * TPC + i, i)
                        if s % 8 == 2:
                            if back:
                                turn(lambda: pe.wait_ge(M["ft_done"], (c - 1) * TPC + i + 1))
                            else:
                                turn(lambda: pe.wait_ge(M["wts_ready"], TPC + i))
                        if s % 8 == 4:
                            logits()
                        if s % 8 == 6:
                            weights()
                down(ST - 2)
                down(ST - 1)

            chunks(pe, chunk)
            for i in range(TPC):
                t = (NCH - 1) * TPC + i
                pe.wait_ge(M["ft_done"], t)
                pe.wait_ge(M["dt_ready"], KT * NCH)
                for k in range(KT):
                    mm = pe.transpose(bank[7][:, k * P:(k + 1) * P], DT[:, k, i * P:(i + 1) * P], ident)
                mm.then_inc(M["ft_ready"], 1)
            attention(1, A[1])

            pe.wait_ge(F["w8_ready"], 4)

            def hidden(c, f, free):
                if past(c, 1) or f >= 4:
                    pe.wait_ge(free, c * NF + f - 3)
                for k in range(KT):
                    mm = pe.matmul(bank[f % 4][:, :], WF8[:, k, f * P:(f + 1) * P], X8[:, k, bass.ds(c * CH, CH)],
                                   start=(k == 0), stop=(k == KT - 1))
                mm.then_inc(F["h_ready"], 1)

            def first_pass(c, j):
                pe.wait_ge(F["x8_ready"], c + 1)
                for f in range(NF):
                    hidden(c, f, F["hm_done"])

            def project(c, j):
                pe.wait_ge(F["h8_ready"], (c + 1) * NF)
                for i in range(TPC):
                    if past(c, 1):
                        pe.wait_ge(F["y_done"], c * TPC + i - 3)
                    for f in range(NF):
                        mm = pe.matmul(bank[4 + i][:, 0:H], H8[j][:, f, i * P:(i + 1) * P], WP8[:, f, :], start=(f == 0), stop=(f == NF - 1))
                    mm.then_inc(F["y_ready"], 1)

            def second_pass(c, j):
                for f in range(NF):
                    hidden(c, f, F["r_ready"])
                if past(c, 1):
                    project(c - 1, 1 - j)

            tiles(pe, NCH, first_pass)
            pe.wait_ge(F["hm_done"], NCH * NF)
            tiles(pe, NCH, second_pass)
            project(NCH - 1, (NCH - 1) % 2)


def kernel(**inputs):
    import concourse.bacc as bacc
    from concourse.bass_utils import run_bass_kernel_spmd as run

    a = {k: np.asarray(v) for k, v in inputs.items()}
    ctx = a["ctx_512"]

    def by_k(w):
        return w.T.reshape(KT, P, -1).transpose(1, 0, 2)

    gu = a["L0_ffn_gu_w"].reshape(NPAIR, 2, 2, I, KT, P).transpose(5, 0, 4, 2, 1, 3).reshape(P, NPAIR, KT * 2 * P)
    dp = a["L0_ffn_dp_w"].reshape(NPAIR, 2, H, I).transpose(1, 3, 0, 2).reshape(P, NPAIR, H)
    small = np.concatenate([by_k(a["L0_ffn_gate_w"]), by_k(a["L0_ffn_sh_gate_w"]), by_k(a["L0_ffn_sh_up_w"]),
                            by_k(np.broadcast_to(a["L0_ffn_sh_gate1_w"], (E, H)))], axis=2)
    arrays = {
        "x": a["x"].reshape(B * S, H),
        "ctx": ctx,
        "ctxT": ctx.transpose(2, 0, 1).reshape(C, B * S),
        "g_xattn": a["g_xattn"],
        "g_ffn": a["g_ffn"],
        "consts": const_table(),
        "wpairs": np.concatenate([gu, dp], axis=2),
        "wsmall": small.reshape(P, KT * SMW),
        "wshdown": a["L0_ffn_sh_down_w"].T,
        "wc": by_k(a["L1_xattn_Wc"]),
        "bc": a["L1_xattn_bc"],
        "wfc": by_k(a["L1_ffn_w_fc"]).reshape(P, KT * FF),
        "wproj": a["L1_ffn_w_proj"].T.reshape(NF, P, H).transpose(1, 0, 2).reshape(P, NF * H),
    }
    nc = bacc.Bacc("TRN2", target_bir_lowering=False, num_devices=1)
    data, args = {}, {}
    for name, v in arrays.items():
        v = np.ascontiguousarray(v)
        data[f"in_{name}"] = v
        args[name] = nc.dram_tensor(f"in_{name}", v.shape, mybir.dt.from_np(v.dtype), kind="ExternalInput").ap()
    out = nc.dram_tensor("out", (B * S, H), F32, kind="ExternalOutput").ap()
    flamingo_block(nc, args["x"], args["ctx"], args["ctxT"], (args["g_xattn"], args["g_ffn"]), args["consts"],
                   args["wpairs"], args["wsmall"], args["wshdown"], args["wc"], args["bc"], args["wfc"], args["wproj"], out)
    r = run(nc, [data], core_ids=[0])
    return r.results[0]["out"].reshape(B, S, H)
```

```python
from collections import namedtuple

import numpy as np
import concourse.bass as bass
from concourse import mybir

ALU = mybir.AluOpType
ACT = mybir.ActivationFunctionType
AX = mybir.AxisListType
F32 = mybir.dt.float32
F16 = mybir.dt.float16
BF16 = mybir.dt.bfloat16
RMAX = bass.bass_isa.ReduceOp.max

P = 128
B, S, H = 64, 64, 256
C = 64
NT = B * S // P
G = 4
E, I = 64, 64
NPAIR = E // 2
CH = 512
NCH = B * S // CH
TPC = CH // P
KT = H // P
FF = 1024
NF = FF // P
LATE = 20
NWB = 4
WPART = {LATE + 4 + 2 * n: n for n in range(4)}
PW = KT * 2 * P + H
SMW = 4 * 64
EPS = 1e-5
FP8_MAX = 448.0
GRID = float(2 ** 20)
FLOOR = 1.5 * 2.0 ** 14
LAST = (NT, NT + 2)
LAYERS = ((8, 8), (4, 16))


def const_columns():
    at, out = 0, {}
    for name, width in (("ident", P), ("mask0", 8), ("mask1", 4), ("neg0", 8), ("neg1", 4),
                        ("vmask0", 4 * C), ("vmask1", 2 * C), ("ones0", 4 * 8), ("ones1", 2 * 4)):
        out[name] = (at, width)
        at += width
    return out, at


def const_table():
    cols, width = const_columns()
    t = np.zeros((P, width), np.float32)
    r = np.arange(P)[:, None]

    def put(name, block):
        a, w = cols[name]
        t[:, a:a + w] = block.reshape(P, w)

    put("ident", np.eye(P))
    for layer, (nk, d) in enumerate(LAYERS):
        k = np.arange(nk)[None, :]
        put(f"mask{layer}", (r % C) // d == k)
        put(f"neg{layer}", np.where(r < C, r // d == k, -1.0 * (r - C == k)))
        pair = np.arange(nk // 2)[None, :, None]
        head = 2 * pair + (r[:, :, None] >= S)
        put(f"vmask{layer}", np.arange(C)[None, None, :] // d == head)
        put(f"ones{layer}", np.arange(nk)[None, None, :] == head)
    return t


Router = namedtuple("Router", "xn lg mr exl mk wu wd v8 nv su ri")


def known(t):
    return isinstance(t, int)


def stand_alone(eng, side):
    eng.sem_inc(side, 1)


def inside(t):
    return not known(t) or 0 <= t < NT


def past(t, n):
    return not known(t) or t >= n


def sweep(eng, step, last):
    for t in range(-3, 4):
        step(t, t % 2)
    with eng.Fori(4, NT - 5, 2) as t:
        step(t, 0)
        step(t + 1, 1)
    for t in range(NT - 4, last + 1):
        step(t, t % 2)


def chunks(eng, body):
    body(0, False, True)
    with eng.Fori(1, NCH - 1) as c:
        body(c, True, True)
    body(NCH - 1, True, False)


def tiles(eng, n, body, tail=0):
    body(0, 0)
    body(1, 1)
    with eng.Fori(2, n - tail - 1, 2) as t:
        body(t, 0)
        body(t + 1, 1)
    for t in range(n - tail, n):
        body(t, t % 2)


def flamingo_block(nc, x_in, ctx, ctxT, gates, consts, wpairs, wsmall, wshdown, wc_in, bc_in, wfc_in, wproj_in, out):
    sb = lambda name, shape, dt=F32: nc.alloc_sbuf_tensor(name, shape, dt)
    sem = nc.alloc_semaphore

    cols, CW = const_columns()
    x = sb("x", [P, NT, H])
    cst = sb("cst", [P, CW])
    region = sb("region", [P, NPAIR * PW * 2], F16)
    WH = region[:, 0:NPAIR * PW].rearrange("p (n w) -> p n w", w=PW)
    WL = region[:, NPAIR * PW:2 * NPAIR * PW].rearrange("p (n w) -> p n w", w=PW)
    V = sb("V", [P, B, C])
    KH = sb("KH", [P, B, S], F16)
    KL = sb("KL", [P, B, S], F16)
    gate = sb("gate", [P, 4])
    tg = sb("tg", [P, 4])
    neghalf = sb("neghalf", [P, 1])
    epsilon = sb("epsilon", [P, 1])
    small_h = sb("small_h", [P, KT, SMW], F16)
    small_l = sb("small_l", [P, KT, SMW], F16)
    shd_h = sb("shd_h", [I, H], F16)
    shd_l = sb("shd_l", [I, H], F16)

    AM, HM, FS = sb("AM", [P, NT]), sb("HM", [P, NCH * NF]), sb("FS", [P, 24])
    st = sb("st", [P, 4, 6])
    mv = sb("mv", [P, 4, 2])
    ve = sb("ve", [P, 4, 1])
    rs = sb("rs", [P, 4, 1])

    arena_bytes = 41 * 1024 + 512
    arena = sb("arena", [P, arena_bytes // 4])
    used = [0]

    def carve(shape, dt=F32):
        n = int(np.prod(shape))
        size = 4 if dt == F32 else 2
        a = used[0]
        used[0] += -(-n * size // 64) * 16
        assert used[0] <= arena_bytes // 4, used[0] * 4
        v = arena[:, a:a + -(-n * size // 4)]
        if dt != F32:
            v = v.bitcast(dt)
        if len(shape) == 2:
            v = v.rearrange("p (a b) -> p a b", b=shape[1])
        if len(shape) == 3:
            v = v.rearrange("p (a b c) -> p a b c", b=shape[1], c=shape[2])
        if len(shape) == 4:
            v = v.rearrange("p (a b c d) -> p a b c d", b=shape[1], c=shape[2], d=shape[3])
        return v

    W0 = C + 8
    XG = [carve([G, C + W0]) for _ in range(2)]
    Q1 = [carve([G, P], F16) for _ in range(2)]
    Q2 = [carve([G, P], F16) for _ in range(2)]
    KD1 = [carve([2, 8 * S], F16) for _ in range(2)]
    KD2 = [carve([2, 8 * S], F16) for _ in range(2)]
    VD = [carve([2, 4 * W0]) for _ in range(2)]
    EX = [carve([512]) for _ in range(4)]
    PVS = carve([G, P])
    RC = carve([G, 8])
    ON = [carve([H]) for _ in range(2)]
    ont_at = used[0]
    stage = [carve([PW]) for _ in range(2)]
    used[0] = ont_at
    ONT = [carve([KT, P]) for _ in range(2)]
    XD = [carve([H]) for _ in range(2)]
    used[0] = 0
    XNH, XNL = carve([KT, CH], F16), carve([KT, CH], F16)
    XCH, XCL = carve([KT, CH], F16), carve([KT, CH], F16)
    WNT = carve([CH])
    LOOP = Router(*(carve([n]) for n in (H, E, E, E, E, E, 2 * E, 8, 1, 1, 1)))
    SL = [carve([CH]) for _ in range(2)]
    IN = [carve([CH]) for _ in range(2)]
    IH = [carve([CH], F16) for _ in range(3)]
    IL = [carve([CH], F16) for _ in range(3)]
    SG = carve([CH])
    DT = carve([KT, CH])
    WB = [carve([CH]) for _ in range(NWB)]
    FIRSTS = [Router((SL + IN)[i][:, 0:H], *(WB[i][:, n * E:(n + 1) * E] for n in range(5)), WB[i][:, 5 * E:7 * E],
                     *(WB[i][:, 7 * E + a:7 * E + z] for a, z in ((0, 8), (8, 9), (9, 10), (10, 11)))) for i in range(TPC)]
    routing = nc.dram_tensor("routing", (NCH, E, CH), F32, kind="Internal").ap()
    used[0] = 0
    R, HS, CC, UU = ([carve([CH]) for _ in range(4)] for _ in range(4))
    YO = [carve([2 * H]) for _ in range(2)]
    CX = [arena[:, n * 2 * CH:(n + 1) * 2 * CH] for n in range(2)]
    UX = [arena[:, n * 2 * CH:(n + 1) * 2 * CH] for n in range(2, 4)]
    fr = region[:, :].bitcast(F32)
    XF = fr[:, 0:KT * NT * P].rearrange("p (k n) -> p k n", k=KT)
    WF = fr[:, 0:KT * FF]
    WP = fr[:, 2048:2048 + NF * H]
    wc = fr[:, 22528:23040].rearrange("p (k h) -> p k h", k=KT)
    bc, bcg = fr[:, 23040:23296], fr[:, 23296:23552]
    hb = region[:, 24576:].bitcast(BF16)
    CW8, UW8 = ([fr[:, 12288 + 1024 * n:12288 + 1024 * (n + 1)] for n in (2 * m, 2 * m + 1)] for m in range(2))
    X8 = hb[:, 0:KT * NT * P].rearrange("p (k n) -> p k n", k=KT)
    WF8 = hb[:, 8192:8192 + KT * FF].rearrange("p (k f) -> p k f", k=KT)
    WP8 = hb[:, 10240:10240 + NF * H].rearrange("p (f h) -> p f h", f=NF)
    H8 = [hb[:, 12288 + 4096 * n:12288 + 4096 * (n + 1)].rearrange("p (f t) -> p f t", f=NF) for n in range(2)]

    bank = [nc.alloc_psum_tensor(f"bank{n}", [P, 512], F32) for n in range(8)]

    def cv(name):
        a, w = cols[name]
        return cst[:, a:a + w]

    ident = cv("ident")

    d_small, d_late, d_w = (sem(n) for n in ("d_small", "d_late", "d_w"))
    d_stage = [sem(f"d_stage{n}") for n in range(2)]
    d_wb = [sem(f"d_wb{i}") for i in range(NWB)]
    routed = sem("routed")
    d_x, d_kt, d_ctx = ([sem(f"{n}{part}") for part in range(parts)] for n, parts in (("d_x", 3), ("d_kt", 2), ("d_ctx", 2)))
    FIRST = ((0, 8), (8, B))
    PIECES = (FIRST[0],) + tuple((8 + 14 * n, 22 + 14 * n) for n in range(4))
    d_wsm, d_wf, d_wp = (sem(n) for n in ("d_wsm", "d_wf", "d_wp"))
    stored = [sem(f"stored{i}") for i in range(2)]
    kt_hi, kv_ready, kv_ones, tanh_done = sem("kt_hi"), sem("kv_ready"), sem("kv_ones"), sem("tanh_done")
    whi_done, wlo_done = sem("whi_done"), sem("wlo_done")
    sm_hi, sm_ready, bcg_done, half_set = sem("sm_hi"), sem("sm_ready"), sem("bcg_done"), sem("half_set")
    side_v, side_s = sem("side_vector"), sem("side_sync")
    lnames = ("stats", "mv", "ve", "rs", "twice", "out")
    LNA = {n: sem("ln_" + n) for n in lnames}
    LND = {n: sem("lnd_" + n) for n in lnames}
    names = ("t1_ready", "q_hi", "q_ready", "kd_ready", "kl_ready", "bias_in", "vd_set", "vd_ready", "mx_ready", "mx_done", "t2_ready", "q2_ready",
             "sc_ready", "ex_ready", "pv_ready", "pvs_ready", "ot_ready", "rc_done", "on_ready",
             "ont_ready", "onts_ready", "y_ready", "x_done")
    A = [{n: sem(f"{n}{layer}") for n in names} for layer in range(2)]

    KF = region[:, NPAIR * PW * 2 - 2 * B * S:].bitcast(F32)
    smf = region[:, NPAIR * PW * 2 - 2 * B * S - 2 * (KT * SMW + H):NPAIR * PW * 2 - 2 * B * S].bitcast(F32)

    STAT_BASE = [0, NT, 2 * NT, 0]
    LNS = [LNA, LNA, LNA, LND]

    xv = x_in.rearrange("(n p) h -> p n h", p=P)
    ov = out.rearrange("(n p) h -> p n h", p=P)

    def tile_x(t):
        return x[:, bass.ds(t, 1), :].rearrange("p a h -> p (a h)") if not known(t) else x[:, t, :]

    def attention_shape(layer):
        nk, d = LAYERS[layer]
        return nk, d, nk // 2, C + nk, G * nk * S // 512, nk // 4

    mnames = ("tp_ready", "xt_hi", "xt_ready", "lg_ready", "lg_done", "v8_done", "mr_done", "nv_done", "ex_done", "mk_done",
              "wu_done", "su_done", "ri_done", "wd_done", "wt_ready", "wts_ready", "turned",
              "g_ready", "u_ready", "sl_ready", "ut_done", "in_ready", "ih_ready", "il_ready", "dn_done",
              "z_ready", "sg_ready", "dt_ready", "ft_ready", "ft_done")
    M = {n: sem("m_" + n) for n in mnames}
    ST = NPAIR + 1
    fnames = ("tp_ready", "xf_ready", "am_done", "amx", "ams", "abs_ready", "c_done", "sx_ready", "u_done", "x8_ready",
              "wam", "wamx", "was", "wabs", "wc_done", "wu_done", "w8_ready", "hm_done", "hmx",
              "hr", "fs", "h_ready", "r_ready", "hs_ready", "hc_done", "hu_done", "h8_ready", "y_ready", "y_done")
    F = {n: sem("f_" + n) for n in fnames}

    with nc.Block() as block:

        @block.sync
        def _(sp):
            sp.dma_start(cst[:, :], consts).then_inc(d_small, 16)
            sp.dma_start(x[:, 0:4, :], xv[:, 0:4, :]).then_inc(d_x[0], 16)
            for n, g in enumerate(gates):
                sp.dma_start(gate[:, 2 * n:2 * n + 2], g.rearrange("(a d) -> a d", a=1).to_broadcast([P, 2])).then_inc(d_small, 16)

            def keys(part):
                b0, b1 = FIRST[part]
                for half in range(2):
                    sp.dma_start(KF[half * C:(half + 1) * C, b0 * S:b1 * S], ctxT[:, b0 * S:b1 * S]).then_inc(d_kt[part], 16)

            def values(part):
                b0, b1 = FIRST[part]
                for half in range(2):
                    sp.dma_start(V[half * S:(half + 1) * S, b0:b1, :], ctx[b0:b1].rearrange("b t c -> t b c")).then_inc(d_ctx[part], 16)

            keys(0)
            values(0)
            for n in range(2):
                sp.dma_start(stage[n], wpairs[:, n, :]).then_inc(d_stage[n], 16)
            keys(1)
            sp.dma_start(x[:, 4:12, :], xv[:, 4:12, :]).then_inc(d_x[1], 16)
            values(1)
            sp.dma_start(x[:, 12:NT, :], xv[:, 12:NT, :]).then_inc(d_x[2], 16)
            sp.dma_start(smf[:, 0:KT * SMW], wsmall).then_inc(d_wsm, 16)
            sp.dma_start(smf[0:I, KT * SMW:KT * SMW + H], wshdown).then_inc(d_wsm, 16)
            with sp.Fori(2, NPAIR - 1, 2) as n:
                for j in range(2):
                    sp.wait_ge(wlo_done, n + j - 1)
                    stand_alone(sp, side_s)
                    sp.dma_start(stage[j], wpairs[:, bass.ds(n + j, 1), :].rearrange("p a w -> p (a w)")).then_inc(d_w, 16)
                    sp.wait_ge(d_w, 16 * (n + j - 1))
                    stand_alone(sp, side_s)
            sp.wait_ge(A[0]["x_done"], NT)
            sp.wait_ge(wlo_done, NPAIR)

            def route(c):
                sp.wait_ge(M["wts_ready"], (c + 1) * TPC)
                stand_alone(sp, side_s)
                sp.dma_start(routing[bass.ds(c, 1)].rearrange("a e t -> (a e) t"), WNT[0:E, :]).then_inc(routed, 16)
                sp.wait_ge(routed, 16 * (c + 1))
                stand_alone(sp, side_s)

            def spread(c, back, ahead):
                for s in range(NPAIR):
                    if not ahead and s == LATE - 2:
                        sp.wait_ge(M["dn_done"], c * ST + -(-4096 * 2 // PW))
                        sp.dma_start(WF, wfc_in).then_inc(d_wf, 16)
                        sp.dma_start(WP, wproj_in).then_inc(d_wp, 16)
                    if back or s >= NWB:
                        sp.wait_ge(M["in_ready"], c * ST + s + 1 - NWB - (s < NWB))
                        stand_alone(sp, side_s)
                    for half in range(2):
                        sp.dma_start(WB[s % NWB][half * I:(half + 1) * I, :],
                                     routing[bass.ds(c, 1), 2 * s + half, :].to_broadcast([I, CH])).then_inc(d_wb[s % NWB], 16)
                if ahead:
                    route(c + 1)

            route(0)
            chunks(sp, spread)
            sp.wait_ge(M["dn_done"], NCH * ST)
            sp.dma_start(wc, wc_in).then_inc(d_late, 16)
            sp.dma_start(bc, bc_in.rearrange("(a d) -> a d", a=1).to_broadcast([P, H])).then_inc(d_late, 16)
            with sp.Fori(0, NCH) as c:
                for i in range(2):
                    sp.wait_ge(F["y_done"], 2 * c + i + 1)
                    stand_alone(sp, side_s)
                    sp.dma_start(ov[:, bass.ds(c * TPC + 2 * i, 2), :], YO[i].rearrange("p (a h) -> p a h", h=H)).then_inc(stored[i], 16)
            for i in range(2):
                sp.wait_ge(stored[i], 16 * NCH)

        @block.gpsimd
        def _(pool):
            pool.memset(neghalf[:, :], -0.5).then_inc(half_set, 1)
            pool.memset(epsilon[:, :], EPS).then_inc(half_set, 1)
            pool.wait_ge(half_set, 2)
            pool.memset(KL[C:P, :, :].rearrange("p b t -> p (b t)"), 1.0).then_inc(kv_ones, 1)
            pool.wait_ge(kv_ones, 1)

            def rstd(t, j, layer):
                n, l = STAT_BASE[layer] + t + 1, LNS[layer]
                pool.wait_ge(l["mv"], n)
                pool.tensor_tensor(ve[:, j, :], mv[:, j, 1:2], epsilon[:, :], ALU.add).then_inc(l["ve"], 1)
                pool.wait_ge(l["ve"], n)
                pool.tensor_tensor(rs[:, j, :], ve[:, j, :], neghalf[:, :], ALU.pow).then_inc(l["rs"], 1)

            def attention(layer, a):
                nk, d, npair, w, _, _ = attention_shape(layer)
                mask, neg = cv(f"mask{layer}"), cv(f"neg{layer}")
                vmask, ones = cv(f"vmask{layer}"), cv(f"ones{layer}")
                if layer == 0:
                    pool.wait_ge(d_small, 16 * 3)
                else:
                    pool.wait_ge(M["ft_done"], NT)
                for j in range(2):
                    for b in range(2):
                        pool.tensor_copy(VD[j][:, b, 0:npair * w].rearrange("p (n w) -> p n w", w=w)[:, :, C:w],
                                         ones.rearrange("p (n k) -> p n k", k=nk)).then_inc(a["vd_set"], 1)

                def diagonal(t, dst, keys, m, done):
                    for b in range(2):
                        pool.tensor_tensor(dst[:, b, 0:nk * S].rearrange("p (k t) -> p k t", k=nk),
                                           keys[:, bass.ds(t * 2 + b, 1), :].to_broadcast([P, nk, S]),
                                           m.unsqueeze(2).to_broadcast([P, nk, S]), ALU.mult).then_inc(done, 1)

                def step(t, j):
                    if inside(t + 2):
                        if past(t, 0):
                            pool.wait_ge(a["sc_ready"], (t + 1) * 2 * (nk // 4))
                        if layer == 0 and known(t) and t in (-2, 2, 3):
                            pool.wait_ge(kv_ready, {-2: 1, 2: 2, 3: len(PIECES)}[t])
                            pool.wait_ge(d_ctx[t > 0], 32)
                        diagonal(t + 2, KD1[j], KH, mask, a["kd_ready"])
                    if layer == 1 and inside(t - 2):
                        rstd(t - 2, 2 + j, 3)
                    if inside(t + 3):
                        rstd(t + 3, 1 - j, 0 if layer == 0 else 2)
                    if inside(t + 2):
                        diagonal(t + 2, KD2[j], KL, neg, a["kl_ready"])
                    if layer == 1 and inside(t):
                        pool.wait_ge(LNA["out"], STAT_BASE[2] + t + 1)
                        pool.tensor_tensor(tile_x(t), tile_x(t), bcg, ALU.add).then_inc(a["bias_in"], 1)
                    if inside(t + 2):
                        if past(t, 0):
                            pool.wait_ge(a["pv_ready"], t + 1)
                        for b in range(2):
                            pool.tensor_tensor(VD[j][:, b, 0:npair * w].rearrange("p (n w) -> p n w", w=w)[:, :, 0:C],
                                               V[:, bass.ds((t + 2) * 2 + b, 1), :].to_broadcast([P, npair, C]),
                                               vmask.rearrange("p (n c) -> p n c", c=C), ALU.mult).then_inc(a["vd_ready"], 1)

                sweep(pool, step, LAST[layer])

            attention(0, A[0])

            def low(n, s):
                pool.wait_ge(M["ih_ready"], n)
                pool.tensor_tensor(IL[s % 3], IN[s % 2], IH[s % 3], ALU.subtract).then_inc(M["il_ready"], 1)

            for t in range(TPC):
                rstd(t, t, 1)

            def chunk(c, back, ahead):
                for s in range(ST):
                    low(c * ST + s + 1, s)
                    if not ahead and s == LATE + 2:
                        pool.wait_ge(F["wam"], 2)
                        pool.partition_all_reduce(FS[:, 4:6], FS[:, 1:3], P, RMAX).then_inc(F["wamx"], 1)
                    if ahead and s % 8 == 0 and s < NPAIR:
                        i = s // 8
                        rstd((c + 1) * TPC + i, i % 2, 1)

            chunks(pool, chunk)
            attention(1, A[1])

            pool.wait_ge(F["am_done"], NT + 1)
            pool.partition_all_reduce(FS[:, 3:4], FS[:, 0:1], P, RMAX).then_inc(F["amx"], 1)

            def rounded_x(c, j):
                if past(c, 1):
                    pool.wait_ge(F["sx_ready"], c)
                    pool.wait_ge(F["c_done"], c + 1)
                    pool.tensor_tensor(UX[j], UX[j], CX[j], ALU.add).then_inc(F["u_done"], 1)
                pool.wait_ge(F["u_done"], c + 1)
                pool.tensor_tensor(X8[:, :, bass.ds(c * CH, CH)], UX[j].rearrange("p (k t) -> p k t", k=KT),
                                   CX[j].rearrange("p (k t) -> p k t", k=KT), ALU.subtract).then_inc(F["x8_ready"], 1)

            tiles(pool, NCH, rounded_x)
            pool.wait_ge(F["hr"], 1)
            pool.partition_all_reduce(FS[:, 7:8], FS[:, 6:7], P, RMAX).then_inc(F["hmx"], 1)

            def rounded(c, j):
                if past(c, 2):
                    pool.wait_ge(F["y_ready"], (c - 1) * 2)
                for f in range(NF):
                    pool.wait_ge(F["hu_done"], c * NF + f + 1)
                    pool.tensor_tensor(H8[j][:, f, :], UU[f % 4], CC[f % 4], ALU.subtract).then_inc(F["h8_ready"], 1)

            tiles(pool, NCH, rounded)

        @block.scalar
        def _(act):
            act.wait_ge(d_small, 16 * 3)
            act.activation(tg[:, :], gate[:, :], ACT.Tanh).then_inc(tanh_done, 1)

            def high_keys(n):
                b0, b1 = PIECES[n]
                act.wait_ge(d_kt[min(n, 1)], 32)
                act.copy(KH[:, b0:b1, :].rearrange("p b t -> p (b t)"), KF[:, b0 * S:b1 * S]).then_inc(kt_hi, 1)

            high_keys(0)

            def attention(layer, a):
                nk, d, npair, w, nmx, nsc = attention_shape(layer)

                def exps(t, j, u):
                    n = t * 2 * nsc + u
                    back = 4 // (2 * nsc)
                    if past(t, back):
                        act.wait_ge(a["pv_ready"], t - back + 1)
                    act.wait_ge(a["sc_ready"], n + 1)
                    act.activation(EX[(u + (0 if nsc == 2 else 2 * j)) % 4], bank[4 + u % 2][:, :], ACT.Exp,
                                   scale=d ** -0.5).then_inc(a["ex_ready"], 1)

                def step(t, j):
                    if inside(t):
                        for u in range(nsc):
                            exps(t, j, u)
                    if layer == 0 and inside(t):
                        if known(t) and t < 2:
                            act.wait_ge(d_stage[t], 16)
                        else:
                            act.wait_ge(d_w, 16 * (t - 1))
                        act.copy(WH[:, bass.ds(t, 1), :].rearrange("p a w -> p (a w)"), stage[j]).then_inc(whi_done, 1)
                    if inside(t):
                        for u in range(nsc, 2 * nsc):
                            exps(t, j, u)
                    if inside(t + 2):
                        if past(t, 0):
                            act.wait_ge(a["sc_ready"], (t + 1) * 2 * nsc)
                        act.wait_ge(a["t1_ready"], t + 3)
                        act.copy(Q1[j], bank[0][:, :].rearrange("p (g s) -> p g s", g=G)).then_inc(a["q_hi"], 1)
                    if inside(t + 1):
                        act.wait_ge(a["t2_ready"], t + 2)
                        act.copy(Q2[1 - j][0:w], bank[1][0:w, :].rearrange("p (g s) -> p g s", g=G)).then_inc(a["q2_ready"], 1)
                    if layer == 1 and inside(t - 1):
                        act.wait_ge(a["ont_ready"], t)
                        act.copy(ONT[1 - j], bank[7][:, 0:H].rearrange("p (k t) -> p k t", k=KT)).then_inc(a["onts_ready"], 1)
                    if inside(t):
                        act.wait_ge(a["pv_ready"], t + 1)
                        if past(t, 1):
                            act.wait_ge(a["ot_ready"], t)
                        act.copy(PVS[0:w].rearrange("p g (b s) -> p g b s", b=2),
                                 bank[6][0:w, :].rearrange("p (b g s) -> p g b s", b=2, g=G)).then_inc(a["pvs_ready"], 1)
                    if layer == 0 and known(t) and -1 <= t < 3:
                        high_keys(t + 2)
                    if layer == 1 and inside(t - 3):
                        act.wait_ge(F["tp_ready"], t - 2)
                        act.copy(XF[:, :, bass.ds((t - 3) * P, P)], bank[0][:, 0:H].rearrange("p (k t) -> p k t", k=KT)).then_inc(F["xf_ready"], 1)

                sweep(act, step, LAST[layer])

            attention(0, A[0])

            def prep(t, i, r, bk):
                cols_i = slice(i * P, (i + 1) * P)

                def turn():
                    act.wait_ge(M["tp_ready"], t + 1)
                    act.copy(XNH[:, :, cols_i], bk[:, 0:H].rearrange("p (k t) -> p k t", k=KT)).then_inc(M["xt_hi"], 1)

                def exp():
                    act.wait_ge(M["nv_done"], t + 1)
                    act.activation(r.exl, r.lg, ACT.Exp, bias=r.nv).then_inc(M["ex_done"], 1)

                def weights(before):
                    act.wait_ge(M["wt_ready"], t + 1)
                    if i == 0 and not (known(before) and before == 0):
                        act.wait_ge(routed, 16 * before)
                    act.copy(WNT[0:E, cols_i], bk[0:E, 0:P]).then_inc(M["wts_ready"], 1)

                return turn, exp, weights

            act.wait_ge(A[0]["x_done"], NT)
            for t in range(TPC):
                prep(t, t, FIRSTS[t], bank[4 + t])[0]()
            for t in range(TPC):
                prep(t, t, FIRSTS[t], bank[4 + t])[1]()
            for t in range(TPC):
                prep(t, t, FIRSTS[t], bank[4 + t])[2](0)

            def chunk(c, back, ahead):
                base = c * ST

                def silu(s):
                    rows = P if s < NPAIR else I
                    act.wait_ge(M["g_ready"], base + s + 1)
                    if back or s >= 2:
                        act.wait_ge(M["in_ready"], base + max(s - 1, 0))
                    act.activation(SL[s % 2][0:rows, :], bank[s % 2][0:rows, :], ACT.Silu).then_inc(M["sl_ready"], 1)

                def high(s):
                    rows = P if s < NPAIR else I
                    act.wait_ge(M["in_ready"], base + s + 1)
                    if back or s >= 3:
                        act.wait_ge(M["dn_done"], base + s - 2)
                    act.copy(IH[s % 3][0:rows, :], IN[s % 2][0:rows, :]).then_inc(M["ih_ready"], 1)

                def evacuate(c):
                    act.wait_ge(M["dn_done"], (c + 1) * ST)
                    for k in range(KT):
                        act.mul(DT[:, k, :], bank[5 + k][:, :], tg[:, 2:3]).then_inc(M["dt_ready"], 1)

                for s in range(ST):
                    if s == NPAIR:
                        act.wait_ge(M["z_ready"], c + 1)
                        act.activation(SG[0:I, :], bank[4][0:I, :], ACT.Sigmoid).then_inc(M["sg_ready"], 1)
                    silu(s)
                    if s >= 1:
                        high(s - 1)
                    if s == 1 and back:
                        evacuate(c - 1)
                    i, at = s // 8, s % 8
                    if ahead:
                        if s and at == 0:
                            prep((c + 1) * TPC + i - 1, i - 1, LOOP, bank[7])[2](c + 1)
                        if at == 4:
                            prep((c + 1) * TPC + i, i, LOOP, bank[7])[0]()
                        if at == 6:
                            prep((c + 1) * TPC + i, i, LOOP, bank[7])[1]()
                    elif s in WPART:
                        n = WPART[s]
                        act.wait_ge(F["was"], 3)
                        if n >= 2:
                            act.wait_ge(F["w8_ready"], n - 1)
                        src = (WF, WP)[n // 2][:, (n % 2) * 2 * CH:(n % 2 + 1) * 2 * CH]
                        act.activation(CW8[n % 2], src, ACT.Abs, scale=FS[:, 18 + n // 2:19 + n // 2]).then_inc(F["wabs"], 1)
                high(ST - 1)
                if not ahead:
                    evacuate(c)

            chunks(act, chunk)
            attention(1, A[1])

            act.wait_ge(F["ams"], 4)
            act.wait_ge(F["xf_ready"], NT)

            def magnitudes(c, j):
                if past(c, 2):
                    act.wait_ge(F["x8_ready"], c - 1)
                act.activation(CX[j].rearrange("p (k t) -> p k t", k=KT), XF[:, :, bass.ds(c * CH, CH)], ACT.Abs,
                               scale=FS[:, 17:18]).then_inc(F["abs_ready"], 1)
                if past(c, 1):
                    act.activation(UX[j].rearrange("p (k t) -> p k t", k=KT), XF[:, :, bass.ds(c * CH, CH)], ACT.Copy,
                                   scale=FS[:, 11:12]).then_inc(F["sx_ready"], 1)

            tiles(act, NCH, magnitudes)
            act.wait_ge(F["fs"], 1)

            def squares(c, j):
                def square(f):
                    n = c * NF + f
                    act.wait_ge(F["r_ready"], n + 1)
                    if past(c, 1) or f >= 4:
                        act.wait_ge(F["hu_done"], n - 3)
                    act.activation(HS[f % 4], R[f % 4], ACT.Square).then_inc(F["hs_ready"], 1)

                for f in range(NF):
                    if past(c, 1) or f >= 4:
                        act.wait_ge(F["hs_ready"], c * NF + f - 3)
                    act.wait_ge(F["h_ready"], NCH * NF + c * NF + f + 1)
                    act.activation(R[f % 4], bank[f % 4][:, :], ACT.Relu, scale=FS[:, 16:17]).then_inc(F["r_ready"], 1)
                    if f:
                        square(f - 1)
                square(NF - 1)

            tiles(act, NCH, squares)

        @block.vector
        def _(dve):
            def low_keys(n):
                b0, b1 = PIECES[n]
                dve.wait_ge(kt_hi, n + 1)
                dve.tensor_tensor(KL[0:C, b0:b1, :].rearrange("p b t -> p (b t)"), KF[0:C, b0 * S:b1 * S],
                                  KH[0:C, b0:b1, :].rearrange("p b t -> p (b t)"), ALU.subtract).then_inc(kv_ready, 1)

            def small_halves():
                dve.wait_ge(d_wsm, 32)
                dve.tensor_copy(small_h[:, :, :].rearrange("p k w -> p (k w)"), smf[:, 0:KT * SMW]).then_inc(sm_hi, 1)
                dve.tensor_copy(shd_h[:, :], smf[0:I, KT * SMW:KT * SMW + H]).then_inc(sm_hi, 1)
                dve.wait_ge(sm_hi, 2)
                dve.tensor_tensor(small_l[:, :, :].rearrange("p k w -> p (k w)"), smf[:, 0:KT * SMW],
                                  small_h[:, :, :].rearrange("p k w -> p (k w)"), ALU.subtract).then_inc(sm_ready, 1)
                dve.tensor_tensor(shd_l[:, :], smf[0:I, KT * SMW:KT * SMW + H], shd_h[:, :], ALU.subtract).then_inc(sm_ready, 1)

            def stats(t, j, layer):
                n, l = STAT_BASE[layer] + t + 1, LNS[layer]
                dve.bn_stats(st[:, j, :], tile_x(t)).then_inc(l["stats"], 1)
                dve.wait_ge(l["stats"], n)
                stand_alone(dve, side_v)
                dve.bn_aggr(mv[:, j, :], st[:, j, :]).then_inc(l["mv"], 1)

            def norm(t, j, layer, dst, src):
                l = LNS[layer]
                dve.wait_ge(l["rs"], STAT_BASE[layer] + t + 1)
                for d in dst[:-1]:
                    dve.tensor_scalar(d, src, mv[:, j, 0:1], rs[:, j, :], ALU.subtract, ALU.mult).then_inc(l["twice"], 1)
                dve.tensor_scalar(dst[-1], src, mv[:, j, 0:1], rs[:, j, :], ALU.subtract, ALU.mult).then_inc(l["out"], 1)

            def biggest(dst, src, done):
                dve.tensor_reduce(dst, src, AX.X, ALU.max, apply_absolute_value=True).then_inc(done, 1)

            def weight_scales(s):
                if s == LATE:
                    dve.wait_ge(d_wf, 16)
                    biggest(FS[:, 1:2], WF, F["wam"])
                elif s == LATE + 1:
                    dve.wait_ge(d_wp, 16)
                    biggest(FS[:, 2:3], WP, F["wam"])
                else:
                    dve.wait_ge(F["wamx"], 1)
                    dve.tensor_scalar(FS[:, 9:11], FS[:, 4:6], 1.0 / FP8_MAX, 1e-6, ALU.mult, ALU.max).then_inc(F["was"], 1)
                    dve.wait_ge(F["was"], 1)
                    dve.reciprocal(FS[:, 12:14], FS[:, 9:11]).then_inc(F["was"], 1)
                    dve.wait_ge(F["was"], 2)
                    dve.tensor_scalar(FS[:, 18:20], FS[:, 12:14], GRID, None, ALU.mult).then_inc(F["was"], 1)

            def quantise(src, inv, cc, uu, n, kind):
                dve.wait_ge(F[{"w": "wabs", "": "abs_ready"}[kind]], n + 1)
                dve.tensor_scalar(cc, cc, FLOOR, None, ALU.max).then_inc(F[kind + "c_done"], 1)
                dve.wait_ge(F[kind + "c_done"], n + 1)
                dve.scalar_tensor_tensor(uu, src, inv, cc, ALU.mult, ALU.add).then_inc(F[kind + "u_done"], 1)

            def attention(layer, a):
                nk, d, npair, w, nmx, nsc = attention_shape(layer)
                gpu = G // nmx
                ln = 0 if layer == 0 else 2
                if layer == 0:
                    low_keys(0)
                    dve.wait_ge(tanh_done, 1)
                else:
                    dve.wait_ge(M["ft_done"], NT)
                    dve.wait_ge(d_late, 16 * 2)
                    dve.tensor_scalar(bcg, bc, tg[:, 1:2], None, ALU.mult).then_inc(bcg_done, 1)
                    dve.wait_ge(bcg_done, 1)

                def heads(ap):
                    return ap.rearrange("p (k g d) -> p g k d", g=G, d=d)

                def maxima(t, j, u):
                    n = t * nmx + u + 1
                    dve.wait_ge(a["mx_ready"], n)
                    dve.tensor_reduce(XG[j][:, u * gpu:(u + 1) * gpu, 2 * C:C + w],
                                      bank[2 + u % 2][:, :].rearrange("p (g k t) -> p g k t", g=gpu, t=S),
                                      AX.X, ALU.max).then_inc(a["mx_done"], 1)

                def step(t, j):
                    if inside(t + 1):
                        for u in range(nmx // 2):
                            maxima(t + 1, 1 - j, u)
                    if inside(t - 1):
                        o = bank[7][:, 0:G * w].rearrange("p (g w) -> p g w", g=G)
                        dve.wait_ge(a["ot_ready"], t)
                        dve.reciprocal(RC[:, :, 0:nk], o[:, :, C:w]).then_inc(a["rc_done"], 1)
                    if inside(t + 1):
                        for u in range(nmx // 2, nmx):
                            maxima(t + 1, 1 - j, u)
                    if inside(t - 1):
                        dve.wait_ge(a["rc_done"], t)
                        if layer == 1 and past(t, 3):
                            dve.wait_ge(a["ont_ready"], t - 2)
                        dve.tensor_tensor(heads(ON[1 - j]), o[:, :, 0:C].rearrange("p g (k d) -> p g k d", d=d),
                                          RC[:, :, 0:nk].unsqueeze(3).to_broadcast([P, G, nk, d]), ALU.mult).then_inc(a["on_ready"], 1)
                    if layer == 1 and inside(t - 2):
                        dve.wait_ge(a["x_done"], t - 1)
                        stand_alone(dve, side_v)
                        stats(t - 2, 2 + j, 3)
                    if inside(t + 3):
                        if layer == 0 and known(t) and t == -3:
                            dve.wait_ge(d_x[0], 16)
                        if layer == 0 and known(t) and t in (1, 3):
                            dve.wait_ge(d_x[(t + 1) // 2], 16)
                        stats(t + 3, 1 - j, ln)
                    if inside(t - 1) and layer == 0:
                        dve.wait_ge(a["on_ready"], t)
                        dve.scalar_tensor_tensor(tile_x(t - 1), ON[1 - j], tg[:, 0:1], tile_x(t - 1), ALU.mult, ALU.add).then_inc(a["x_done"], 1)
                    if layer == 0 and inside(t):
                        dve.wait_ge(whi_done, t + 1)
                        dve.tensor_tensor(WL[:, bass.ds(t, 1), :].rearrange("p a w -> p (a w)"), stage[j],
                                          WH[:, bass.ds(t, 1), :].rearrange("p a w -> p (a w)"), ALU.subtract).then_inc(wlo_done, 1)
                    if inside(t + 2):
                        dve.wait_ge(a["q_hi"], t + 3)
                        dve.tensor_tensor(Q1[j][C:P], bank[0][C:P, :].rearrange("p (g s) -> p g s", g=G),
                                          Q1[j][C:P], ALU.subtract).then_inc(a["q_ready"], 1)
                    if layer == 1 and inside(t - 2):
                        if past(t, 4):
                            dve.wait_ge(F["tp_ready"], t - 3)
                        norm(t - 2, 2 + j, 3, [XD[j]], tile_x(t - 2))
                    if inside(t + 3):
                        if past(t, -1):
                            dve.wait_ge(a["t2_ready"], t + 2)
                        norm(t + 3, 1 - j, ln, [XG[1 - j][:, :, r * C:(r + 1) * C].rearrange("p g (k d) -> p g k d", d=d) for r in range(2)],
                             heads(tile_x(t + 3)))
                    if layer == 1 and inside(t - 2):
                        dve.wait_ge(LND["out"], t - 1)
                        dve.tensor_reduce(AM[:, bass.ds(t - 2, 1)], XD[j], AX.X, ALU.max, apply_absolute_value=True).then_inc(F["am_done"], 1)
                    if inside(t - 1) and layer == 1:
                        dve.wait_ge(a["y_ready"], t)
                        dve.wait_ge(a["bias_in"], t)
                        dve.scalar_tensor_tensor(tile_x(t - 1), bank[1][:, 0:H], tg[:, 1:2], tile_x(t - 1), ALU.mult, ALU.add).then_inc(a["x_done"], 1)
                    if layer == 0 and known(t) and -1 <= t < 3:
                        low_keys(t + 2)
                    if layer == 0 and known(t) and t == 3:
                        small_halves()
                    if layer == 0 and known(t) and t == NT - 1:
                        dve.wait_ge(a["x_done"], TPC)
                        for i in range(TPC):
                            stats(i, i, 1)

                sweep(dve, step, LAST[layer])

            attention(0, A[0])

            dve.wait_ge(A[0]["x_done"], NT)
            dve.wait_ge(wlo_done, NPAIR)

            def prep(t, i, slot, r, bk):
                cols_i = slice(i * P, (i + 1) * P)

                def measure():
                    stats(t, slot, 1)

                def normalise():
                    if past(t, TPC):
                        dve.wait_ge(M["tp_ready"], t)
                    norm(t, slot, 1, [r.xn], tile_x(t))

                def turn():
                    dve.wait_ge(M["xt_hi"], t + 1)
                    dve.tensor_tensor(XNL[:, :, cols_i], bk[:, 0:H].rearrange("p (k t) -> p k t", k=KT),
                                      XNH[:, :, cols_i], ALU.subtract).then_inc(M["xt_ready"], 1)

                def take():
                    dve.wait_ge(M["lg_ready"], t + 1)
                    dve.tensor_copy(r.lg, bk[:, 0:E]).then_inc(M["lg_done"], 1)

                def top():
                    dve.wait_ge(M["lg_done"], t + 1)
                    stand_alone(dve, side_v)
                    dve.max(r.v8, r.lg).then_inc(M["v8_done"], 1)

                def without_top():
                    dve.wait_ge(M["v8_done"], t + 1)
                    dve.tensor_scalar(r.nv, r.v8[:, 0:1], -1.0, None, ALU.mult).then_inc(M["nv_done"], 1)
                    dve.match_replace(r.mr, r.v8, r.lg, -3.0e38).then_inc(M["mr_done"], 1)

                def mask():
                    dve.wait_ge(M["mr_done"], t + 1)
                    dve.tensor_tensor(r.mk, r.mr, r.lg, ALU.not_equal).then_inc(M["mk_done"], 1)

                def masked():
                    dve.wait_ge(M["mk_done"], t + 1)
                    dve.wait_ge(M["ex_done"], t + 1)
                    dve.tensor_tensor(r.wu, r.exl, r.mk, ALU.mult).then_inc(M["wu_done"], 1)

                def total():
                    dve.wait_ge(M["wu_done"], t + 1)
                    dve.tensor_reduce(r.su, r.wu, AX.X, ALU.add).then_inc(M["su_done"], 1)

                def inverse():
                    dve.wait_ge(M["su_done"], t + 1)
                    dve.reciprocal(r.ri, r.su).then_inc(M["ri_done"], 1)

                def divide():
                    dve.wait_ge(M["ri_done"], t + 1)
                    dve.tensor_scalar(r.wd.rearrange("p (a e) -> p a e", a=2), r.wu.unsqueeze(1).to_broadcast([P, 2, E]),
                                      r.ri, None, ALU.mult).then_inc(M["wd_done"], 1)

                return (measure,), (normalise,), (turn,), (take, top, without_top, mask), (masked, total, inverse, divide)

            def hand_over(c):
                if not (known(c) and c == 0):
                    dve.wait_ge(M["u_ready"], c * ST)
                dve.wait_ge(M["xt_ready"], (c + 1) * TPC)
                dve.tensor_copy(XCH.rearrange("p k t -> p (k t)"), XNH.rearrange("p k t -> p (k t)")).then_inc(M["turned"], 1)
                dve.tensor_copy(XCL.rearrange("p k t -> p (k t)"), XNL.rearrange("p k t -> p (k t)")).then_inc(M["turned"], 1)

            firsts = [prep(t, t, t, FIRSTS[t], bank[4 + t]) for t in range(TPC)]
            for part in range(1, 5):
                for n in range(len(firsts[0][part])):
                    for t in range(TPC):
                        firsts[t][part][n]()
                if part == 2:
                    hand_over(0)

            def hand_back(t, bk=bank[7]):
                dve.wait_ge(M["ft_ready"], t + 1)
                dve.tensor_tensor(tile_x(t), tile_x(t), bk[:, 0:H], ALU.add).then_inc(M["ft_done"], 1)

            def chunk(c, back, ahead):
                base = c * ST
                for s in range(ST):
                    rows = P if s < NPAIR else I
                    if s == ST - 1 and ahead:
                        hand_over(c + 1)
                    dve.wait_ge(M["sl_ready"], base + s + 1)
                    dve.wait_ge(M["u_ready"], base + s + 1)
                    dve.tensor_tensor(SL[s % 2][0:rows, :], bank[2 + s % 2][0:rows, :], SL[s % 2][0:rows, :],
                                      ALU.mult).then_inc(M["ut_done"], 1)
                    dve.wait_ge(M["ut_done"], base + s + 1)
                    if back or s >= 2:
                        dve.wait_ge(M["il_ready"], base + max(s - 1, 0))
                    if s < NPAIR:
                        dve.wait_ge(d_wb[s % NWB], 32 * (c * (NPAIR // NWB) + s // NWB + 1))
                        w = WB[s % NWB]
                    else:
                        dve.wait_ge(M["sg_ready"], c + 1)
                        w = SG[0:I, :]
                    dve.tensor_tensor(IN[s % 2][0:rows, :], SL[s % 2][0:rows, :], w, ALU.mult).then_inc(M["in_ready"], 1)
                    i, at = s // 8, s % 8
                    if back and at == 2:
                        hand_back((c - 1) * TPC + i)
                    if ahead:
                        for part, place in enumerate((0, 1, 4, 5, 6)):
                            if at == place and s < NPAIR:
                                for do in prep((c + 1) * TPC + i, i, i % 2, LOOP, bank[7])[part]:
                                    do()
                    if not ahead and s in (LATE, LATE + 1, LATE + 3):
                        weight_scales(s)
                    if not ahead and s in WPART:
                        n = WPART[s]
                        part = slice((n % 2) * 2 * CH, (n % 2 + 1) * 2 * CH)
                        src = (WF, WP)[n // 2][:, part]
                        dst = (WF8, WP8)[n // 2].rearrange("p k f -> p (k f)")[:, part]
                        quantise(src, FS[:, 12 + n // 2:13 + n // 2], CW8[n % 2], UW8[n % 2], n, "w")
                        dve.wait_ge(F["wu_done"], n + 1)
                        dve.tensor_tensor(dst, UW8[n % 2], CW8[n % 2], ALU.subtract).then_inc(F["w8_ready"], 1)

            chunks(dve, chunk)
            for i in range(TPC):
                hand_back((NCH - 1) * TPC + i, bank[i])
            attention(1, A[1])

            dve.wait_ge(F["am_done"], NT)
            biggest(FS[:, 0:1], AM[:, :], F["am_done"])
            dve.wait_ge(F["amx"], 1)
            dve.tensor_scalar(FS[:, 8:9], FS[:, 3:4], 1.0 / FP8_MAX, 1e-6, ALU.mult, ALU.max).then_inc(F["ams"], 1)
            dve.wait_ge(F["ams"], 1)
            dve.reciprocal(FS[:, 11:12], FS[:, 8:9]).then_inc(F["ams"], 1)
            dve.wait_ge(F["ams"], 2)
            dve.tensor_scalar(FS[:, 17:18], FS[:, 11:12], GRID, None, ALU.mult).then_inc(F["ams"], 1)
            dve.tensor_tensor(FS[:, 16:17], FS[:, 8:9], FS[:, 9:10], ALU.mult).then_inc(F["ams"], 1)
            dve.wait_ge(F["ams"], 4)

            def round_x(c, j):
                both = lambda ap: ap.rearrange("p (k t) -> p k t", k=KT)
                if past(c, 2):
                    dve.wait_ge(F["x8_ready"], c - 1)
                if known(c) and c == 0:
                    quantise(XF[:, :, 0:CH], FS[:, 11:12], both(CX[j]), both(UX[j]), c, "")
                else:
                    dve.wait_ge(F["abs_ready"], c + 1)
                    dve.tensor_scalar(CX[j], CX[j], FLOOR, None, ALU.max).then_inc(F["c_done"], 1)

            def first_pass(c, j):
                if not known(c) or c + 1 < NCH:
                    round_x(c + 1, 1 - j)
                for f in range(NF):
                    dve.wait_ge(F["h_ready"], c * NF + f + 1)
                    dve.tensor_reduce(HM[:, bass.ds(c * NF + f, 1)], bank[f % 4][:, :], AX.X, ALU.max).then_inc(F["hm_done"], 1)

            round_x(0, 0)
            tiles(dve, NCH, first_pass, 2)
            dve.wait_ge(F["hm_done"], NCH * NF)
            dve.tensor_reduce(FS[:, 6:7], HM[:, :], AX.X, ALU.max).then_inc(F["hr"], 1)
            dve.wait_ge(F["hmx"], 1)
            dve.tensor_scalar(FS[:, 20:21], FS[:, 7:8], 0.0, FS[:, 16:17], ALU.max, ALU.mult).then_inc(F["ams"], 1)
            dve.wait_ge(F["ams"], 5)
            dve.tensor_tensor(FS[:, 21:22], FS[:, 20:21], FS[:, 20:21], ALU.mult).then_inc(F["ams"], 1)
            dve.wait_ge(F["ams"], 6)
            dve.tensor_scalar(FS[:, 20:21], FS[:, 21:22], 1.0 / FP8_MAX, 1e-6, ALU.mult, ALU.max).then_inc(F["ams"], 1)
            dve.wait_ge(F["ams"], 7)
            dve.reciprocal(FS[:, 21:22], FS[:, 20:21]).then_inc(F["ams"], 1)
            dve.tensor_scalar(FS[:, 23:24], FS[:, 20:21], FS[:, 10:11], tg[:, 3:4], ALU.mult, ALU.mult).then_inc(F["ams"], 1)
            dve.wait_ge(F["ams"], 9)
            dve.tensor_scalar(FS[:, 22:23], FS[:, 21:22], GRID, None, ALU.mult).then_inc(F["fs"], 1)
            dve.wait_ge(F["fs"], 1)

            def rounding(c, j):
                for f in range(NF):
                    n = c * NF + f
                    dve.wait_ge(F["hs_ready"], n + 1)
                    if past(c, 1) or f >= 4:
                        dve.wait_ge(F["h8_ready"], n - 3)
                    dve.tensor_scalar(CC[f % 4], HS[f % 4], FS[:, 22:23], FLOOR, ALU.mult, ALU.max).then_inc(F["hc_done"], 1)
                    dve.wait_ge(F["hc_done"], n + 1)
                    dve.scalar_tensor_tensor(UU[f % 4], HS[f % 4], FS[:, 21:22], CC[f % 4],
                                             ALU.mult, ALU.add).then_inc(F["hu_done"], 1)
                if past(c, 1):
                    finish(c - 1, 1 - j)

            def finish(c, j):
                for i in range(2):
                    dve.wait_ge(F["y_ready"], 2 * c + i + 1)
                    if past(c, 1):
                        dve.wait_ge(stored[i], 16 * c)
                    dve.scalar_tensor_tensor(YO[i], bank[4 + 2 * j + i][:, :], FS[:, 23:24],
                                             x[:, bass.ds(c * TPC + 2 * i, 2), :].rearrange("p a h -> p (a h)"),
                                             ALU.mult, ALU.add).then_inc(F["y_done"], 1)

            tiles(dve, NCH, rounding)
            finish(NCH - 1, (NCH - 1) % 2)

        @block.tensor
        def _(pe):
            def attention(layer, a):
                nk, d, npair, w, nmx, nsc = attention_shape(layer)
                gpu = G // nmx
                if layer == 0:
                    pe.wait_ge(d_small, 16 * 3)
                else:
                    pe.wait_ge(M["ft_done"], NT)
                ln = STAT_BASE[0 if layer == 0 else 2]

                def maxima(t, j, u):
                    n = t * nmx + u
                    if past(t, 1) or u >= 2:
                        pe.wait_ge(a["mx_done"], n - 1)
                    for g in range(gpu):
                        for b in range(2):
                            mm = pe.matmul(bank[2 + u % 2][b * S:(b + 1) * S, g * nk * S:(g + 1) * nk * S],
                                           Q1[j][:, u * gpu + g, b * S:(b + 1) * S], KD1[j][:, b, 0:nk * S],
                                           start=True, stop=True)
                    mm.then_inc(a["mx_ready"], 1)

                def scores(t, j, u):
                    n = t * 2 * nsc + u
                    if past(t, 1) or u >= 2:
                        pe.wait_ge(a["ex_ready"], n - 1)
                    b, first = u // nsc, 2 * (u % nsc)
                    for p in range(2):
                        o = bank[4 + u % 2][:, p * 256:(p + 1) * 256]
                        kc = slice((first + p) * P, (first + p + 1) * P)
                        pe.matmul(o, KD1[j][:, b, kc], Q1[j][:, :, b * S:(b + 1) * S], start=True, stop=False)
                        mm = pe.matmul(o, KD2[j][0:w, b, kc], Q2[j][0:w, :, b * S:(b + 1) * S], start=False, stop=True)
                    mm.then_inc(a["sc_ready"], 1)

                def values(t, j, b):
                    if b == 0:
                        pe.wait_ge(a["vd_ready"], 2 * t + 2)
                        if past(t, 1):
                            pe.wait_ge(a["pvs_ready"], t)
                    pe.wait_ge(a["ex_ready"], t * 2 * nsc + (b + 1) * nsc)
                    for p in range(npair):
                        e = EX[(b * nsc + p // 2 + (0 if nsc == 2 else 2 * j)) % 4]
                        mm = pe.matmul(bank[6][0:w, b * 256:(b + 1) * 256], VD[j][:, b, p * w:(p + 1) * w],
                                       e[:, (p % 2) * 256:(p % 2 + 1) * 256], start=(p == 0), stop=(p == npair - 1))
                    if b == 1:
                        mm.then_inc(a["pv_ready"], 1)

                def step(t, j):
                    if inside(t + 1):
                        pe.wait_ge(a["q_ready"], t + 2)
                        pe.wait_ge(a["kd_ready"], 2 * (t + 2))
                        for u in range(nmx // 2):
                            maxima(t + 1, 1 - j, u)
                    if inside(t):
                        pe.wait_ge(a["q2_ready"], t + 1)
                        pe.wait_ge(a["kl_ready"], 2 * (t + 1))
                        for u in range(nsc):
                            scores(t, j, u)
                    if inside(t - 1):
                        pe.wait_ge(a["pvs_ready"], t)
                        if past(t, 2):
                            pe.wait_ge(a["on_ready"], t - 1)
                            if layer == 1:
                                pe.wait_ge(a["onts_ready"], t - 1)
                        for g in range(G):
                            mm = pe.transpose(bank[7][:, g * w:(g + 1) * w],
                                              PVS[0:w, g, :], ident[0:w, 0:w])
                        mm.then_inc(a["ot_ready"], 1)
                    if inside(t):
                        for u in range(nsc, 2 * nsc):
                            scores(t, j, u)
                    if inside(t + 1):
                        for u in range(nmx // 2, nmx):
                            maxima(t + 1, 1 - j, u)
                    if inside(t + 2):
                        pe.wait_ge(LNA["out"], ln + t + 3)
                        if past(t, -1):
                            pe.wait_ge(a["q_ready"], t + 2)
                        if layer == 1 and past(t, 4):
                            pe.wait_ge(F["xf_ready"], t - 3)
                        for g in range(G):
                            mm = pe.transpose(bank[0][:, g * P:(g + 1) * P],
                                              XG[j][:, g, 0:2 * C], ident)
                        mm.then_inc(a["t1_ready"], 1)
                    if inside(t):
                        values(t, j, 0)
                    if inside(t + 1):
                        pe.wait_ge(a["mx_done"], (t + 2) * nmx)
                        if past(t, 0):
                            pe.wait_ge(a["q2_ready"], t + 1)
                        if layer == 1 and past(t, 2):
                            pe.wait_ge(a["x_done"], t - 1)
                        for g in range(G):
                            mm = pe.transpose(bank[1][0:w, g * P:(g + 1) * P], XG[1 - j][:, g, C:C + w], ident)
                        mm.then_inc(a["t2_ready"], 1)
                    if inside(t - 1) and layer == 1:
                        pe.wait_ge(a["on_ready"], t)
                        for k in range(KT):
                            mm = pe.transpose(bank[7][:, k * P:(k + 1) * P], ON[1 - j][:, k * P:(k + 1) * P], ident)
                        mm.then_inc(a["ont_ready"], 1)
                    if inside(t):
                        values(t, j, 1)
                    if inside(t - 1) and layer == 1:
                        pe.wait_ge(a["onts_ready"], t)
                        pe.wait_ge(a["q2_ready"], min(t + 2, NT) if known(t) else t + 2)
                        for k in range(KT):
                            mm = pe.matmul(bank[1][:, 0:H], ONT[1 - j][:, k, :], wc[:, k, :], start=(k == 0), stop=(k == KT - 1))
                        mm.then_inc(a["y_ready"], 1)
                    if layer == 1 and inside(t - 3):
                        pe.wait_ge(LND["out"], t - 2)
                        pe.wait_ge(a["q_ready"], min(t + 3, NT) if known(t) else t + 3)
                        if past(t, 4):
                            pe.wait_ge(F["xf_ready"], t - 3)
                        for k in range(KT):
                            mm = pe.transpose(bank[0][:, k * P:(k + 1) * P], XD[1 - j][:, k * P:(k + 1) * P], ident)
                        mm.then_inc(F["tp_ready"], 1)

                if layer == 1:
                    pe.wait_ge(d_late, 16 * 2)
                pe.wait_ge(A[layer]["vd_set"], 4)
                sweep(pe, step, LAST[layer])

            attention(0, A[0])

            def prep(t, i, r, bk):
                def turn(after):
                    pe.wait_ge(LNA["out"], STAT_BASE[1] + t + 1)
                    after()
                    for k in range(KT):
                        mm = pe.transpose(bk[:, k * P:(k + 1) * P], r.xn[:, k * P:(k + 1) * P], ident)
                    mm.then_inc(M["tp_ready"], 1)

                def logits():
                    pe.wait_ge(M["xt_ready"], t + 1)
                    n = 0
                    for k in range(KT):
                        for xx, ww in ((XNH, small_h), (XNH, small_l), (XNL, small_h)):
                            mm = pe.matmul(bk[:, 0:E], xx[:, k, i * P:(i + 1) * P], ww[:, k, 0:E], start=(n == 0), stop=(n == 3 * KT - 1))
                            n += 1
                    mm.then_inc(M["lg_ready"], 1)

                def weights():
                    pe.wait_ge(M["wd_done"], t + 1)
                    pe.transpose(bk[:, 0:P], r.wd, ident).then_inc(M["wt_ready"], 1)

                return turn, logits, weights

            pe.wait_ge(A[0]["x_done"], NT)
            pe.wait_ge(sm_ready, 2)
            pe.wait_ge(wlo_done, NPAIR)
            for t in range(TPC):
                prep(t, t, FIRSTS[t], bank[4 + t])[0](lambda: None)
            for t in range(TPC):
                prep(t, t, FIRSTS[t], bank[4 + t])[1]()

            def chunk(c, back, ahead):
                base = c * ST
                pe.wait_ge(M["turned"], 2 * (c + 1))

                def into(o, wh, wl, m0, rows):
                    n = 0
                    for k in range(KT):
                        for ww, xx in ((wh, XCH), (wl, XCH), (wh, XCL)):
                            mm = pe.matmul(o, ww(k), xx[:, k, :], start=(n == 0), stop=(n == 3 * KT - 1))
                            n += 1
                    return mm

                def gate_up(s):
                    if back or s >= 2:
                        pe.wait_ge(M["sl_ready"], base + max(s - 1, 0))
                    rows = P if s < NPAIR else I
                    for part, (b, done) in enumerate(((bank[s % 2], "g_ready"), (bank[2 + s % 2], "u_ready"))):
                        if part and (back or s >= 2):
                            pe.wait_ge(M["ut_done"], base + max(s - 1, 0))
                        if s < NPAIR:
                            cc = lambda k: slice((2 * k + part) * P, (2 * k + part + 1) * P)
                            mm = into(b[:, :], lambda k: WH[:, s, cc(k)], lambda k: WL[:, s, cc(k)], 0, rows)
                        else:
                            cc = slice(E * (part + 1), E * (part + 2))
                            mm = into(b[0:I, :], lambda k: small_h[:, k, cc], lambda k: small_l[:, k, cc], 0, rows)
                        mm.then_inc(M[done], 1)
                        if part == 0 and s == NPAIR:
                            if back:
                                pe.wait_ge(M["sg_ready"], c)
                            z = slice(3 * E, 4 * E)
                            into(bank[4][0:I, :], lambda k: small_h[:, k, z], lambda k: small_l[:, k, z], 0, I).then_inc(M["z_ready"], 1)

                def down(s, base=base):
                    pe.wait_ge(M["il_ready"], base + s + 1)
                    if s == 0 and back:
                        pe.wait_ge(M["dt_ready"], KT * c)
                    rows = P if s < NPAIR else I
                    for k in range(KT):
                        hc = slice(k * P, (k + 1) * P)
                        wh = WH[:, s, 2 * KT * P:PW] if s < NPAIR else shd_h[:, :]
                        wl = WL[:, s, 2 * KT * P:PW] if s < NPAIR else shd_l[:, :]
                        for n, (ww, ii) in enumerate(((wh, IH), (wl, IH), (wh, IL))):
                            mm = pe.matmul(bank[5 + k][:, :], ww[:, hc], ii[s % 3][0:rows, :],
                                           start=(s == 0 and n == 0), stop=(s == ST - 1 and n == 2))
                    mm.then_inc(M["dn_done"], 1)

                def turn_back(t, i):
                    if i == 0:
                        pe.wait_ge(M["dt_ready"], KT * c)
                    for k in range(KT):
                        mm = pe.transpose(bank[7][:, k * P:(k + 1) * P], DT[:, k, i * P:(i + 1) * P], ident)
                    mm.then_inc(M["ft_ready"], 1)

                for s in range(ST):
                    gate_up(s)
                    if back and s < 2:
                        down(ST - 2 + s, base - ST)
                    if not back and s == 0:
                        for t in range(TPC):
                            pe.wait_ge(M["lg_done"], t + 1)
                            prep(t, t, FIRSTS[t], bank[4 + t])[2]()
                    i = s // 8
                    if back and s % 8 == 2:
                        t = (c - 1) * TPC + i
                        if ahead or i == 0:
                            pe.wait_ge(M["wts_ready"], (c + 1) * TPC + i)
                        else:
                            pe.wait_ge(M["ft_done"], t)
                        turn_back(t, i)
                    if s >= 2:
                        down(s - 2)
                    if s == NPAIR:
                        break
                    if ahead:
                        turn, logits, weights = prep((c + 1) * TPC + i, i, LOOP, bank[7])
                        if s % 8 == 3:
                            if back:
                                turn(lambda: pe.wait_ge(M["ft_done"], (c - 1) * TPC + i + 1))
                            else:
                                turn(lambda: pe.wait_ge(M["wts_ready"], TPC + i))
                        if s % 8 == 5:
                            logits()
                        if s % 8 == 7:
                            weights()
                if not ahead:
                    down(ST - 2)
                    down(ST - 1)

            chunks(pe, chunk)
            pe.wait_ge(M["sl_ready"], NCH * ST)
            pe.wait_ge(M["ut_done"], NCH * ST)
            pe.wait_ge(M["dt_ready"], KT * NCH)
            for i in range(TPC):
                for k in range(KT):
                    mm = pe.transpose(bank[i][:, k * P:(k + 1) * P], DT[:, k, i * P:(i + 1) * P], ident)
                mm.then_inc(M["ft_ready"], 1)
            attention(1, A[1])

            pe.wait_ge(F["w8_ready"], 4)

            def hidden(c, f, free):
                if past(c, 1) or f >= 4:
                    pe.wait_ge(free, c * NF + f - 3)
                for k in range(KT):
                    mm = pe.matmul(bank[f % 4][:, :], WF8[:, k, f * P:(f + 1) * P], X8[:, k, bass.ds(c * CH, CH)],
                                   start=(k == 0), stop=(k == KT - 1))
                mm.then_inc(F["h_ready"], 1)

            def first_pass(c, j):
                pe.wait_ge(F["x8_ready"], c + 1)
                for f in range(NF):
                    hidden(c, f, F["hm_done"])

            def product(j, i, f):
                return pe.matmul(bank[4 + 2 * j + i // 2][:, (i % 2) * H:(i % 2 + 1) * H], H8[j][:, f, i * P:(i + 1) * P], WP8[:, f, :],
                                 start=(f == 0), stop=(f == NF - 1))

            def project(c, j):
                pe.wait_ge(F["h8_ready"], (c + 1) * NF)
                if past(c, 2):
                    pe.wait_ge(F["y_done"], 2 * c - 2)
                for i in range(TPC):
                    for f in range(NF):
                        mm = product(j, i, f)
                    if i % 2:
                        mm.then_inc(F["y_ready"], 1)

            def second_pass(c, j):
                for f in range(NF):
                    hidden(c, f, F["r_ready"])
                if past(c, 1):
                    project(c - 1, 1 - j)

            tiles(pe, NCH, first_pass)
            pe.wait_ge(F["hm_done"], NCH * NF)
            tiles(pe, NCH, second_pass)
            c, j = NCH - 1, (NCH - 1) % 2
            pe.wait_ge(F["y_done"], 2 * c - 2)
            for f in range(NF):
                pe.wait_ge(F["h8_ready"], c * NF + f + 1)
                for i in (0, 2):
                    product(j, i, f)
            for i in (1, 3):
                for f in range(NF):
                    mm = product(j, i, f)
                mm.then_inc(F["y_ready"], 1)


def kernel(**inputs):
    import concourse.bacc as bacc
    from concourse.bass_utils import run_bass_kernel_spmd as run

    a = {k: np.asarray(v) for k, v in inputs.items()}
    ctx = a["ctx_512"]

    def by_k(w):
        return w.T.reshape(KT, P, -1).transpose(1, 0, 2)

    gu = a["L0_ffn_gu_w"].reshape(NPAIR, 2, 2, I, KT, P).transpose(5, 0, 4, 2, 1, 3).reshape(P, NPAIR, KT * 2 * P)
    dp = a["L0_ffn_dp_w"].reshape(NPAIR, 2, H, I).transpose(1, 3, 0, 2).reshape(P, NPAIR, H)
    small = np.concatenate([by_k(a["L0_ffn_gate_w"]), by_k(a["L0_ffn_sh_gate_w"]), by_k(a["L0_ffn_sh_up_w"]),
                            by_k(np.broadcast_to(a["L0_ffn_sh_gate1_w"], (E, H)))], axis=2)
    arrays = {
        "x": a["x"].reshape(B * S, H),
        "ctx": ctx,
        "ctxT": ctx.transpose(2, 0, 1).reshape(C, B * S),
        "g_xattn": a["g_xattn"],
        "g_ffn": a["g_ffn"],
        "consts": const_table(),
        "wpairs": np.concatenate([gu, dp], axis=2),
        "wsmall": small.reshape(P, KT * SMW),
        "wshdown": a["L0_ffn_sh_down_w"].T,
        "wc": by_k(a["L1_xattn_Wc"]),
        "bc": a["L1_xattn_bc"],
        "wfc": by_k(a["L1_ffn_w_fc"]).reshape(P, KT * FF),
        "wproj": a["L1_ffn_w_proj"].T.reshape(NF, P, H).transpose(1, 0, 2).reshape(P, NF * H),
    }
    nc = bacc.Bacc("TRN2", target_bir_lowering=False, num_devices=1)
    data, args = {}, {}
    for name, v in arrays.items():
        v = np.ascontiguousarray(v)
        data[f"in_{name}"] = v
        args[name] = nc.dram_tensor(f"in_{name}", v.shape, mybir.dt.from_np(v.dtype), kind="ExternalInput").ap()
    out = nc.dram_tensor("out", (B * S, H), F32, kind="ExternalOutput").ap()
    flamingo_block(nc, args["x"], args["ctx"], args["ctxT"], (args["g_xattn"], args["g_ffn"]), args["consts"],
                   args["wpairs"], args["wsmall"], args["wshdown"], args["wc"], args["bc"], args["wfc"], args["wproj"], out)
    r = run(nc, [data], core_ids=[0])
    return r.results[0]["out"].reshape(B, S, H)
```
